# Optimizing a Trainium2 kernel written in Bass

```python
import numpy as np
import jax
import jax.numpy as jnp

def _softmax(x, axis=-1):
    return jax.nn.softmax(x, axis=axis)

def _gelu(x):
    return jax.nn.gelu(x, approximate=True)

def _silu(x):
    return jax.nn.silu(x)

def _sigmoid(x):
    return jax.nn.sigmoid(x)

def _layernorm(x, axis=-1, eps=1e-05):
    m = jnp.mean(x, axis=axis, keepdims=True)
    v = jnp.var(x, axis=axis, keepdims=True)
    return (x - m) / jnp.sqrt(v + eps)

def _scatter_add(tgt, idx, src, axis=0):
    return tgt.at[idx].add(src)

def _segment_sum(src, seg, n):
    return jax.ops.segment_sum(src, seg, n)
kernel_name = 'mk_xattn_ffn_d1_seqx_r8_b92c80'

def setup_inputs(seed: int=0):
    np.random.seed(seed)
    _w = jnp.asarray

    def _rec_inputs():
        import jax
        import jax.numpy as jnp
        _rk = jax.random.key(seed)
        x = 7.22e-05 + 1 * jax.random.normal(jax.random.fold_in(_rk, 1), (64, 64, 256), jnp.float32)
        _lenS = 64 - jax.random.randint(jax.random.fold_in(_rk, 7), (64,), 0, max(1, 64 // 4) + 1, jnp.int32)
        _lenS2 = 64 - jax.random.randint(jax.random.fold_in(_rk, 8), (64,), 0, max(1, 64 // 4) + 1, jnp.int32)
        _ctx_2048P = jax.random.normal(jax.random.fold_in(_rk, 11), (64, 16, 256), jnp.float32)
        _ctx_2048c = jax.random.dirichlet(jax.random.fold_in(_rk, 511), 0.3 * jnp.ones((16,), jnp.float32), (64, 64))
        _ctx_2048t = jnp.einsum('bsk,bkd->bsd', _ctx_2048c, _ctx_2048P)
        _ctx_2048t = _ctx_2048t * jax.lax.rsqrt(jnp.mean(jnp.square(_ctx_2048t)) + 1e-12) * 0.953939
        ctx_2048 = 4.13588e-05 + 0.999923 * (_ctx_2048t + 0.3 * jax.random.normal(jax.random.fold_in(_rk, 611), (64, 64, 256), jnp.float32))
        return (x, ctx_2048)
    x, ctx_2048 = _rec_inputs()

    def _L0_xattn_setup():
        import jax, jax.numpy as jnp
        import numpy as np
        import math
        EMBED = 256
        HEADS = 32
        GROUPS = 8
        GROUP_HEADS = HEADS // GROUPS
        HEAD_DIM = EMBED // HEADS
        B, S = (4, 128)
        key = jax.random.key(seed)
        ks = jax.random.split(key, 8)
        sc = 0.02
        return {'q': jax.random.normal(ks[0], (B, S, EMBED), jnp.float32), 'k': jax.random.normal(ks[1], (B, S, EMBED), jnp.float32), 'v': jax.random.normal(ks[2], (B, S, EMBED), jnp.float32), 'Wq': jax.random.normal(ks[3], (EMBED, EMBED), jnp.float32) * sc, 'Wk': jax.random.normal(ks[4], (GROUPS * HEAD_DIM, EMBED), jnp.float32) * sc, 'Wv': jax.random.normal(ks[5], (GROUPS * HEAD_DIM, EMBED), jnp.float32) * sc, 'Wfc': jax.random.normal(ks[6], (EMBED, EMBED), jnp.float32) * sc, 'bfc': jnp.zeros((EMBED,), jnp.float32)}
    _L0_xattn_all = _L0_xattn_setup()
    _L0_xattn_in = {k: v for k, v in _L0_xattn_all.items() if k in ('Wq', 'Wk', 'Wv', 'Wfc', 'bfc')}
    del _L0_xattn_all

    def _L0_ffn_setup():
        import jax, jax.numpy as jnp
        import numpy as np
        from jax import lax
        TOP_K = 2
        N_EXPERTS = 8
        key = jax.random.key(seed)
        ks = jax.random.split(key, 7)
        B, S, H, I, E = (4, 256, 256, 176, N_EXPERTS)
        s_h = 1.0 / np.sqrt(H)
        s_i = 1.0 / np.sqrt(I)
        return {'hidden_states': jax.random.normal(ks[0], (B, S, H), jnp.float32), 'gate_w': jax.random.normal(ks[1], (E, H), jnp.float32) * s_h, 'w1': jax.random.normal(ks[2], (E, H, 2 * I), jnp.float32) * s_h, 'w2': jax.random.normal(ks[3], (E, I, H), jnp.float32) * s_i, 'sw1': jax.random.normal(ks[4], (I, H), jnp.float32) * s_h, 'sw2': jax.random.normal(ks[5], (I, H), jnp.float32) * s_h, 'sw3': jax.random.normal(ks[6], (H, I), jnp.float32) * s_i}
    _L0_ffn_all = _L0_ffn_setup()
    _L0_ffn_in = {k: v for k, v in _L0_ffn_all.items() if k in ('gate_w', 'w1', 'w2', 'sw1', 'sw2', 'sw3')}
    del _L0_ffn_all
    return {'x': x, 'ctx_2048': ctx_2048, 'L0_xattn_Wq': _L0_xattn_in['Wq'], 'L0_xattn_Wk': _L0_xattn_in['Wk'], 'L0_xattn_Wv': _L0_xattn_in['Wv'], 'L0_xattn_Wfc': _L0_xattn_in['Wfc'], 'L0_xattn_bfc': _L0_xattn_in['bfc'], 'L0_ffn_gate_w': _L0_ffn_in['gate_w'], 'L0_ffn_w1': _L0_ffn_in['w1'], 'L0_ffn_w2': _L0_ffn_in['w2'], 'L0_ffn_sw1': _L0_ffn_in['sw1'], 'L0_ffn_sw2': _L0_ffn_in['sw2'], 'L0_ffn_sw3': _L0_ffn_in['sw3']}

def reference(x, ctx_2048, L0_xattn_Wq, L0_xattn_Wk, L0_xattn_Wv, L0_xattn_Wfc, L0_xattn_bfc, L0_ffn_gate_w, L0_ffn_w1, L0_ffn_w2, L0_ffn_sw1, L0_ffn_sw2, L0_ffn_sw3):
    import jax
    import jax.numpy as jnp

    def _L0_xattn_ref(q, k, v, Wq, Wk, Wv, Wfc, bfc):
        import jax, jax.numpy as jnp
        import numpy as np
        import math
        EMBED = 256
        HEADS = 32
        GROUPS = 8
        GROUP_HEADS = HEADS // GROUPS
        HEAD_DIM = EMBED // HEADS
        B, S = (4, 128)
        N, S_, _ = q.shape
        qh = (q @ Wq.T).reshape(N, S_, HEADS, HEAD_DIM).transpose(0, 2, 1, 3)
        kh = (k @ Wk.T).reshape(N, S_, GROUPS, HEAD_DIM).transpose(0, 2, 1, 3)
        vh = (v @ Wv.T).reshape(N, S_, GROUPS, HEAD_DIM).transpose(0, 2, 1, 3)
        kh = jnp.repeat(kh, GROUP_HEADS, axis=1)
        vh = jnp.repeat(vh, GROUP_HEADS, axis=1)
        score = jnp.einsum('bhqd,bhkd->bhqk', qh, kh) / math.sqrt(HEAD_DIM)
        attn = jax.nn.softmax(score, axis=-1)
        out = jnp.einsum('bhqk,bhkd->bhqd', attn, vh)
        out = out.transpose(0, 2, 1, 3).reshape(N, S_, EMBED)
        return out @ Wfc.T + bfc

    def _L0_ffn_ref(hidden_states, gate_w, w1, w2, sw1, sw2, sw3):
        import jax, jax.numpy as jnp
        import numpy as np
        from jax import lax
        TOP_K = 2
        N_EXPERTS = 8
        B, S, H = hidden_states.shape
        x = hidden_states.reshape(-1, H)
        T = x.shape[0]
        logits = jnp.einsum('th,eh->te', x.astype(jnp.float32), gate_w.astype(jnp.float32))
        scores = jax.nn.softmax(logits, axis=-1)
        topk_w, topk_idx = lax.top_k(scores, TOP_K)
        topk_w = topk_w / (topk_w.sum(-1, keepdims=True) + 1e-20)
        topk_w = topk_w.astype(hidden_states.dtype)
        cw = jnp.zeros((T, N_EXPERTS), hidden_states.dtype).at[jnp.arange(T)[:, None], topk_idx].add(topk_w)

        def body(acc, ew):
            w1e, w2e, cwe = ew
            h = x @ w1e
            g, u = jnp.split(h, 2, axis=-1)
            y = jax.nn.silu(g) * u @ w2e
            return (acc + cwe[:, None] * y, None)
        moe, _ = lax.scan(body, jnp.zeros_like(x), (w1, w2, cw.T))
        moe = moe.reshape(B, S, H)
        shared = jnp.einsum('bsi,hi->bsh', jax.nn.silu(jnp.einsum('bsh,ih->bsi', hidden_states, sw1)) * jnp.einsum('bsh,ih->bsi', hidden_states, sw2), sw3)
        return moe + shared
    x = x + _L0_xattn_ref(_layernorm(x, axis=-1), ctx_2048, ctx_2048, L0_xattn_Wq, L0_xattn_Wk, L0_xattn_Wv, L0_xattn_Wfc, L0_xattn_bfc)
    x = x + _L0_ffn_ref(_layernorm(x, axis=-1), L0_ffn_gate_w, L0_ffn_w1, L0_ffn_w2, L0_ffn_sw1, L0_ffn_sw2, L0_ffn_sw3)
    return x

_drawn_inputs = setup_inputs


def setup_inputs(seed=0):
    import zlib

    import numpy as np

    out = dict(_drawn_inputs(seed))
    spreads = {'L0_xattn_bfc': (0.0, 0.1)}
    factors = {'L0_xattn_Wq': 4.81, 'L0_xattn_Wk': 5.024}
    for name, (base, spread) in spreads.items():
        noise = np.random.default_rng([zlib.crc32(name.encode()), seed]).standard_normal(out[name].shape)
        drawn = base * np.exp(spread * noise) if base else spread * noise
        out[name] = jnp.asarray(drawn.astype(out[name].dtype))
    for name, factor in factors.items():
        out[name] = (out[name] * factor).astype(out[name].dtype)
    return out
```

```python
import math
from contextlib import ExitStack

import concourse.bass as bass
from concourse import mybir

F32 = mybir.dt.float32
BF16 = mybir.dt.bfloat16
I32 = mybir.dt.int32
U32 = mybir.dt.uint32
ALU = mybir.AluOpType
ACT = mybir.ActivationFunctionType
AX = mybir.AxisListType

P = 128
BATCH, SEQ, EMBED = 64, 64, 256
TOKENS = BATCH * SEQ
TILES = TOKENS // P
HALVES = EMBED // P
HEADS, GROUPS, HEAD_DIM = 32, 8, 8
KV = GROUPS * HEAD_DIM
CHUNK_TILES = 4
CHUNK = CHUNK_TILES * P
CHUNKS = TOKENS // CHUNK
RUN = CHUNK_TILES * SEQ
SCALE = 1.0 / math.sqrt(HEAD_DIM)
EPS = 1e-5
Q_PART = (0, 0, 0, 1, 1, 2)
K_PART = (0, 1, 2, 0, 1, 0)
UNITS = 4
HP = HEADS // 2
EXPERTS, INNER, TOP_K = 8, 176, 2
INNER_B = INNER - P


def run_slots(eng, total, first, period, slot):
    turns = (total - first) // period
    while turns > 0 and first + turns * period > total - 1:
        turns -= 1
    if turns < 2:
        return 0
    for s in range(first):
        slot(s, 0)
    if turns > 0:
        with eng.Fori(0, turns) as r:
            for i in range(period):
                slot(first + i, r)
    return first + turns * period


def held(eng, value):
    return value if isinstance(value, int) else eng.to_reg(value)


class Sizes:
    pass


def load_operands(sp, io, keep, c, b):
    q_op, k_op, v_op, qkv_in = keep.q_op, keep.k_op, keep.v_op, keep.qkv_in
    for a in range(2):
        for n in range(len(Q_PART)):
            rows = slice(64 * a + HEAD_DIM * n, 64 * a + HEAD_DIM * (n + 1))
            sp.dma_start(k_op[b][rows, :, a, :],
                         io.k_dram[K_PART[n] * KV:(K_PART[n] + 1) * KV, bass.ds(c, 1),
                                   a * RUN:(a + 1) * RUN]
                         .rearrange("(g d) c n -> d g (c n)", d=HEAD_DIM)).then_inc(qkv_in[b], 16)
            sp.dma_start(q_op[b][rows, :, :],
                         io.q_dram[Q_PART[n] * EMBED:(Q_PART[n] + 1) * EMBED, bass.ds(c, 1),
                                   a * RUN:(a + 1) * RUN]
                         .rearrange("(h d) c n -> d h (c n)", d=HEAD_DIM)).then_inc(qkv_in[b], 16)
    sp.dma_start(v_op[b][:].rearrange("p i g m -> p (i g m)"), io.v_dram[bass.ds(c * P, P)]
                 ).then_inc(qkv_in[b], 16)


def project_phase(nc, ctx0, io, keep):
    with ExitStack() as ctx:
        def sb(name, shape, dt):
            return ctx.enter_context(nc.sbuf_tensor(name, shape, dt))

        def psum(name, shape, dt):
            return ctx.enter_context(nc.psum_tensor(name, shape, dt))

        def sem(name):
            return ctx.enter_context(nc.semaphore(name))

        x_sb, ident, bias_sb = keep.x_sb, keep.ident, keep.bias_sb
        wq, wkv = sb("wq", [P, HALVES, EMBED], F32), sb("wkv", [P, HALVES, 2 * KV], F32)
        ctx_t = sb("ctx_t", [P, 2, HALVES, CHUNK], F32)
        stats = sb("stats", [P, 2, CHUNK_TILES, 6], F32)
        mean_var = sb("mean_var", [P, 2, CHUNK_TILES, 2], F32)
        var_eps = sb("var_eps", [P, 2, CHUNK_TILES], F32)
        rstd = sb("rstd", [P, 2, CHUNK_TILES], F32)
        minus_half = sb("minus_half", [P, CHUNK_TILES], F32)
        xn = sb("xn", [P, 2, CHUNK_TILES, EMBED], F32)
        xn_t = sb("xn_t", [P, 2, HALVES, CHUNK], F32)
        q_parts = sb("q_parts", [P, 2, 3, HALVES, CHUNK], BF16)
        q_rest = sb("q_rest", [P, HALVES, CHUNK], F32)
        k_parts = sb("k_parts", [KV, 2, 3, CHUNK], BF16)
        k_rest = sb("k_rest", [KV, CHUNK], F32)
        v_t = sb("v_t", [P, 2, CHUNK], F32)
        v_blocks = sb("v_blocks", [P, 2, CHUNK_TILES, GROUPS, 32], F32)

        xt_ps = [psum(f"xt_ps{i}", [P, CHUNK], F32) for i in range(HALVES)]
        q_ps = [psum(f"q_ps{i}", [P, CHUNK], F32) for i in range(HALVES)]
        kv_ps = psum("kv_ps", [P, CHUNK], F32)
        v_ps = psum("v_ps", [P, CHUNK_TILES, KV], F32)

        weights_in = sem("weights_in")
        x_in, ctx_in = [sem(f"x_in{b}") for b in range(2)], [sem(f"ctx_in{b}") for b in range(2)]
        stats_done, stats_ready, eps_added, rstd_ready, half_set = (
            sem("stats_done"), sem("stats_ready"), sem("eps_added"), sem("rstd_ready"), sem("half_set"))
        xn_ready, xt_done, xt_ready = sem("xn_ready"), sem("xt_done"), sem("xt_ready")
        q_done, kv_done, vt_done = sem("q_done"), sem("kv_done"), sem("vt_done")
        q1_ready, q_rest_ready, q2_ready, q3_ready = (
            sem("q1_ready"), sem("q_rest_ready"), sem("q2_ready"), sem("q3_ready"))
        k1_ready, k_rest_ready, k2_ready, k3_ready = (
            sem("k1_ready"), sem("k_rest_ready"), sem("k2_ready"), sem("k3_ready"))
        v_t_ready, v_blocks_ready = sem("v_t_ready"), sem("v_blocks_ready")
        blocks_set, bias_added = sem("blocks_set"), sem("bias_added")
        zeros_set = sem("zeros_set")
        stored = [sem(f"stored{b}") for b in range(2)]
        STORED = 3 * 16

        block = ctx.enter_context(nc.Block())

        @block.sync
        def _(sp):
            def load_x(k, c, b):
                if k >= 2:
                    sp.wait_ge(stats_ready, CHUNK_TILES * (c - 1))
                sp.dma_start(x_sb[:, bass.ds(c * CHUNK_TILES, CHUNK_TILES), :],
                             io.x[bass.ds(c * CHUNK, CHUNK), :].rearrange("(i p) f -> p i f", p=P)
                             ).then_inc(x_in[b], 16)

            def load_context(k, c, b):
                if k >= 2:
                    sp.wait_ge(kv_done, c - 1)
                sp.dma_start(ctx_t[:, b], io.ctx_t[bass.ds(c * P, P)]).then_inc(ctx_in[b], 16)

            def store(c, b):
                sp.wait_ge(q3_ready, HALVES * (c + 1))
                sp.dma_start(io.q_dram[:, bass.ds(c, 1)].rearrange("(t p) c n -> p t (c n)", p=P),
                             q_parts[:, b].rearrange("p t h n -> p (t h) n")).then_inc(stored[b], 16)
                sp.wait_ge(k3_ready, c + 1)
                sp.dma_start(io.k_dram[:, bass.ds(c, 1)].rearrange("(t p) c n -> p t (c n)", p=KV),
                             k_parts[:, b]).then_inc(stored[b], 16)
                sp.wait_ge(v_blocks_ready, c + 1)
                sp.dma_start(io.v_dram[bass.ds(c * P, P)],
                             v_blocks[:, b].rearrange("p i g m -> p (i g m)")).then_inc(stored[b], 16)

            def slot(k, r):
                s = k + 2 * r
                if k == 0:
                    load_x(0, 0, 0)
                if k <= CHUNKS - 2:
                    load_x(k + 1, s + 1, (k + 1) % 2)
                if k == 0:
                    sp.dma_start(ident[:], io.ident).then_inc(weights_in, 16)
                    sp.dma_start(wq[:], io.wq).then_inc(weights_in, 16)
                if k >= 3:
                    if k == CHUNKS - 1 or k == CHUNKS:
                        sp.wait_ge(stored[(k - 3) % 2], STORED * ((k - 3) // 2))
                    store(s - 3, (k - 3) % 2)
                if k <= CHUNKS - 1:
                    load_context(k, s, k % 2)
                if k == 0:
                    sp.dma_start(wkv[:], io.wkv).then_inc(weights_in, 16)
                    sp.dma_start(bias_sb[:], io.bias.partition_broadcast(P)).then_inc(weights_in, 16)
                if k == CHUNKS - 1 or k == CHUNKS:
                    sp.wait_ge(zeros_set, len(keep.zeroed))
                    load_operands(sp, io, keep, k - CHUNKS + 1, k - CHUNKS + 1)
            for s in range(run_slots(sp, CHUNKS, 3, 2, slot), CHUNKS + 3):
                slot(s, 0)
            for b in range(2):
                sp.wait_ge(stored[b], STORED * (CHUNKS // 2))

        @block.gpsimd
        def _(pool):
            nc.gpsimd.memset(minus_half[:], -0.5).then_inc(half_set, 1)
            nc.gpsimd.memset(v_blocks[:], 0.0).then_inc(half_set, 1)
            pool.wait_ge(half_set, 2)
            for a in range(2):
                rows = slice(a * SEQ, (a + 1) * SEQ)
                for b in range(2):
                    ones = v_blocks[rows, b, :, :, 16 * a + 8:16 * a + 16].rearrange("p i g d -> p (i g) d")
                    nc.gpsimd.memset(ones, 1.0).then_inc(blocks_set, 1)

            def reciprocal_deviation(c):
                b = c % 2
                pool.wait_ge(stats_ready, CHUNK_TILES * (c + 1))
                if c >= 2:
                    pool.wait_ge(xn_ready, CHUNK_TILES * (c - 1))
                nc.gpsimd.tensor_scalar(var_eps[:, b], mean_var[:, b, :, 1], EPS, None, ALU.add
                                        ).then_inc(eps_added, 1)
                pool.wait_ge(eps_added, c + 1)
                nc.gpsimd.tensor_tensor(rstd[:, b], var_eps[:, b], minus_half[:], ALU.pow
                                        ).then_inc(rstd_ready, 1)

            def add_bias(c):
                pool.wait_ge(xn_ready, CHUNK_TILES * (c + 1))
                tiles = slice(c * CHUNK_TILES, (c + 1) * CHUNK_TILES)
                nc.gpsimd.tensor_tensor(x_sb[:, tiles, :], x_sb[:, tiles, :],
                                        bias_sb[:].unsqueeze(1).to_broadcast([P, CHUNK_TILES, EMBED]), ALU.add
                                        ).then_inc(bias_added, 1)
            for c in range(CHUNKS + 2):
                if c < CHUNKS:
                    reciprocal_deviation(c)
                if 1 <= c <= len(keep.zeroed):
                    nc.gpsimd.memset(keep.zeroed[c - 1].bitcast(F32), 0.0).then_inc(zeros_set, 1)
                if c == 1:
                    pool.wait_ge(weights_in, 64)
                if c >= 2:
                    add_bias(c - 2)

        @block.vector
        def _(dve):
            def moments(k, c, b, turn):
                dve.wait_ge(x_in[b], 16 * (turn + 1))
                for i in range(CHUNK_TILES):
                    nc.vector.bn_stats(stats[:, b, i, :], x_sb[:, bass.ds(c * CHUNK_TILES + i, 1), :]
                                       ).then_inc(stats_done, 1)
                for i in range(CHUNK_TILES):
                    so_far = held(dve, CHUNK_TILES * c + i + 1)
                    dve.wait_ge(blocks_set, 4)
                    dve.wait_ge(stats_done, so_far)
                    nc.vector.bn_aggr(mean_var[:, b, i, :], stats[:, b, i, :]).then_inc(stats_ready, 1)

            def normalise(k, c, b):
                dve.wait_ge(rstd_ready, c + 1)
                if k >= 2:
                    dve.wait_ge(xt_done, c - 1)
                for i in range(CHUNK_TILES):
                    nc.vector.tensor_scalar(xn[:, b, i, :], x_sb[:, bass.ds(c * CHUNK_TILES + i, 1), :],
                                            mean_var[:, b, i, 0:1], rstd[:, b, i:i + 1],
                                            ALU.subtract, ALU.mult).then_inc(xn_ready, 1)

            def split_middle(k, c, b):
                if k >= 1:
                    dve.wait_ge(q3_ready, HALVES * c)
                    dve.wait_ge(k3_ready, c)
                for h in range(HALVES):
                    dve.wait_ge(q1_ready, HALVES * c + h + 1)
                    nc.vector.scalar_tensor_tensor(q_rest[:, h], q_ps[h][:], SCALE, q_parts[:, b, 0, h],
                                                   ALU.mult, ALU.subtract).then_inc(q_rest_ready, 1)
                dve.wait_ge(k1_ready, c + 1)
                nc.vector.tensor_tensor(k_rest[:], kv_ps[0:KV, :], k_parts[:, b, 0], ALU.subtract
                                        ).then_inc(k_rest_ready, 1)

            def split_small(c, b):
                for h in range(HALVES):
                    dve.wait_ge(q2_ready, HALVES * c + h + 1)
                    nc.vector.tensor_tensor(q_parts[:, b, 2, h], q_rest[:, h], q_parts[:, b, 1, h],
                                            ALU.subtract).then_inc(q3_ready, 1)
                dve.wait_ge(k2_ready, c + 1)
                nc.vector.tensor_tensor(k_parts[:, b, 2], k_rest[:], k_parts[:, b, 1], ALU.subtract
                                        ).then_inc(k3_ready, 1)

            def place_values(k, c, b, turn):
                dve.wait_ge(vt_done, c + 1)
                if k >= 2:
                    dve.wait_ge(stored[b], STORED * turn)
                for a in range(2):
                    rows = slice(a * SEQ, (a + 1) * SEQ)
                    last = nc.vector.tensor_copy(v_blocks[rows, b, :, :, 16 * a:16 * a + 8],
                                                 v_ps[rows].rearrange("p i (g d) -> p i g d", g=GROUPS))
                    if a == 1:
                        last.then_inc(v_blocks_ready, 1)
            dve.wait_ge(blocks_set, 4)

            def slot(k, r):
                s = k + 2 * r
                if 1 <= k <= CHUNKS:
                    normalise(k - 1, s - 1, (k - 1) % 2)
                if 3 <= k <= CHUNKS + 2:
                    split_middle(k - 3, s - 3, (k - 3) % 2)
                if k <= CHUNKS - 1:
                    moments(k, s, k % 2, k // 2 + r)
                if 3 <= k <= CHUNKS + 2:
                    split_small(s - 3, (k - 3) % 2)
                if k >= 4:
                    place_values(k - 4, s - 4, k % 2, (k - 4) // 2 + r)
            for s in range(run_slots(dve, CHUNKS, 6, 2, slot), CHUNKS + 4):
                slot(s, 0)

        @block.scalar
        def _(act):
            def evacuate(k, c, b):
                act.wait_ge(xt_done, c + 1)
                if k >= 2:
                    act.wait_ge(kv_done, c - 1)
                for h in range(HALVES):
                    nc.scalar.activation(
                        xn_t[:, b, h].rearrange("p (a q i) -> p a i q", a=2, i=CHUNK_TILES),
                        xt_ps[h][:].rearrange("p (i a q) -> p a i q", a=2, i=CHUNK_TILES),
                        ACT.Copy).then_inc(xt_ready, 1)

            def split_large(k, c, b, turn):
                if k >= 2:
                    act.wait_ge(stored[b], STORED * turn)
                for h in range(HALVES):
                    act.wait_ge(q_done, HALVES * c + h + 1)
                    nc.scalar.activation(q_parts[:, b, 0, h], q_ps[h][:], ACT.Copy, scale=SCALE
                                         ).then_inc(q1_ready, 1)
                act.wait_ge(kv_done, c + 1)
                nc.scalar.activation(k_parts[:, b, 0], kv_ps[0:KV, :], ACT.Copy).then_inc(k1_ready, 1)
                nc.scalar.activation(v_t[KV:P, b], kv_ps[KV:P, :], ACT.Copy).then_inc(v_t_ready, 1)

            def split_middle(c, b):
                for h in range(HALVES):
                    act.wait_ge(q_rest_ready, HALVES * c + h + 1)
                    nc.scalar.activation(q_parts[:, b, 1, h], q_rest[:, h], ACT.Copy).then_inc(q2_ready, 1)
                act.wait_ge(k_rest_ready, c + 1)
                nc.scalar.activation(k_parts[:, b, 1], k_rest[:], ACT.Copy).then_inc(k2_ready, 1)

            def slot(k, r):
                s = k + 2 * r
                if k <= CHUNKS - 1:
                    evacuate(k, s, k % 2)
                if k >= 2:
                    split_middle(s - 2, k % 2)
                if 1 <= k <= CHUNKS:
                    split_large(k - 1, s - 1, (k - 1) % 2, (k - 1) // 2 + r)
            for s in range(run_slots(act, CHUNKS, 3, 2, slot), CHUNKS + 2):
                slot(s, 0)

        @block.tensor
        def _(pe):
            pe.wait_ge(weights_in, 64)

            def transpose_x(k, c, b):
                pe.wait_ge(xn_ready, CHUNK_TILES * (c + 1))
                if k >= 1:
                    pe.wait_ge(xt_ready, HALVES * c)
                for i in range(CHUNK_TILES):
                    for h in range(HALVES):
                        last = nc.tensor.transpose(xt_ps[h][:, i * P:(i + 1) * P],
                                                   xn[:, b, i, h * P:(h + 1) * P], ident[:])
                last.then_inc(xt_done, 1)

            def project(k, c, b, turn):
                pe.wait_ge(ctx_in[b], 16 * (turn + 1))
                pe.wait_ge(xt_ready, HALVES * (c + 1))
                for m in range(HALVES):
                    if k >= 1:
                        pe.wait_ge(q_rest_ready, HALVES * c)
                    for h in range(HALVES):
                        last = nc.tensor.matmul(q_ps[m][:], wq[:, h, m * P:(m + 1) * P], xn_t[:, b, h],
                                                start=(h == 0), stop=(h == HALVES - 1))
                    last.then_inc(q_done, 1)
                if k >= 1:
                    pe.wait_ge(k_rest_ready, c)
                    pe.wait_ge(v_t_ready, c)
                for h in range(HALVES):
                    last = nc.tensor.matmul(kv_ps[:], wkv[:, h], ctx_t[:, b, h],
                                            start=(h == 0), stop=(h == HALVES - 1))
                last.then_inc(kv_done, 1)

            def transpose_v(k, c, b):
                chunks, before = held(pe, c + 1), held(pe, c)
                pe.wait_ge(weights_in, 64)
                pe.wait_ge(v_t_ready, chunks)
                if k >= 1:
                    pe.wait_ge(v_blocks_ready, before)
                for i in range(CHUNK_TILES):
                    keys = v_t[KV:P, b].rearrange("p (n i) -> p n i", i=CHUNK_TILES)[:, :, i]
                    last = nc.tensor.transpose(v_ps[:, i, :], keys, ident[KV:P, KV:P])
                last.then_inc(vt_done, 1)

            def slot(k, r):
                s = k + 2 * r
                if k <= CHUNKS - 1:
                    transpose_x(k, s, k % 2)
                if k >= 2:
                    transpose_v(k - 2, s - 2, k % 2)
                if 1 <= k <= CHUNKS:
                    project(k - 1, s - 1, (k - 1) % 2, (k - 1) // 2 + r)
            for s in range(run_slots(pe, CHUNKS, 3, 2, slot), CHUNKS + 2):
                slot(s, 0)


def attention_phase(nc, ctx0, io, keep):
    with ExitStack() as ctx:
        def sb(name, shape, dt):
            return ctx.enter_context(nc.sbuf_tensor(name, shape, dt))

        def psum(name, shape, dt):
            return ctx.enter_context(nc.psum_tensor(name, shape, dt))

        def sem(name):
            return ctx.enter_context(nc.semaphore(name))

        x_sb, ident = keep.x_sb, keep.ident
        q_op, k_op = keep.q_op, keep.k_op
        v_op, qkv_in = keep.v_op, keep.qkv_in
        w_out = sb("w_out", [P, 2, EMBED], F32)
        select = sb("select", [SEQ, HP, P], BF16)
        ident_b = sb("ident_b", [P, P], BF16)
        row_max = sb("row_max", [P, 2, 2 * HP], F32)
        minus_max = sb("minus_max", [P, 2, 2, 2 * HP], BF16)
        max_t = sb("max_t", [SEQ, 2, P], BF16)
        probs = sb("probs", [P, UNITS, 512], F32)
        pv_sb = sb("pv_sb", [P, 512], F32)
        recip = sb("recip", [P, 2 * HP], F32)
        heads_out = sb("heads_out", [P, 2, P], F32)
        heads_t = sb("heads_t", [P, 2, 2, SEQ], F32)

        score_ps = [psum(f"score_ps{b}", [P, 512], F32) for b in range(2)]
        shift_ps = [psum(f"shift_ps{b}", [P, 512], F32) for b in range(2)]
        pv_ps = psum("pv_ps", [P, 512], F32)
        nat_ps = psum("nat_ps", [P, 512], F32)
        misc_ps = psum("misc_ps", [P, 512], F32)
        max_ps = misc_ps[:].bitcast(BF16)[0:SEQ, 0:P]
        back_ps = misc_ps[:, 0:2 * P]
        out_ps = psum("out_ps", [P, EMBED], F32)

        consts_in, identb_ready = sem("consts_in"), sem("identb_ready")
        scores_done, max_ready, hi_ready, minus_ready = (
            sem("scores_done"), sem("max_ready"), sem("hi_ready"), sem("minus_ready"))
        max_t_done, max_t_ready = sem("max_t_done"), sem("max_t_ready")
        shifted_done, probs_ready = sem("shifted_done"), sem("probs_ready")
        pv_done, pv_ready = sem("pv_done"), sem("pv_ready")
        nat_done, recip_ready, heads_ready = sem("nat_done"), sem("recip_ready"), sem("heads_ready")
        back_done, heads_t_ready = sem("back_done"), sem("heads_t_ready")
        out_done, x_ready = sem("out_done"), sem("x_ready")
        LOADS = 2 * (2 * len(Q_PART)) + 1
        PERIOD = 2 * CHUNK_TILES

        block = ctx.enter_context(nc.Block())

        @block.sync
        def _(sp):
            sp.dma_start(select[:], io.select).then_inc(consts_in, 16)
            sp.dma_start(w_out[:], io.wfc).then_inc(consts_in, 16)

            for src, dst in keep.prefetch:
                sp.dma_start(dst, src).then_inc(keep.prefetched, 16)
            with sp.Fori(1, CHUNKS // 2) as r:
                for b in range(2):
                    sp.wait_ge(pv_done, CHUNK_TILES * (2 * r + b - 1))
                    load_operands(sp, io, keep, 2 * r + b, b)
            sp.wait_ge(keep.prefetched, 16 * len(keep.prefetch))

        @block.tensor
        def _(pe):
            pe.wait_ge(consts_in, 32)
            pe.wait_ge(identb_ready, 1)

            def scores(k, p, us, kc, turn):
                b, i = kc
                if us[0] == 0:
                    pe.wait_ge(qkv_in[b], 16 * LOADS * (turn + 1))
                for u in us:
                    if UNITS * k + u >= 2:
                        pe.wait_ge(max_ready, UNITS * p + u - 1)
                    for j in range(4):
                        g, hp = 2 * u + j // 2, 4 * u + j
                        q = q_op[b][:, 2 * hp:2 * hp + 2].rearrange("p h (q i) -> p (h q) i", i=CHUNK_TILES)[:, :, i]
                        kk = k_op[b][:, g].rearrange("p a (q i) -> p (a q) i", i=CHUNK_TILES)[:, :, i]
                        last = nc.tensor.matmul(score_ps[u % 2][:, j * P:(j + 1) * P], q, kk,
                                                start=True, stop=True)
                    last.then_inc(scores_done, 1)

            def transpose_max(k, p):
                tile, before = held(pe, p + 1), held(pe, p - 1)
                pe.wait_ge(identb_ready, 1)
                pe.wait_ge(minus_ready, tile)
                if k >= 2:
                    pe.wait_ge(heads_t_ready, before)
                nc.tensor.transpose(max_ps, minus_max[:, k % 2].rearrange("p t n -> p (t n)"), ident_b[:]
                                    ).then_inc(max_t_done, 1)

            def shifted(k, p, u, kc):
                b, i = kc
                if u == 0:
                    pe.wait_ge(max_t_ready, p + 1)
                if UNITS * k + u >= 2:
                    pe.wait_ge(probs_ready, UNITS * p + u - 1)
                for g in (2 * u, 2 * u + 1):
                    out = shift_ps[u % 2][:, (g % 2) * 256:(g % 2) * 256 + 256]
                    q = q_op[b][:, 4 * g:4 * g + 4].rearrange("p h (q i) -> p (h q) i", i=CHUNK_TILES)[:, :, i]
                    kk = k_op[b][:, g].rearrange("p a (q i) -> p (a q) i", i=CHUNK_TILES)[:, :, i]
                    nc.tensor.matmul(out, kk, q, start=True, stop=False)
                    for j in range(2):
                        last = nc.tensor.matmul(out[:, j * P:(j + 1) * P], select[:, 2 * g + j, :],
                                                max_t[:, k % 2, :], start=False, stop=(j == 1))
                last.then_inc(shifted_done, 1)

            def values(k, p, u, kc):
                b, i = kc
                if u == 0 and k >= 1:
                    pe.wait_ge(pv_ready, p)
                pe.wait_ge(probs_ready, UNITS * p + u + 1)
                for g in (2 * u, 2 * u + 1):
                    gi, half = g % 4, g // 4
                    last = nc.tensor.matmul(pv_ps[32 * gi:32 * gi + 32, 256 * half:256 * half + 256],
                                            v_op[b][:, i, g, :], probs[:, u, (g % 2) * 256:(g % 2) * 256 + 256],
                                            start=True, stop=True)
                if u == UNITS - 1:
                    last.then_inc(pv_done, 1)

            def to_tokens(k, p):
                pe.wait_ge(pv_ready, p + 1)
                if k >= 1:
                    pe.wait_ge(heads_ready, p)
                for n in range(4):
                    last = nc.tensor.transpose(nat_ps[:, n * P:(n + 1) * P], pv_sb[:, n * P:(n + 1) * P],
                                               ident[:])
                last.then_inc(nat_done, 1)

            def to_features(k, p, more):
                pe.wait_ge(heads_ready, p + 1)
                if more:
                    pe.wait_ge(max_t_ready, p + 2)
                for a in range(2):
                    last = nc.tensor.transpose(back_ps[:, a * P:(a + 1) * P], heads_out[:, a, :], ident[:])
                last.then_inc(back_done, 1)

            def project_out(k, p):
                pe.wait_ge(heads_t_ready, p + 1)
                if k >= 1:
                    pe.wait_ge(x_ready, p)
                for jj in range(2):
                    last = nc.tensor.matmul(out_ps[:], heads_t[:, jj].rearrange("p a q -> p (a q)"),
                                            w_out[:, jj], start=(jj == 0), stop=(jj == 1))
                last.then_inc(out_done, 1)

            def slot(k, r):
                s = k + PERIOD * r
                now = ((k // CHUNK_TILES) % 2, k % CHUNK_TILES)
                before = (((k - 1) // CHUNK_TILES) % 2, (k - 1) % CHUNK_TILES)
                turn = k // PERIOD + r
                a_on, b_on, f_on = k <= TILES - 1, 1 <= k <= TILES, 2 <= k
                if b_on:
                    transpose_max(k - 1, s - 1)
                if a_on:
                    scores(k, s, (0, 1), now, turn)
                if f_on:
                    to_tokens(k - 2, s - 2)
                if a_on:
                    scores(k, s, (2, 3), now, turn)
                if b_on:
                    shifted(k - 1, s - 1, 0, before)
                    shifted(k - 1, s - 1, 1, before)
                if f_on:
                    to_features(k - 2, s - 2, b_on)
                if b_on:
                    shifted(k - 1, s - 1, 2, before)
                    values(k - 1, s - 1, 0, before)
                    shifted(k - 1, s - 1, 3, before)
                    values(k - 1, s - 1, 1, before)
                if f_on:
                    project_out(k - 2, s - 2)
                if b_on:
                    values(k - 1, s - 1, 2, before)
                    values(k - 1, s - 1, 3, before)
            for s in range(run_slots(pe, TILES, 3, PERIOD, slot), TILES + 2):
                slot(s, 0)

        @block.scalar
        def _(act):
            def exponentials(k, p, us):
                for u in us:
                    act.wait_ge(shifted_done, UNITS * p + u + 1)
                    if u == 0 and k >= 1:
                        act.wait_ge(pv_done, p)
                    nc.scalar.activation(probs[:, u], shift_ps[u % 2][:], ACT.Exp).then_inc(probs_ready, 1)

            def copy_pv(k, p):
                act.wait_ge(pv_done, p + 1)
                if k >= 1:
                    act.wait_ge(nat_done, p)
                nc.scalar.activation(pv_sb[:], pv_ps[:], ACT.Copy).then_inc(pv_ready, 1)

            def copy_heads(k, p):
                act.wait_ge(back_done, p + 1)
                if k >= 1:
                    act.wait_ge(out_done, p)
                nc.scalar.activation(heads_t[:].rearrange("p j a q -> p a j q"),
                                     back_ps.rearrange("p (a j q) -> p a j q", a=2, j=2),
                                     ACT.Copy).then_inc(heads_t_ready, 1)

            def slot(k, r):
                s = k + PERIOD * r
                b_on, f_on = 1 <= k <= TILES, 2 <= k
                if b_on:
                    exponentials(k - 1, s - 1, (0, 1))
                if f_on:
                    copy_heads(k - 2, s - 2)
                if b_on:
                    exponentials(k - 1, s - 1, (2, 3))
                    copy_pv(k - 1, s - 1)
            for s in range(run_slots(act, TILES, 3, PERIOD, slot), TILES + 2):
                slot(s, 0)

        @block.vector
        def _(dve):
            dve.wait_ge(consts_in, 32)
            nc.vector.tensor_copy(ident_b[:], ident[:]).then_inc(identb_ready, 1)

            def maxima(k, p, us):
                for u in us:
                    dve.wait_ge(scores_done, UNITS * p + u + 1)
                    if u == 0 and k >= 2:
                        dve.wait_ge(minus_ready, p - 1)
                    nc.vector.reduce_max(row_max[:, k % 2, 8 * u:8 * u + 8],
                                         score_ps[u % 2][:].rearrange("p (n t) -> p n t", t=SEQ), AX.X
                                         ).then_inc(max_ready, 1)

            def negate_maxima(k, p):
                dve.wait_ge(max_ready, UNITS * (p + 1))
                if k >= 2:
                    dve.wait_ge(max_t_done, p - 1)
                nc.vector.tensor_scalar(minus_max[:, k % 2, 0], row_max[:, k % 2], -1.0, None, ALU.mult
                                        ).then_inc(hi_ready, 1)
                dve.wait_ge(hi_ready, p + 1)
                nc.vector.scalar_tensor_tensor(minus_max[:, k % 2, 1], row_max[:, k % 2], -1.0,
                                               minus_max[:, k % 2, 0], ALU.mult, ALU.subtract
                                               ).then_inc(minus_ready, 1)

            def copy_max(k, p):
                dve.wait_ge(max_t_done, p + 1)
                if k >= 2:
                    dve.wait_ge(shifted_done, UNITS * (p - 1))
                nc.vector.tensor_copy(max_t[:, k % 2], max_ps).then_inc(max_t_ready, 1)

            def normalise(k, p):
                sums = nat_ps[:].rearrange("p (n m) -> p n m", m=16)
                dve.wait_ge(nat_done, p + 1)
                if k >= 1:
                    dve.wait_ge(heads_ready, p)
                nc.vector.reciprocal(recip[:], sums[:, :, 8]).then_inc(recip_ready, 1)
                dve.wait_ge(recip_ready, p + 1)
                if k >= 1:
                    dve.wait_ge(back_done, p)
                nc.vector.tensor_tensor(
                    heads_out[:].rearrange("p a (n d) -> p n a d", d=HEAD_DIM),
                    nat_ps[:].rearrange("p (n a m) -> p n a m", a=2, m=16)[:, :, :, 0:8],
                    recip[:].rearrange("p (n a) -> p n a", a=2).unsqueeze(3).to_broadcast([P, HP, 2, HEAD_DIM]),
                    ALU.mult).then_inc(heads_ready, 1)

            def add_residual(k, p):
                dve.wait_ge(out_done, p + 1)
                nc.vector.tensor_tensor(x_sb[:, bass.ds(p, 1), :], out_ps[:].unsqueeze(1),
                                        x_sb[:, bass.ds(p, 1), :], ALU.add).then_inc(x_ready, 1)

            def slot(k, r):
                s = k + PERIOD * r
                a_on, b_on, f_on = k <= TILES - 1, 1 <= k <= TILES, 2 <= k
                if b_on:
                    copy_max(k - 1, s - 1)
                if a_on:
                    maxima(k, s, (0, 1))
                if f_on:
                    normalise(k - 2, s - 2)
                if a_on:
                    maxima(k, s, (2, 3))
                    negate_maxima(k, s)
                if f_on:
                    add_residual(k - 2, s - 2)
            for s in range(run_slots(dve, TILES, 3, PERIOD, slot), TILES + 2):
                slot(s, 0)


MAX_TILES = TOKENS * TOP_K // P + EXPERTS - 1
SHARED = EXPERTS
WINDOW, WINDOW_FIRST = 7, 4
WINDOWS = len(range(WINDOW_FIRST, MAX_TILES - WINDOW + 1, 4))
SHARED_FIRST = 16


def routing_phase(nc, ctx0, io, keep):
    with ExitStack() as ctx:
        def sb(name, shape, dt):
            return ctx.enter_context(nc.sbuf_tensor(name, shape, dt))

        def psum(name, shape, dt):
            return ctx.enter_context(nc.psum_tensor(name, shape, dt))

        def sem(name):
            return ctx.enter_context(nc.semaphore(name))

        x_sb, ident, xn_all = keep.x_sb, keep.ident, keep.xn_all
        NE = TILES * EXPERTS
        stats = sb("r_stats", [P, 2, CHUNK_TILES, 6], F32)
        mean_var = sb("r_mean_var", [P, 2, CHUNK_TILES, 2], F32)
        var_eps = sb("r_var_eps", [P, 2, CHUNK_TILES], F32)
        rstd = sb("r_rstd", [P, 2, CHUNK_TILES], F32)
        minus_half = sb("r_minus_half", [P, CHUNK_TILES], F32)
        xn = sb("r_xn", [P, 2, CHUNK_TILES, EMBED], F32)
        xn_t = sb("r_xn_t", [P, 2, HALVES, CHUNK], F32)
        gate = sb("r_gate", [P, HALVES, EXPERTS], F32)
        logit_t = sb("r_logit_t", [EXPERTS, CHUNK], F32)
        expert_iota = sb("r_expert_iota", [P, EXPERTS], F32)
        tile_iota = sb("r_tile_iota", [1, MAX_TILES], F32)
        before, ones = sb("r_before", [P, P], BF16), sb("r_ones", [P, P], BF16)
        logits = sb("r_logits", [P, TILES, EXPERTS], F32)
        work = sb("r_work", [P, TILES, EXPERTS], F32)
        scores = sb("r_scores", [P, TILES, EXPERTS], F32)
        hot = [sb(f"r_hot{n}", [P, TILES, EXPERTS], F32) for n in range(TOP_K)]
        mask = sb("r_mask", [P, TILES, EXPERTS], BF16)
        col = sb("r_col", [P, 8, TILES], F32)
        PAD = TILES // 2
        scan = [sb(f"r_scan{n}", [P, EXPERTS, PAD + TILES], F32) for n in range(2)]
        tiles_i = sb("r_tiles_i", [P, 2, EXPERTS], I32)
        ends = [sb(f"r_ends{n}", [P, EXPERTS // 2 + EXPERTS], F32) for n in range(2)]
        place = sb("r_place", [P, TILES, EXPERTS], F32)
        of_tile = sb("r_of_tile", [1, MAX_TILES, EXPERTS], F32)
        window_sum = sb("r_window_sum", [1, WINDOWS], F32)
        of_tile_sum = sb("r_of_tile_sum", [1, MAX_TILES], F32)

        xt_ps = [psum(f"r_xt_ps{i}", [P, CHUNK], F32) for i in range(HALVES)]
        gate_ps = psum("r_gate_ps", [EXPERTS, CHUNK], F32)
        logit_ps = psum("r_logit_ps", [P, CHUNK_TILES, EXPERTS], F32)
        rank_ps = psum("r_rank_ps", [P, TILES, EXPERTS], F32)
        count_ps = psum("r_count_ps", [P, TILES, EXPERTS], F32)

        consts_in, half_set = sem("r_consts_in"), sem("r_half_set")
        stats_done, stats_ready, eps_added, rstd_ready = (
            sem("r_stats_done"), sem("r_stats_ready"), sem("r_eps_added"), sem("r_rstd_ready"))
        xn_ready, kept, xt_done, xt_ready = (
            sem("r_xn_ready"), sem("r_kept"), sem("r_xt_done"), sem("r_xt_ready"))
        gate_done, gate_ready, logit_done, logit_ready = (
            sem("r_gate_done"), sem("r_gate_ready"), sem("r_logit_done"), sem("r_logit_ready"))
        step, exp_done, mask_ready, ranked = sem("r_step"), sem("r_exp_done"), sem("r_mask_ready"), sem("r_ranked")

        block = ctx.enter_context(nc.Block())

        @block.sync
        def _(sp):
            for dst, src in ((gate, io.gate), (expert_iota, io.expert_iota), (tile_iota, io.tile_iota),
                             (before, io.before)):
                sp.dma_start(dst[:], src).then_inc(consts_in, 16)
            sp.wait_ge(consts_in, 64)

        @block.gpsimd
        def _(pool):
            nc.gpsimd.memset(minus_half[:], -0.5).then_inc(half_set, 1)
            nc.gpsimd.memset(ones[:], 1.0).then_inc(half_set, 1)
            for n in range(2):
                nc.gpsimd.memset(scan[n][:], 0.0).then_inc(half_set, 1)
                nc.gpsimd.memset(ends[n][:], 0.0).then_inc(half_set, 1)
            pool.wait_ge(half_set, 1)

            def reciprocal_deviation(k, r):
                c, b = k + 2 * r, k % 2
                tiles, before = held(pool, CHUNK_TILES * (c + 1)), held(pool, CHUNK_TILES * (c - 1))
                pool.wait_ge(half_set, 1)
                pool.wait_ge(stats_ready, tiles)
                if k >= 2:
                    pool.wait_ge(xn_ready, before)
                nc.gpsimd.tensor_scalar(var_eps[:, b], mean_var[:, b, :, 1], EPS, None, ALU.add
                                        ).then_inc(eps_added, 1)
                pool.wait_ge(eps_added, c + 1)
                nc.gpsimd.tensor_tensor(rstd[:, b], var_eps[:, b], minus_half[:], ALU.pow
                                        ).then_inc(rstd_ready, 1)
            for s in range(run_slots(pool, CHUNKS, 2, 2, reciprocal_deviation), CHUNKS):
                reciprocal_deviation(s, 0)

        @block.scalar
        def _(act):
            def evacuate(k, c, b):
                act.wait_ge(xt_done, c + 1)
                if k >= 2:
                    act.wait_ge(gate_done, c - 1)
                for h in range(HALVES):
                    nc.scalar.activation(xn_t[:, b, h], xt_ps[h][:], ACT.Copy).then_inc(xt_ready, 1)

            def keep_normalised(c, b):
                act.wait_ge(xn_ready, CHUNK_TILES * (c + 1))
                nc.scalar.activation(xn_all[:, bass.ds(c * CHUNK_TILES, CHUNK_TILES), :], xn[:, b], ACT.Copy
                                     ).then_inc(kept, 1)

            def copy_gate(k, c):
                act.wait_ge(gate_done, c + 1)
                if k >= 1:
                    act.wait_ge(logit_done, c)
                nc.scalar.activation(logit_t[:], gate_ps[:], ACT.Copy).then_inc(gate_ready, 1)

            def slot(k, r):
                s = k + 2 * r
                if k <= CHUNKS - 1:
                    evacuate(k, s, k % 2)
                if k >= 1:
                    copy_gate(k - 1, s - 1)
                if k <= CHUNKS - 1:
                    keep_normalised(s, k % 2)
            for s in range(run_slots(act, CHUNKS, 2, 2, slot), CHUNKS + 1):
                slot(s, 0)
            act.wait_ge(exp_done, 1)
            nc.scalar.activation(scores[:], work[:], ACT.Exp).then_inc(exp_done, 1)

        @block.tensor
        def _(pe):
            pe.wait_ge(consts_in, 64)

            def transpose_x(k, c, b):
                pe.wait_ge(xn_ready, CHUNK_TILES * (c + 1))
                if k >= 1:
                    pe.wait_ge(xt_ready, HALVES * c)
                for i in range(CHUNK_TILES):
                    for h in range(HALVES):
                        last = nc.tensor.transpose(xt_ps[h][:, i * P:(i + 1) * P],
                                                   xn[:, b, i, h * P:(h + 1) * P], ident[:])
                last.then_inc(xt_done, 1)

            def gate_scores(k, c, b):
                pe.wait_ge(xt_ready, HALVES * (c + 1))
                if k >= 1:
                    pe.wait_ge(gate_ready, c)
                for h in range(HALVES):
                    last = nc.tensor.matmul(gate_ps[:], gate[:, h], xn_t[:, b, h],
                                            start=(h == 0), stop=(h == HALVES - 1))
                last.then_inc(gate_done, 1)

            def transpose_logits(k, c):
                chunks, before = held(pe, c + 1), held(pe, c)
                pe.wait_ge(consts_in, 64)
                pe.wait_ge(gate_ready, chunks)
                if k >= 1:
                    pe.wait_ge(logit_ready, before)
                for i in range(CHUNK_TILES):
                    last = nc.tensor.transpose(logit_ps[:, i, :], logit_t[:, i * P:(i + 1) * P],
                                               ident[0:EXPERTS, 0:EXPERTS])
                last.then_inc(logit_done, 1)

            def slot(k, r):
                s = k + 2 * r
                if k <= CHUNKS - 1:
                    transpose_x(k, s, k % 2)
                if 1 <= k <= CHUNKS:
                    gate_scores(k - 1, s - 1, (k - 1) % 2)
                if k >= 2:
                    transpose_logits(k - 2, s - 2)
            for s in range(run_slots(pe, CHUNKS, 3, 2, slot), CHUNKS + 2):
                slot(s, 0)
            pe.wait_ge(half_set, 6)
            pe.wait_ge(mask_ready, 1)
            chosen = mask[:].rearrange("p t e -> p (t e)")
            nc.tensor.matmul(rank_ps[:].rearrange("p t e -> p (t e)"), before[:], chosen, start=True, stop=True)
            nc.tensor.matmul(count_ps[:].rearrange("p t e -> p (t e)"), ones[:], chosen, start=True, stop=True
                             ).then_inc(ranked, 1)

        @block.vector
        def _(dve):
            def moments(k, c, b):
                for i in range(CHUNK_TILES):
                    nc.vector.bn_stats(stats[:, b, i, :], x_sb[:, bass.ds(c * CHUNK_TILES + i, 1), :]
                                       ).then_inc(stats_done, 1)
                for i in range(CHUNK_TILES):
                    so_far = held(dve, CHUNK_TILES * c + i + 1)
                    dve.wait_ge(half_set, 1)
                    dve.wait_ge(stats_done, so_far)
                    nc.vector.bn_aggr(mean_var[:, b, i, :], stats[:, b, i, :]).then_inc(stats_ready, 1)

            def normalise(k, c, b):
                dve.wait_ge(rstd_ready, c + 1)
                if k >= 2:
                    dve.wait_ge(xt_done, c - 1)
                    dve.wait_ge(kept, c - 1)
                for i in range(CHUNK_TILES):
                    nc.vector.tensor_scalar(xn[:, b, i, :], x_sb[:, bass.ds(c * CHUNK_TILES + i, 1), :],
                                            mean_var[:, b, i, 0:1], rstd[:, b, i:i + 1],
                                            ALU.subtract, ALU.mult).then_inc(xn_ready, 1)

            def copy_logits(c):
                dve.wait_ge(logit_done, c + 1)
                nc.vector.tensor_copy(logits[:, bass.ds(c * CHUNK_TILES, CHUNK_TILES), :], logit_ps[:]
                                      ).then_inc(logit_ready, 1)

            def slot(k, r):
                s = k + 2 * r
                if 1 <= k <= CHUNKS:
                    normalise(k - 1, s - 1, (k - 1) % 2)
                if k <= CHUNKS - 1:
                    moments(k, s, k % 2)
                if k >= 4:
                    copy_logits(s - 4)
            for s in range(run_slots(dve, CHUNKS, 4, 2, slot), CHUNKS + 4):
                slot(s, 0)

            done = [0]

            def then(instruction):
                instruction.then_inc(step, 1)
                done[0] += 1
                dve.wait_ge(step, done[0])

            def by_tile(c):
                return c.unsqueeze(2).to_broadcast([P, TILES, EXPERTS])

            iota = expert_iota[:].unsqueeze(1).to_broadcast([P, TILES, EXPERTS])
            dve.wait_ge(half_set, 6)
            dve.wait_ge(consts_in, 64)
            dve.wait_ge(logit_ready, CHUNKS)
            then(nc.vector.reduce_max(col[:, 0], logits[:], AX.X))
            nc.vector.tensor_tensor(work[:], logits[:], by_tile(col[:, 0]), ALU.subtract).then_inc(exp_done, 1)
            dve.wait_ge(exp_done, 2)
            then(nc.vector.reduce_sum(col[:, 1], scores[:], AX.X))
            then(nc.vector.reciprocal(col[:, 2], col[:, 1]))
            then(nc.vector.tensor_tensor(scores[:], scores[:], by_tile(col[:, 2]), ALU.mult))
            for n in range(TOP_K):
                best = col[:, 3 + n]
                then(nc.vector.reduce_max(best, scores[:], AX.X))
                then(nc.vector.tensor_tensor(work[:], scores[:], by_tile(best), ALU.is_equal))
                then(nc.vector.scalar_tensor_tensor(work[:], work[:], -float(EXPERTS), iota, ALU.mult, ALU.add))
                then(nc.vector.tensor_reduce(col[:, 5], work[:], AX.X, ALU.min))
                then(nc.vector.tensor_scalar(col[:, 5], col[:, 5], float(EXPERTS), None, ALU.add))
                then(nc.vector.tensor_tensor(hot[n][:], iota, by_tile(col[:, 5]), ALU.is_equal))
                if n == 0:
                    then(nc.vector.scalar_tensor_tensor(scores[:], hot[0][:], -2.0, scores[:], ALU.mult, ALU.add))
            nc.vector.tensor_tensor(mask[:], hot[0][:], hot[1][:], ALU.add).then_inc(mask_ready, 1)
            then(nc.vector.tensor_tensor(col[:, 6], col[:, 3], col[:, 4], ALU.add))
            then(nc.vector.tensor_scalar(col[:, 6], col[:, 6], 1e-20, None, ALU.add))
            then(nc.vector.reciprocal(col[:, 7], col[:, 6]))
            for n in range(TOP_K):
                then(nc.vector.tensor_tensor(keep.weight[:, n], col[:, 3 + n], col[:, 7], ALU.mult))
            dve.wait_ge(ranked, 1)
            then(nc.vector.tensor_copy(scan[0][:, :, PAD:], count_ps[:].rearrange("p t e -> p e t")))
            side, far = 0, 1
            while far < TILES:
                then(nc.vector.tensor_tensor(scan[1 - side][:, :, PAD:], scan[side][:, :, PAD:],
                                             scan[side][:, :, PAD - far:PAD + TILES - far], ALU.add))
                side, far = 1 - side, 2 * far
            upto = scan[side]
            then(nc.vector.tensor_scalar(tiles_i[:, 0], upto[:, :, PAD + TILES - 1], float(P - 1), None, ALU.add))
            then(nc.vector.tensor_scalar(tiles_i[:, 1], tiles_i[:, 0], 7, None, ALU.logical_shift_right))
            LEFT = EXPERTS // 2
            then(nc.vector.tensor_copy(ends[0][:, LEFT:], tiles_i[:, 1]))
            e_side, far = 0, 1
            while far < EXPERTS:
                then(nc.vector.tensor_tensor(ends[1 - e_side][:, LEFT:], ends[e_side][:, LEFT:],
                                             ends[e_side][:, LEFT - far:LEFT + EXPERTS - far], ALU.add))
                e_side, far = 1 - e_side, 2 * far
            end = ends[e_side]
            first_tile = end[:, LEFT - 1:LEFT + EXPERTS - 1].unsqueeze(1).to_broadcast([P, TILES, EXPERTS])
            then(nc.vector.tensor_tensor(place[:], rank_ps[:],
                                         upto[:, :, PAD - 1:PAD + TILES - 1].rearrange("p e t -> p t e"), ALU.add))
            then(nc.vector.scalar_tensor_tensor(place[:], first_tile, float(P), place[:], ALU.mult, ALU.add))
            for n in range(TOP_K):
                then(nc.vector.tensor_tensor(work[:], hot[n][:], place[:], ALU.mult))
                then(nc.vector.reduce_sum(col[:, 5], work[:], AX.X))
                then(nc.vector.tensor_copy(keep.row[:, n], col[:, 5]))
            then(nc.vector.tensor_tensor(
                of_tile[:], end[0:1, LEFT:].unsqueeze(1).to_broadcast([1, MAX_TILES, EXPERTS]),
                tile_iota[:].unsqueeze(2).to_broadcast([1, MAX_TILES, EXPERTS]), ALU.is_le))
            then(nc.vector.reduce_sum(of_tile_sum[:], of_tile[:], AX.X))
            then(nc.vector.tensor_scalar(of_tile_sum[:], of_tile_sum[:], float(EXPERTS - 1), None, ALU.min))
            then(nc.vector.tensor_copy(keep.tile_expert[:], of_tile_sum[:]))
            then(nc.vector.tensor_copy(window_sum[:], of_tile_sum[:, WINDOW_FIRST:MAX_TILES - WINDOW + 1:4]))
            for n in range(1, WINDOW):
                then(nc.vector.scalar_tensor_tensor(
                    window_sum[:], of_tile_sum[:, WINDOW_FIRST + n:MAX_TILES - WINDOW + 1 + n:4],
                    float(EXPERTS ** n), window_sum[:], ALU.mult, ALU.add))
            then(nc.vector.tensor_copy(keep.windows[:], window_sum[:]))


def ffn_phase(nc, ctx0, io, keep):
    with ExitStack() as ctx:
        def sb(name, shape, dt):
            return ctx.enter_context(nc.sbuf_tensor(name, shape, dt))

        def psum(name, shape, dt):
            return ctx.enter_context(nc.psum_tensor(name, shape, dt))

        def sem(name):
            return ctx.enter_context(nc.semaphore(name))

        x_sb, ident, xn_all = keep.x_sb, keep.ident, keep.xn_all
        w_up, w_down, w_down_b = keep.w_up, keep.w_down, keep.w_down_b
        WAYS = 4
        x_in = [sb(f"f_x_in{way}", [P, EMBED], F32) for way in range(WAYS)]
        x_t = [sb(f"f_x_t{b}", [P, HALVES, P], F32) for b in range(2)]
        gated = [sb(f"f_gated{b}", [P, INNER], F32) for b in range(2)]
        act_sb = [sb(f"f_act{b}", [P, INNER], F32) for b in range(2)]
        act_t = [sb(f"f_act_t{b}", [P, 2, P], F32) for b in range(2)]
        y_sb = [sb(f"f_y{way}", [P, EMBED], F32) for way in range(WAYS)]
        chosen = sb("f_chosen", [P, TILES, TOP_K, EMBED], F32)

        xt_ps = [psum(f"f_xt_ps{b}", [P, HALVES, P], F32) for b in range(2)]
        up_ps = [psum(f"f_up_ps{b}", [P, 2 * INNER], F32) for b in range(2)]
        at_ps = [psum(f"f_at_ps{b}", [P, 2, P], F32) for b in range(2)]
        y_ps = [psum(f"f_y_ps{b}", [P, EMBED], F32) for b in range(2)]

        x_loaded = [sem(f"f_x_loaded{way}") for way in range(WAYS)]
        sorted_in, y_stored = sem("f_sorted_in"), [sem(f"f_y_stored{way}") for way in range(WAYS)]
        xt_done, xt_ready = sem("f_xt_done"), sem("f_xt_ready")
        up_done, gated_ready, act_ready = sem("f_up_done"), sem("f_gated_ready"), sem("f_act_ready")
        at_done, at_a_ready, at_b_ready = sem("f_at_done"), sem("f_at_a_ready"), sem("f_at_b_ready")
        down_done, y_ready = sem("f_down_done"), sem("f_y_ready")
        gathered = [sem(f"f_gathered{n}") for n in range(TILES)]
        summed, added, out_stored = sem("f_summed"), sem("f_added"), sem("f_out_stored")

        ITEMS = TILES + MAX_TILES
        COMBINE_LAG = 4
        EXPERT_END = SHARED_FIRST + MAX_TILES

        def tile_of(k, r):
            return (k if k < SHARED_FIRST else k - MAX_TILES) + WAYS * r

        def is_sorted(k):
            return SHARED_FIRST <= k < EXPERT_END

        def pipeline(eng, stages, ahead=None, straight=None):
            lag = len(stages) - 1

            def slot(k, r, slots=1):
                if ahead is not None and slots > 0:
                    ahead(k, r, slots)
                for j in range(lag, -1, -1):
                    if stages[j] is not None and 0 <= k - j < ITEMS:
                        stages[j](k - j, r)

            s = 0
            for start, end in ((0, SHARED_FIRST), (SHARED_FIRST, EXPERT_END), (EXPERT_END, ITEMS)):
                while s < min(end, start + lag + WAYS):
                    slot(s, 0)
                    s += 1
                turns = (end - s) // WAYS
                if turns > 1 and start != straight:
                    with eng.Fori(0, turns) as r:
                        for i in range(WAYS):
                            slot(s + i, r, WAYS if i == 0 else 0)
                    s += WAYS * turns
                while s < end:
                    slot(s, 0)
                    s += 1
            for s in range(ITEMS, ITEMS + lag):
                slot(s, 0)

        block = ctx.enter_context(nc.Block())

        @block.sync
        def _(sp):
            def load(k, r):
                way = k % WAYS
                if k >= WAYS:
                    sp.wait_ge(xt_done, k + WAYS * r - WAYS + 1)
                if is_sorted(k):
                    if k == SHARED_FIRST:
                        sp.wait_ge(sorted_in, 16 * TOP_K * TILES)
                    sp.dma_start(x_in[way][:], io.sorted_x[bass.ds((k - SHARED_FIRST + WAYS * r) * P, P), :]
                                 ).then_inc(x_loaded[way], 16)
                else:
                    sp.dma_start(x_in[way][:].unsqueeze(1), xn_all[:, bass.ds(tile_of(k, r), 1), :]
                                 ).then_inc(x_loaded[way], 16)

            def store(k, r):
                if is_sorted(k):
                    sp.wait_ge(y_ready, k + WAYS * r + 1)
                    sp.dma_start(io.sorted_y[bass.ds((k - SHARED_FIRST + WAYS * r) * P, P), :],
                                 y_sb[k % WAYS][:]).then_inc(y_stored[k % WAYS], 16)
            pipeline(sp, [load, None, None, None, None, None, store])
            for t in range(TILES):
                sp.wait_ge(summed, t + 1)
                sp.dma_start(io.out[t * P:(t + 1) * P, :], x_sb[:, t, :]).then_inc(out_stored, 16)
            sp.wait_ge(out_stored, 16 * TILES)

        @block.gpsimd
        def _(pool):
            for t in range(TILES):
                for n in range(TOP_K):
                    nc.gpsimd.indirect_dma_start(
                        io.sorted_x, bass.IndirectOffsetOnAxis(ap=keep.row[:, n, t:t + 1], axis=0),
                        xn_all[:, t, :], None).then_inc(sorted_in, 16)
            for way in range(WAYS):
                pool.wait_ge(y_stored[way], 16 * len(range(way, MAX_TILES, WAYS)))
            for t in range(TILES):
                for n in range(TOP_K):
                    nc.gpsimd.indirect_dma_start(
                        chosen[:, t, n, :], None,
                        io.sorted_y, bass.IndirectOffsetOnAxis(ap=keep.row[:, n, t:t + 1], axis=0)
                        ).then_inc(gathered[t], 16)

        @block.tensor
        def _(pe):
            def transpose_x(k, r):
                b, way = k % 2, k % WAYS
                pe.wait_ge(x_loaded[way], 16 * (k // WAYS + 1 + r))
                if k >= 2:
                    pe.wait_ge(xt_ready, k + WAYS * r - 1)
                for h in range(HALVES):
                    last = nc.tensor.transpose(xt_ps[b][:, h], x_in[way][:, h * P:(h + 1) * P], ident[:])
                last.then_inc(xt_done, 1)

            experts = {}

            def find_experts(k, r, slots):
                window = None if slots == 1 else pe.value_load(
                    keep.windows[0:1, bass.ds(r, 1)], min_val=0, max_val=EXPERTS ** WINDOW - 1)
                for n, item in enumerate(range(k - 3, k + slots - 1)):
                    if not is_sorted(item):
                        experts[item] = slice(SHARED, SHARED + 1)
                    elif window is not None:
                        experts[item] = bass.ds(pe.snap((window >> (3 * n)) & (EXPERTS - 1),
                                                        min_val=0, max_val=EXPERTS - 1), 1)
                    elif slots == 1 and r == 0 and item not in fresh:
                        fresh.add(item)
                        experts[item] = bass.ds(pe.value_load(
                            keep.tile_expert[0:1, item - SHARED_FIRST:item - SHARED_FIRST + 1],
                            min_val=0, max_val=EXPERTS - 1), 1)
            fresh = set()

            def up(k, r):
                b, e = k % 2, experts[k]
                pe.wait_ge(xt_ready, k + WAYS * r + 1)
                if k >= 2:
                    pe.wait_ge(act_ready, k + WAYS * r - 1)
                for h in range(HALVES):
                    last = nc.tensor.matmul(up_ps[b][:], x_t[b][:, h], w_up[:, h, e, :],
                                            start=(h == 0), stop=(h == HALVES - 1))
                last.then_inc(up_done, 1)

            def transpose_act(k, r):
                b = k % 2
                pe.wait_ge(act_ready, k + WAYS * r + 1)
                if k >= 2:
                    pe.wait_ge(at_a_ready, k + WAYS * r - 1)
                    pe.wait_ge(at_b_ready, k + WAYS * r - 1)
                nc.tensor.transpose(at_ps[b][:, 0], act_sb[b][:, 0:P], ident[:])
                nc.tensor.transpose(at_ps[b][0:INNER_B, 1], act_sb[b][:, P:INNER], ident[:]).then_inc(at_done, 1)

            def down(k, r):
                b, e = k % 2, experts[k]
                pe.wait_ge(at_a_ready, k + WAYS * r + 1)
                pe.wait_ge(at_b_ready, k + WAYS * r + 1)
                if k >= 2:
                    pe.wait_ge(y_ready, k + WAYS * r - 1)
                nc.tensor.matmul(y_ps[b][:], act_t[b][:, 0], w_down[:, e, :], start=True, stop=False)
                nc.tensor.matmul(y_ps[b][:], act_t[b][0:INNER_B, 1], w_down_b[:, e, :], start=False, stop=True
                                 ).then_inc(down_done, 1)
            pipeline(pe, [transpose_x, up, transpose_act, down], find_experts)

        @block.scalar
        def _(act):
            def copy_x(k, r):
                b = k % 2
                act.wait_ge(xt_done, k + WAYS * r + 1)
                if k >= 2:
                    act.wait_ge(up_done, k + WAYS * r - 1)
                nc.scalar.activation(x_t[b][:], xt_ps[b][:], ACT.Copy).then_inc(xt_ready, 1)

            def gate(k, r):
                b = k % 2
                act.wait_ge(up_done, k + WAYS * r + 1)
                if k >= 2:
                    act.wait_ge(act_ready, k + WAYS * r - 1)
                nc.scalar.activation(gated[b][:], up_ps[b][:, 0:INNER], ACT.Silu).then_inc(gated_ready, 1)

            def copy_act(k, r):
                b = k % 2
                act.wait_ge(at_done, k + WAYS * r + 1)
                if k >= 2:
                    act.wait_ge(down_done, k + WAYS * r - 1)
                nc.scalar.activation(act_t[b][:, 0], at_ps[b][:, 0], ACT.Copy).then_inc(at_a_ready, 1)
            pipeline(act, [copy_x, gate, copy_act])

        @block.vector
        def _(dve):
            def multiply(k, r):
                b = k % 2
                dve.wait_ge(gated_ready, k + WAYS * r + 1)
                if k >= 2:
                    dve.wait_ge(at_done, k + WAYS * r - 1)
                nc.vector.tensor_tensor(act_sb[b][:], up_ps[b][:, INNER:], gated[b][:], ALU.mult
                                        ).then_inc(act_ready, 1)

            def copy_act_b(k, r):
                b = k % 2
                dve.wait_ge(at_a_ready, k + WAYS * r + 1)
                if k >= 2:
                    dve.wait_ge(down_done, k + WAYS * r - 1)
                nc.vector.tensor_copy(act_t[b][0:INNER_B, 1], at_ps[b][0:INNER_B, 1]).then_inc(at_b_ready, 1)

            def output(k, r):
                b = k % 2
                dve.wait_ge(down_done, k + WAYS * r + 1)
                if is_sorted(k):
                    uses = (k - SHARED_FIRST) // WAYS + r
                    if k >= SHARED_FIRST + WAYS:
                        dve.wait_ge(y_stored[k % WAYS], 16 * uses)
                    nc.vector.tensor_copy(y_sb[k % WAYS][:], y_ps[b][:]).then_inc(y_ready, 1)
                else:
                    t = bass.ds(tile_of(k, r), 1)
                    nc.vector.tensor_tensor(x_sb[:, t, :], y_ps[b][:].unsqueeze(1), x_sb[:, t, :], ALU.add
                                            ).then_inc(y_ready, 1)

            def combine(t):
                dve.wait_ge(gathered[t], 16 * TOP_K)
                for n in range(TOP_K):
                    total = nc.vector.scalar_tensor_tensor(
                        x_sb[:, t, :], chosen[:, t, n, :], keep.weight[:, n, t:t + 1],
                        x_sb[:, t, :], ALU.mult, ALU.add)
                    if n == 0:
                        total.then_inc(added, 1)
                        dve.wait_ge(added, t + 1)
                total.then_inc(summed, 1)

            def combine_ready(k, r):
                t = k - EXPERT_END - COMBINE_LAG
                if isinstance(r, int) and t >= 0:
                    dve.wait_ge(y_ready, k - 1)
                    combine(t)
            pipeline(dve, [multiply, copy_act_b, output, combine_ready], straight=EXPERT_END)
            for t in range(ITEMS - EXPERT_END - COMBINE_LAG, TILES):
                combine(t)



PREFETCH_ZEROS = 8


def cross_attention_experts(nc, io):
    with ExitStack() as ctx:
        def sb(scope, name, shape, dt):
            return scope.enter_context(nc.sbuf_tensor(name, shape, dt))

        def scratch(name, shape, dt):
            return nc.dram_tensor(name, shape, dt, kind="Internal").ap()

        io.q_dram = scratch("q_dram", [3 * EMBED, CHUNKS, CHUNK], BF16)
        io.k_dram = scratch("k_dram", [3 * KV, CHUNKS, CHUNK], BF16)
        io.v_dram = scratch("v_dram", [CHUNKS * P, CHUNK_TILES * GROUPS * 32], F32)
        io.sorted_x = scratch("sorted_x", [MAX_TILES * P, EMBED], F32)
        io.sorted_y = scratch("sorted_y", [MAX_TILES * P, EMBED], F32)

        keep = Sizes()
        keep.x_sb = sb(ctx, "x_sb", [P, TILES, EMBED], F32)
        keep.ident = sb(ctx, "ident", [P, P], F32)
        keep.w_up = sb(ctx, "w_up", [P, HALVES, EXPERTS + 1, 2 * INNER], F32)
        keep.w_down = sb(ctx, "w_down", [P, EXPERTS + 1, EMBED], F32)
        keep.w_down_b = sb(ctx, "w_down_b", [INNER_B, EXPERTS + 1, EMBED], F32)
        keep.prefetched = ctx.enter_context(nc.semaphore("prefetched"))
        with ExitStack() as attention:
            keep.bias_sb = sb(attention, "bias_sb", [P, EMBED], F32)
            keep.q_op = [sb(attention, f"q_op{b}", [P, HEADS, RUN], BF16) for b in range(2)]
            keep.k_op = [sb(attention, f"k_op{b}", [P, GROUPS, 2, RUN], BF16) for b in range(2)]
            keep.v_op = [sb(attention, f"v_op{b}", [P, CHUNK_TILES, GROUPS, 32], F32) for b in range(2)]
            keep.qkv_in = [ctx.enter_context(nc.semaphore(f"qkv_in{b}")) for b in range(2)]
            zeros = sb(attention, "zeros", [P, EMBED], F32)
            keep.zeroed = [op[:].rearrange("p h n -> p (h n)") for op in keep.q_op]
            keep.zeroed += [op[:].rearrange("p g a n -> p (g a n)") for op in keep.k_op]
            keep.zeroed.append(zeros[:].bitcast(BF16))
            keep.prefetch = [(io.w_up, keep.w_up[:]), (io.w_down, keep.w_down[:]),
                             (io.w_down_b, keep.w_down_b[:])]
            for t in range(0, MAX_TILES, PREFETCH_ZEROS):
                n = min(PREFETCH_ZEROS, MAX_TILES - t)
                keep.prefetch.append((zeros[:].unsqueeze(1).to_broadcast([P, n, EMBED]),
                                      io.sorted_x[t * P:(t + n) * P, :].rearrange("(t p) f -> p t f", p=P)))
            project_phase(nc, ctx, io, keep)
            attention_phase(nc, ctx, io, keep)
        keep.xn_all = sb(ctx, "xn_all", [P, TILES, EMBED], F32)
        keep.row = sb(ctx, "row", [P, TOP_K, TILES], I32)
        keep.weight = sb(ctx, "weight", [P, TOP_K, TILES], F32)
        keep.windows = sb(ctx, "windows", [1, WINDOWS], I32)
        keep.tile_expert = sb(ctx, "tile_expert", [1, MAX_TILES], I32)
        routing_phase(nc, ctx, io, keep)
        ffn_phase(nc, ctx, io, keep)


def kernel(**inputs):
    import numpy as _np
    import concourse.bacc as _bacc
    from concourse import mybir as _mybir
    from concourse.bass_utils import run_bass_kernel_spmd as _run

    def rows_first(w, n):
        return w.T.reshape(HALVES, P, n).transpose(1, 0, 2)

    def at(name):
        return _np.asarray(inputs[name])

    pairs = (CHUNKS, CHUNK_TILES, 2, SEQ, HALVES, P)
    w1 = at("L0_ffn_w1").reshape(EXPERTS, HALVES, P, 2 * INNER).transpose(2, 1, 0, 3)
    shared_up = rows_first(_np.concatenate([at("L0_ffn_sw1"), at("L0_ffn_sw2")]), 2 * INNER)
    w_down = _np.concatenate([at("L0_ffn_w2"), at("L0_ffn_sw3").T[None]]).transpose(1, 0, 2)
    token = _np.arange(P)
    row = _np.arange(SEQ)
    select = _np.zeros((SEQ, HP, 2, SEQ), _np.uint16)
    select[row, (row % 32) // 2, row % 2] = 0x3F80
    arrays = {
        "in_x": at("x").reshape(TOKENS, EMBED),
        "in_ctx_t": at("ctx_2048").reshape(pairs).transpose(0, 5, 4, 2, 3, 1).reshape(CHUNKS * P, HALVES, CHUNK),
        "in_wq": rows_first(at("L0_xattn_Wq"), EMBED),
        "in_wkv": rows_first(_np.concatenate([at("L0_xattn_Wk"), at("L0_xattn_Wv")]), 2 * KV),
        "in_wfc": at("L0_xattn_Wfc").T.reshape(2, 4, 2, 2, HEAD_DIM, EMBED)
                  .transpose(0, 2, 1, 4, 3, 5).reshape(P, HALVES, EMBED),
        "in_bias": at("L0_xattn_bfc").reshape(EMBED),
        "in_gate": rows_first(at("L0_ffn_gate_w"), EXPERTS),
        "in_w_up": _np.concatenate([w1, shared_up[:, :, None]], axis=2),
        "in_w_down": w_down[:P],
        "in_w_down_b": w_down[P:],
        "in_ident": _np.eye(P, dtype=_np.float32),
        "in_select": select.reshape(SEQ, HP, P),
        "in_before": _np.where(token[:, None] < token[None], 0x3F80, 0).astype(_np.uint16),
        "in_expert_iota": _np.tile(_np.arange(EXPERTS, dtype=_np.float32), (P, 1)),
        "in_tile_iota": _np.arange(MAX_TILES, dtype=_np.float32)[None],
    }
    nc = _bacc.Bacc("TRN2", target_bir_lowering=False, num_devices=1)
    io = Sizes()
    access = {}
    for name in arrays:
        arrays[name] = a = _np.ascontiguousarray(arrays[name])
        access[name] = nc.dram_tensor(name, a.shape, _mybir.dt.from_np(a.dtype), kind="ExternalInput").ap()
    io.x, io.ctx_t, io.wq, io.wkv = access["in_x"], access["in_ctx_t"], access["in_wq"], access["in_wkv"]
    io.wfc, io.bias, io.gate = access["in_wfc"], access["in_bias"], access["in_gate"]
    io.w_up, io.w_down, io.w_down_b = access["in_w_up"], access["in_w_down"], access["in_w_down_b"]
    io.ident, io.select, io.before = access["in_ident"], access["in_select"].bitcast(BF16), access["in_before"].bitcast(BF16)
    io.expert_iota, io.tile_iota = access["in_expert_iota"], access["in_tile_iota"]
    io.out = nc.dram_tensor("out", (TOKENS, EMBED), F32, kind="ExternalOutput").ap()
    cross_attention_experts(nc, io)
    r = _run(nc, [arrays], core_ids=[0])
    return r.results[0]["out"].reshape(BATCH, SEQ, EMBED)
```

```python
import math
from contextlib import ExitStack

import concourse.bass as bass
from concourse import mybir

F32 = mybir.dt.float32
BF16 = mybir.dt.bfloat16
I32 = mybir.dt.int32
U32 = mybir.dt.uint32
ALU = mybir.AluOpType
ACT = mybir.ActivationFunctionType
AX = mybir.AxisListType

P = 128
BATCH, SEQ, EMBED = 64, 64, 256
TOKENS = BATCH * SEQ
TILES = TOKENS // P
HALVES = EMBED // P
HEADS, GROUPS, HEAD_DIM = 32, 8, 8
KV = GROUPS * HEAD_DIM
CHUNK_TILES = 4
CHUNK = CHUNK_TILES * P
CHUNKS = TOKENS // CHUNK
RUN = CHUNK_TILES * SEQ
SCALE = 1.0 / math.sqrt(HEAD_DIM)
EPS = 1e-5
Q_PART = (0, 0, 0, 1, 1, 2)
K_PART = (0, 1, 2, 0, 1, 0)
UNITS = 4
HP = HEADS // 2
EXPERTS, INNER, TOP_K = 8, 176, 2
INNER_B = INNER - P


def run_slots(eng, total, first, period, slot):
    turns = (total - first) // period
    while turns > 0 and first + turns * period > total - 1:
        turns -= 1
    if turns < 2:
        return 0
    for s in range(first):
        slot(s, 0)
    if turns > 0:
        with eng.Fori(0, turns) as r:
            for i in range(period):
                slot(first + i, r)
    return first + turns * period


def held(eng, value):
    return value if isinstance(value, int) else eng.to_reg(value)


class Sizes:
    pass


def load_operands(sp, io, keep, c, b):
    q_op, k_op, qkv_in = keep.q_op, keep.k_op, keep.qkv_in
    for a in range(2):
        for n in range(len(Q_PART)):
            rows = slice(64 * a + HEAD_DIM * n, 64 * a + HEAD_DIM * (n + 1))
            sp.dma_start(k_op[b][rows, :, a, :],
                         io.k_dram[K_PART[n] * KV:(K_PART[n] + 1) * KV, bass.ds(c, 1),
                                   a * RUN:(a + 1) * RUN]
                         .rearrange("(g d) c n -> d g (c n)", d=HEAD_DIM)).then_inc(qkv_in[b], 16)
            sp.dma_start(q_op[b][rows, :, :],
                         io.q_dram[Q_PART[n] * EMBED:(Q_PART[n] + 1) * EMBED, bass.ds(c, 1),
                                   a * RUN:(a + 1) * RUN]
                         .rearrange("(h d) c n -> d h (c n)", d=HEAD_DIM)).then_inc(qkv_in[b], 16)


def project_phase(nc, ctx0, io, keep):
    with ExitStack() as ctx:
        def sb(name, shape, dt):
            return ctx.enter_context(nc.sbuf_tensor(name, shape, dt))

        def psum(name, shape, dt):
            return ctx.enter_context(nc.psum_tensor(name, shape, dt))

        def sem(name):
            return ctx.enter_context(nc.semaphore(name))

        x_sb, ident, bias_sb = keep.x_sb, keep.ident, keep.bias_sb
        wq, wkv = sb("wq", [P, HALVES, EMBED], F32), sb("wkv", [P, HALVES, 2 * KV], F32)
        blank_rows = sb("blank_rows", [P, WAYS], I32)
        ctx_t = sb("ctx_t", [P, 2, HALVES, CHUNK], F32)
        stats = sb("stats", [P, 2, CHUNK_TILES, 6], F32)
        mean_var = sb("mean_var", [P, 2, CHUNK_TILES, 2], F32)
        var_eps = sb("var_eps", [P, 2, CHUNK_TILES], F32)
        rstd = sb("rstd", [P, 2, CHUNK_TILES], F32)
        minus_half = sb("minus_half", [P, CHUNK_TILES], F32)
        xn = sb("xn", [P, 2, CHUNK_TILES, EMBED], F32)
        xn_t = sb("xn_t", [P, 2, HALVES, CHUNK], F32)
        q_parts = sb("q_parts", [P, 2, 3, HALVES, CHUNK], BF16)
        q_rest = sb("q_rest", [P, HALVES, CHUNK], F32)
        k_parts = sb("k_parts", [KV, 2, 3, CHUNK], BF16)
        k_rest = sb("k_rest", [KV, CHUNK], F32)
        v_t = sb("v_t", [P, 2, CHUNK], F32)

        xt_ps = [psum(f"xt_ps{i}", [P, CHUNK], F32) for i in range(HALVES)]
        q_ps = [psum(f"q_ps{i}", [P, CHUNK], F32) for i in range(HALVES)]
        kv_ps = psum("kv_ps", [P, CHUNK], F32)
        v_ps = psum("v_ps", [P, CHUNK_TILES, KV], F32)

        weights_in = sem("weights_in")
        x_in, ctx_in = [sem(f"x_in{b}") for b in range(2)], [sem(f"ctx_in{b}") for b in range(2)]
        stats_done, stats_ready, eps_added, rstd_ready, half_set = (
            sem("stats_done"), sem("stats_ready"), sem("eps_added"), sem("rstd_ready"), sem("half_set"))
        xn_ready, xt_done, xt_ready = sem("xn_ready"), sem("xt_done"), sem("xt_ready")
        q_done, kv_done, vt_done = sem("q_done"), sem("kv_done"), sem("vt_done")
        q1_ready, q_rest_ready, q2_ready, q3_ready = (
            sem("q1_ready"), sem("q_rest_ready"), sem("q2_ready"), sem("q3_ready"))
        k1_ready, k_rest_ready, k2_ready, k3_ready = (
            sem("k1_ready"), sem("k_rest_ready"), sem("k2_ready"), sem("k3_ready"))
        v_t_ready, v_ready = sem("v_t_ready"), sem("v_ready")
        blocks_set, bias_added = sem("blocks_set"), sem("bias_added")
        zeros_set = sem("zeros_set")
        stored = [sem(f"stored{b}") for b in range(2)]
        STORED = 2 * 16

        block = ctx.enter_context(nc.Block())

        @block.sync
        def _(sp):
            def load_x(k, c, b):
                if k >= 2:
                    sp.wait_ge(stats_ready, CHUNK_TILES * (c - 1))
                sp.dma_start(x_sb[:, bass.ds(c * CHUNK_TILES, CHUNK_TILES), :],
                             io.x[bass.ds(c * CHUNK, CHUNK), :].rearrange("(i p) f -> p i f", p=P)
                             ).then_inc(x_in[b], 16)

            def load_context(k, c, b):
                if k >= 2:
                    sp.wait_ge(kv_done, c - 1)
                sp.dma_start(ctx_t[:, b], io.ctx_t[bass.ds(c * P, P)]).then_inc(ctx_in[b], 16)

            def store(c, b):
                sp.wait_ge(q3_ready, HALVES * (c + 1))
                sp.dma_start(io.q_dram[:, bass.ds(c, 1)].rearrange("(t p) c n -> p t (c n)", p=P),
                             q_parts[:, b].rearrange("p t h n -> p (t h) n")).then_inc(stored[b], 16)
                sp.wait_ge(k3_ready, c + 1)
                sp.dma_start(io.k_dram[:, bass.ds(c, 1)].rearrange("(t p) c n -> p t (c n)", p=KV),
                             k_parts[:, b]).then_inc(stored[b], 16)

            def slot(k, r):
                s = k + 2 * r
                if k == 0:
                    load_x(0, 0, 0)
                if k <= CHUNKS - 2:
                    load_x(k + 1, s + 1, (k + 1) % 2)
                if k == 0:
                    sp.dma_start(ident[:], io.ident).then_inc(weights_in, 16)
                    sp.dma_start(wq[:], io.wq).then_inc(weights_in, 16)
                if k >= 3:
                    if k == CHUNKS - 1:
                        sp.wait_ge(stored[(k - 3) % 2], STORED * ((k - 3) // 2))
                    store(s - 3, (k - 3) % 2)
                if k <= CHUNKS - 1:
                    load_context(k, s, k % 2)
                if k == 0:
                    sp.dma_start(wkv[:], io.wkv).then_inc(weights_in, 16)
                    sp.dma_start(bias_sb[:], io.bias.partition_broadcast(P)).then_inc(weights_in, 16)
                    sp.dma_start(blank_rows[:], io.blank_rows).then_inc(weights_in, 16)
                if k == CHUNKS - 1:
                    sp.wait_ge(zeros_set, 4)
                    load_operands(sp, io, keep, 0, 0)
            for s in range(run_slots(sp, CHUNKS, 3, 2, slot), CHUNKS + 3):
                slot(s, 0)
            for b in range(2):
                sp.wait_ge(stored[b], STORED * (CHUNKS // 2))

        @block.gpsimd
        def _(pool):
            nc.gpsimd.memset(minus_half[:], -0.5).then_inc(half_set, 1)
            pool.wait_ge(half_set, 1)

            def reciprocal_deviation(c):
                b = c % 2
                pool.wait_ge(stats_ready, CHUNK_TILES * (c + 1))
                if c >= 2:
                    pool.wait_ge(xn_ready, CHUNK_TILES * (c - 1))
                nc.gpsimd.tensor_scalar(var_eps[:, b], mean_var[:, b, :, 1], EPS, None, ALU.add
                                        ).then_inc(eps_added, 1)
                pool.wait_ge(eps_added, c + 1)
                nc.gpsimd.tensor_tensor(rstd[:, b], var_eps[:, b], minus_half[:], ALU.pow
                                        ).then_inc(rstd_ready, 1)

            def add_bias(c):
                pool.wait_ge(xn_ready, CHUNK_TILES * (c + 1))
                tiles = slice(c * CHUNK_TILES, (c + 1) * CHUNK_TILES)
                nc.gpsimd.tensor_tensor(x_sb[:, tiles, :], x_sb[:, tiles, :],
                                        bias_sb[:].unsqueeze(1).to_broadcast([P, CHUNK_TILES, EMBED]), ALU.add
                                        ).then_inc(bias_added, 1)
            for c in range(CHUNKS + 2):
                if c < CHUNKS:
                    reciprocal_deviation(c)
                if 1 <= c <= len(keep.zeroed):
                    nc.gpsimd.memset(keep.zeroed[c - 1].bitcast(F32), 0.0).then_inc(zeros_set, 1)
                if c == 1:
                    pool.wait_ge(weights_in, 80)
                if c >= 2:
                    add_bias(c - 2)
                if c == len(keep.zeroed):
                    pool.wait_ge(zeros_set, c)
                    pool.wait_ge(bias_added, c - 1)
                    for a in range(2):
                        if a == 1:
                            pool.wait_ge(blocks_set, len(keep.v_op))
                        rows = slice(a * SEQ, (a + 1) * SEQ)
                        for v_op in keep.v_op:
                            ones = v_op[rows, :, :, 16 * a + 8:16 * a + 16].rearrange("p i g d -> p (i g) d")
                            nc.gpsimd.memset(ones, 1.0).then_inc(blocks_set, 1)
                    pool.wait_ge(blocks_set, 2 * len(keep.v_op))
                    nc.gpsimd.tensor_copy(keep.blank[:, :, EMBED:].bitcast(I32), blank_rows[:].unsqueeze(2)
                                          ).then_inc(keep.blank_set, 1)

        @block.vector
        def _(dve):
            def moments(k, c, b, turn):
                dve.wait_ge(x_in[b], 16 * (turn + 1))
                for i in range(CHUNK_TILES):
                    nc.vector.bn_stats(stats[:, b, i, :], x_sb[:, bass.ds(c * CHUNK_TILES + i, 1), :]
                                       ).then_inc(stats_done, 1)
                for i in range(CHUNK_TILES):
                    so_far = held(dve, CHUNK_TILES * c + i + 1)
                    dve.wait_ge(half_set, 1)
                    dve.wait_ge(stats_done, so_far)
                    nc.vector.bn_aggr(mean_var[:, b, i, :], stats[:, b, i, :]).then_inc(stats_ready, 1)

            def normalise(k, c, b):
                dve.wait_ge(rstd_ready, c + 1)
                if k >= 2:
                    dve.wait_ge(xt_done, c - 1)
                for i in range(CHUNK_TILES):
                    nc.vector.tensor_scalar(xn[:, b, i, :], x_sb[:, bass.ds(c * CHUNK_TILES + i, 1), :],
                                            mean_var[:, b, i, 0:1], rstd[:, b, i:i + 1],
                                            ALU.subtract, ALU.mult).then_inc(xn_ready, 1)

            def split_middle(k, c, b):
                if k >= 1:
                    dve.wait_ge(q3_ready, HALVES * c)
                    dve.wait_ge(k3_ready, c)
                for h in range(HALVES):
                    dve.wait_ge(q1_ready, HALVES * c + h + 1)
                    nc.vector.scalar_tensor_tensor(q_rest[:, h], q_ps[h][:], SCALE, q_parts[:, b, 0, h],
                                                   ALU.mult, ALU.subtract).then_inc(q_rest_ready, 1)
                dve.wait_ge(k1_ready, c + 1)
                nc.vector.tensor_tensor(k_rest[:], kv_ps[0:KV, :], k_parts[:, b, 0], ALU.subtract
                                        ).then_inc(k_rest_ready, 1)

            def split_small(c, b):
                for h in range(HALVES):
                    dve.wait_ge(q2_ready, HALVES * c + h + 1)
                    nc.vector.tensor_tensor(q_parts[:, b, 2, h], q_rest[:, h], q_parts[:, b, 1, h],
                                            ALU.subtract).then_inc(q3_ready, 1)
                dve.wait_ge(k2_ready, c + 1)
                nc.vector.tensor_tensor(k_parts[:, b, 2], k_rest[:], k_parts[:, b, 1], ALU.subtract
                                        ).then_inc(k3_ready, 1)

            def keep_values(c):
                dve.wait_ge(vt_done, c + 1)
                nc.vector.tensor_copy(keep.v_all[:, bass.ds(c * CHUNK_TILES, CHUNK_TILES), :], v_ps[:]
                                      ).then_inc(v_ready, 1)

            def slot(k, r):
                s = k + 2 * r
                if k >= 4:
                    keep_values(s - 4)
                if 1 <= k <= CHUNKS:
                    normalise(k - 1, s - 1, (k - 1) % 2)
                if 3 <= k <= CHUNKS + 2:
                    split_middle(k - 3, s - 3, (k - 3) % 2)
                if k <= CHUNKS - 1:
                    moments(k, s, k % 2, k // 2 + r)
                if 3 <= k <= CHUNKS + 2:
                    split_small(s - 3, (k - 3) % 2)
            for s in range(run_slots(dve, CHUNKS, 6, 2, slot), CHUNKS + 4):
                slot(s, 0)

        @block.scalar
        def _(act):
            def evacuate(k, c, b):
                act.wait_ge(xt_done, c + 1)
                if k >= 2:
                    act.wait_ge(kv_done, c - 1)
                for h in range(HALVES):
                    nc.scalar.activation(
                        xn_t[:, b, h].rearrange("p (a q i) -> p a i q", a=2, i=CHUNK_TILES),
                        xt_ps[h][:].rearrange("p (i a q) -> p a i q", a=2, i=CHUNK_TILES),
                        ACT.Copy).then_inc(xt_ready, 1)

            def split_large(k, c, b, turn):
                if k >= 2:
                    act.wait_ge(stored[b], STORED * turn)
                for h in range(HALVES):
                    act.wait_ge(q_done, HALVES * c + h + 1)
                    nc.scalar.activation(q_parts[:, b, 0, h], q_ps[h][:], ACT.Copy, scale=SCALE
                                         ).then_inc(q1_ready, 1)
                act.wait_ge(kv_done, c + 1)
                nc.scalar.activation(k_parts[:, b, 0], kv_ps[0:KV, :], ACT.Copy).then_inc(k1_ready, 1)
                nc.scalar.activation(v_t[KV:P, b], kv_ps[KV:P, :], ACT.Copy).then_inc(v_t_ready, 1)

            def split_middle(c, b):
                for h in range(HALVES):
                    act.wait_ge(q_rest_ready, HALVES * c + h + 1)
                    nc.scalar.activation(q_parts[:, b, 1, h], q_rest[:, h], ACT.Copy).then_inc(q2_ready, 1)
                act.wait_ge(k_rest_ready, c + 1)
                nc.scalar.activation(k_parts[:, b, 1], k_rest[:], ACT.Copy).then_inc(k2_ready, 1)

            def slot(k, r):
                s = k + 2 * r
                if k <= CHUNKS - 1:
                    evacuate(k, s, k % 2)
                if k >= 2:
                    split_middle(s - 2, k % 2)
                if 1 <= k <= CHUNKS:
                    split_large(k - 1, s - 1, (k - 1) % 2, (k - 1) // 2 + r)
            for s in range(run_slots(act, CHUNKS, 3, 2, slot), CHUNKS + 2):
                slot(s, 0)

        @block.tensor
        def _(pe):
            pe.wait_ge(weights_in, 80)

            def transpose_x(k, c, b):
                pe.wait_ge(xn_ready, CHUNK_TILES * (c + 1))
                if k >= 1:
                    pe.wait_ge(xt_ready, HALVES * c)
                for i in range(CHUNK_TILES):
                    for h in range(HALVES):
                        last = nc.tensor.transpose(xt_ps[h][:, i * P:(i + 1) * P],
                                                   xn[:, b, i, h * P:(h + 1) * P], ident[:])
                last.then_inc(xt_done, 1)

            def project(k, c, b, turn):
                pe.wait_ge(ctx_in[b], 16 * (turn + 1))
                pe.wait_ge(xt_ready, HALVES * (c + 1))
                for m in range(HALVES):
                    if k >= 1:
                        pe.wait_ge(q_rest_ready, HALVES * c)
                    for h in range(HALVES):
                        last = nc.tensor.matmul(q_ps[m][:], wq[:, h, m * P:(m + 1) * P], xn_t[:, b, h],
                                                start=(h == 0), stop=(h == HALVES - 1))
                    last.then_inc(q_done, 1)
                if k >= 1:
                    pe.wait_ge(k_rest_ready, c)
                    pe.wait_ge(v_t_ready, c)
                for h in range(HALVES):
                    last = nc.tensor.matmul(kv_ps[:], wkv[:, h], ctx_t[:, b, h],
                                            start=(h == 0), stop=(h == HALVES - 1))
                last.then_inc(kv_done, 1)

            def transpose_v(k, c, b):
                chunks, before = held(pe, c + 1), held(pe, c)
                pe.wait_ge(weights_in, 80)
                pe.wait_ge(v_t_ready, chunks)
                if k >= 1:
                    pe.wait_ge(v_ready, before)
                for i in range(CHUNK_TILES):
                    keys = v_t[KV:P, b].rearrange("p (n i) -> p n i", i=CHUNK_TILES)[:, :, i]
                    last = nc.tensor.transpose(v_ps[:, i, :], keys, ident[KV:P, KV:P])
                last.then_inc(vt_done, 1)

            def slot(k, r):
                s = k + 2 * r
                if k <= CHUNKS - 1:
                    transpose_x(k, s, k % 2)
                if 1 <= k <= CHUNKS:
                    project(k - 1, s - 1, (k - 1) % 2, (k - 1) // 2 + r)
                if k >= 2:
                    transpose_v(k - 2, s - 2, k % 2)
            for s in range(run_slots(pe, CHUNKS, 3, 2, slot), CHUNKS + 2):
                slot(s, 0)


def attention_phase(nc, ctx0, io, keep):
    with ExitStack() as ctx:
        def sb(name, shape, dt):
            return ctx.enter_context(nc.sbuf_tensor(name, shape, dt))

        def psum(name, shape, dt):
            return ctx.enter_context(nc.psum_tensor(name, shape, dt))

        def sem(name):
            return ctx.enter_context(nc.semaphore(name))

        x_sb, ident = keep.x_sb, keep.ident
        q_op, k_op = keep.q_op, keep.k_op
        v_op, qkv_in, v_placed = keep.v_op, keep.qkv_in, sem("v_placed")
        w_out = sb("w_out", [P, 2, EMBED], F32)
        select = sb("select", [SEQ, HP, P], BF16)
        ident_b = sb("ident_b", [P, P], BF16)
        row_max = sb("row_max", [P, 2, 2 * HP], F32)
        minus_max = sb("minus_max", [P, 2, 2, 2 * HP], BF16)
        max_t = sb("max_t", [SEQ, 2, P], BF16)
        probs = sb("probs", [P, UNITS, 512], F32)
        pv_sb = sb("pv_sb", [P, 512], F32)
        recip = sb("recip", [P, 2 * HP], F32)
        heads_out = sb("heads_out", [P, 2, P], F32)
        heads_t = sb("heads_t", [P, 2, 2, SEQ], F32)

        score_ps = [psum(f"score_ps{b}", [P, 512], F32) for b in range(2)]
        shift_ps = [psum(f"shift_ps{b}", [P, 512], F32) for b in range(2)]
        pv_ps = psum("pv_ps", [P, 512], F32)
        nat_ps = psum("nat_ps", [P, 512], F32)
        misc_ps = psum("misc_ps", [P, 512], F32)
        max_ps = misc_ps[:].bitcast(BF16)[0:SEQ, 0:P]
        back_ps = misc_ps[:, 0:2 * P]
        out_ps = psum("out_ps", [P, EMBED], F32)

        consts_in, identb_ready = sem("consts_in"), sem("identb_ready")
        scores_done, max_ready, hi_ready, minus_ready = (
            sem("scores_done"), sem("max_ready"), sem("hi_ready"), sem("minus_ready"))
        max_t_done, max_t_ready = sem("max_t_done"), sem("max_t_ready")
        shifted_done, probs_ready = sem("shifted_done"), sem("probs_ready")
        pv_done, pv_ready = sem("pv_done"), sem("pv_ready")
        nat_done, recip_ready, heads_ready = sem("nat_done"), sem("recip_ready"), sem("heads_ready")
        back_done, heads_t_ready = sem("back_done"), sem("heads_t_ready")
        out_done, x_ready = sem("out_done"), sem("x_ready")
        LOADS = 2 * (2 * len(Q_PART))
        PERIOD = 2 * CHUNK_TILES

        block = ctx.enter_context(nc.Block())

        @block.sync
        def _(sp):
            sp.dma_start(select[:], io.select).then_inc(consts_in, 16)
            sp.dma_start(w_out[:], io.wfc).then_inc(consts_in, 16)

            load_operands(sp, io, keep, 1, 1)
            sp.wait_ge(keep.blank_set, 1)
            for src, dst in keep.prefetch:
                sp.dma_start(dst, src).then_inc(keep.prefetched, 16)
            with sp.Fori(1, CHUNKS // 2) as r:
                for b in range(2):
                    sp.wait_ge(pv_done, CHUNK_TILES * (2 * r + b - 1))
                    load_operands(sp, io, keep, 2 * r + b, b)
            sp.wait_ge(keep.prefetched, 16 * len(keep.prefetch))

        @block.tensor
        def _(pe):
            pe.wait_ge(consts_in, 32)
            pe.wait_ge(identb_ready, 1)

            def scores(k, p, us, kc, turn):
                b, i = kc
                if us[0] == 0:
                    pe.wait_ge(qkv_in[b], 16 * LOADS * (turn + 1))
                for u in us:
                    if UNITS * k + u >= 2:
                        pe.wait_ge(max_ready, UNITS * p + u - 1)
                    for j in range(4):
                        g, hp = 2 * u + j // 2, 4 * u + j
                        q = q_op[b][:, 2 * hp:2 * hp + 2].rearrange("p h (q i) -> p (h q) i", i=CHUNK_TILES)[:, :, i]
                        kk = k_op[b][:, g].rearrange("p a (q i) -> p (a q) i", i=CHUNK_TILES)[:, :, i]
                        last = nc.tensor.matmul(score_ps[u % 2][:, j * P:(j + 1) * P], q, kk,
                                                start=True, stop=True)
                    last.then_inc(scores_done, 1)

            def transpose_max(k, p):
                tile, before = held(pe, p + 1), held(pe, p - 1)
                pe.wait_ge(identb_ready, 1)
                pe.wait_ge(minus_ready, tile)
                if k >= 2:
                    pe.wait_ge(heads_t_ready, before)
                nc.tensor.transpose(max_ps, minus_max[:, k % 2].rearrange("p t n -> p (t n)"), ident_b[:]
                                    ).then_inc(max_t_done, 1)

            def shifted(k, p, u, kc):
                b, i = kc
                if u == 0:
                    pe.wait_ge(max_t_ready, p + 1)
                if UNITS * k + u >= 2:
                    pe.wait_ge(probs_ready, UNITS * p + u - 1)
                for g in (2 * u, 2 * u + 1):
                    out = shift_ps[u % 2][:, (g % 2) * 256:(g % 2) * 256 + 256]
                    q = q_op[b][:, 4 * g:4 * g + 4].rearrange("p h (q i) -> p (h q) i", i=CHUNK_TILES)[:, :, i]
                    kk = k_op[b][:, g].rearrange("p a (q i) -> p (a q) i", i=CHUNK_TILES)[:, :, i]
                    nc.tensor.matmul(out, kk, q, start=True, stop=False)
                    for j in range(2):
                        last = nc.tensor.matmul(out[:, j * P:(j + 1) * P], select[:, 2 * g + j, :],
                                                max_t[:, k % 2, :], start=False, stop=(j == 1))
                last.then_inc(shifted_done, 1)

            def values(k, p, u, kc, placed):
                b, i = kc
                if u == 0 and k >= 1:
                    pe.wait_ge(pv_ready, p)
                if u == 0 and i == 0:
                    pe.wait_ge(v_placed, placed)
                pe.wait_ge(probs_ready, UNITS * p + u + 1)
                for g in (2 * u, 2 * u + 1):
                    gi, half = g % 4, g // 4
                    last = nc.tensor.matmul(pv_ps[32 * gi:32 * gi + 32, 256 * half:256 * half + 256],
                                            v_op[b][:, i, g, :], probs[:, u, (g % 2) * 256:(g % 2) * 256 + 256],
                                            start=True, stop=True)
                if u == UNITS - 1:
                    last.then_inc(pv_done, 1)

            def to_tokens(k, p):
                pe.wait_ge(pv_ready, p + 1)
                if k >= 1:
                    pe.wait_ge(heads_ready, p)
                for n in range(4):
                    last = nc.tensor.transpose(nat_ps[:, n * P:(n + 1) * P], pv_sb[:, n * P:(n + 1) * P],
                                               ident[:])
                last.then_inc(nat_done, 1)

            def to_features(k, p, more):
                pe.wait_ge(heads_ready, p + 1)
                if more:
                    pe.wait_ge(max_t_ready, p + 2)
                for a in range(2):
                    last = nc.tensor.transpose(back_ps[:, a * P:(a + 1) * P], heads_out[:, a, :], ident[:])
                last.then_inc(back_done, 1)

            def project_out(k, p):
                pe.wait_ge(heads_t_ready, p + 1)
                if k >= 1:
                    pe.wait_ge(x_ready, p)
                for jj in range(2):
                    last = nc.tensor.matmul(out_ps[:], heads_t[:, jj].rearrange("p a q -> p (a q)"),
                                            w_out[:, jj], start=(jj == 0), stop=(jj == 1))
                last.then_inc(out_done, 1)

            def slot(k, r):
                s = k + PERIOD * r
                now = ((k // CHUNK_TILES) % 2, k % CHUNK_TILES)
                before = (((k - 1) // CHUNK_TILES) % 2, (k - 1) % CHUNK_TILES)
                turn = k // PERIOD + r
                placed = (k - 1) // CHUNK_TILES + 2 * r + 1
                a_on, b_on, f_on = k <= TILES - 1, 1 <= k <= TILES, 2 <= k
                if b_on:
                    transpose_max(k - 1, s - 1)
                if a_on:
                    scores(k, s, (0, 1), now, turn)
                if f_on:
                    to_tokens(k - 2, s - 2)
                if b_on:
                    shifted(k - 1, s - 1, 0, before)
                if a_on:
                    scores(k, s, (2,), now, turn)
                if b_on:
                    shifted(k - 1, s - 1, 1, before)
                if a_on:
                    scores(k, s, (3,), now, turn)
                if f_on:
                    to_features(k - 2, s - 2, b_on)
                if b_on:
                    shifted(k - 1, s - 1, 2, before)
                    values(k - 1, s - 1, 0, before, placed)
                    shifted(k - 1, s - 1, 3, before)
                    values(k - 1, s - 1, 1, before, placed)
                if f_on:
                    project_out(k - 2, s - 2)
                if b_on:
                    values(k - 1, s - 1, 2, before, placed)
                    values(k - 1, s - 1, 3, before, placed)
            for s in range(run_slots(pe, TILES, 3, PERIOD, slot), TILES + 2):
                slot(s, 0)

        @block.scalar
        def _(act):
            def exponentials(k, p, us):
                for u in us:
                    act.wait_ge(shifted_done, UNITS * p + u + 1)
                    if u == 0 and k >= 1:
                        act.wait_ge(pv_done, p)
                    nc.scalar.activation(probs[:, u], shift_ps[u % 2][:], ACT.Exp).then_inc(probs_ready, 1)

            def copy_pv(k, p):
                act.wait_ge(pv_done, p + 1)
                if k >= 1:
                    act.wait_ge(nat_done, p)
                nc.scalar.activation(pv_sb[:], pv_ps[:], ACT.Copy).then_inc(pv_ready, 1)

            def copy_heads(k, p):
                act.wait_ge(back_done, p + 1)
                if k >= 1:
                    act.wait_ge(out_done, p)
                nc.scalar.activation(heads_t[:].rearrange("p j a q -> p a j q"),
                                     back_ps.rearrange("p (a j q) -> p a j q", a=2, j=2),
                                     ACT.Copy).then_inc(heads_t_ready, 1)

            def slot(k, r):
                s = k + PERIOD * r
                b_on, f_on = 1 <= k <= TILES, 2 <= k
                if b_on:
                    exponentials(k - 1, s - 1, (0, 1))
                if f_on:
                    copy_heads(k - 2, s - 2)
                if b_on:
                    exponentials(k - 1, s - 1, (2, 3))
                    copy_pv(k - 1, s - 1)
            for s in range(run_slots(act, TILES, 3, PERIOD, slot), TILES + 2):
                slot(s, 0)

        @block.vector
        def _(dve):
            dve.wait_ge(consts_in, 32)
            nc.vector.tensor_copy(ident_b[:], ident[:]).then_inc(identb_ready, 1)

            def place_values(k, c, b, used):
                if k >= CHUNK_TILES:
                    dve.wait_ge(pv_done, used)
                tiles = bass.ds(c * CHUNK_TILES, CHUNK_TILES)
                for a in range(2):
                    rows = slice(a * SEQ, (a + 1) * SEQ)
                    last = nc.vector.tensor_copy(
                        v_op[b][rows, :, :, 16 * a:16 * a + 8],
                        keep.v_all[rows, tiles, :].rearrange("p i (g d) -> p i g d", g=GROUPS))
                last.then_inc(v_placed, 1)

            def maxima(k, p, us):
                for u in us:
                    dve.wait_ge(scores_done, UNITS * p + u + 1)
                    if u == 0 and k >= 2:
                        dve.wait_ge(minus_ready, p - 1)
                    nc.vector.reduce_max(row_max[:, k % 2, 8 * u:8 * u + 8],
                                         score_ps[u % 2][:].rearrange("p (n t) -> p n t", t=SEQ), AX.X
                                         ).then_inc(max_ready, 1)

            def negate_maxima(k, p):
                dve.wait_ge(max_ready, UNITS * (p + 1))
                if k >= 2:
                    dve.wait_ge(max_t_done, p - 1)
                nc.vector.tensor_scalar(minus_max[:, k % 2, 0], row_max[:, k % 2], -1.0, None, ALU.mult
                                        ).then_inc(hi_ready, 1)
                dve.wait_ge(hi_ready, p + 1)
                nc.vector.scalar_tensor_tensor(minus_max[:, k % 2, 1], row_max[:, k % 2], -1.0,
                                               minus_max[:, k % 2, 0], ALU.mult, ALU.subtract
                                               ).then_inc(minus_ready, 1)

            def copy_max(k, p):
                dve.wait_ge(max_t_done, p + 1)
                if k >= 2:
                    dve.wait_ge(shifted_done, UNITS * (p - 1))
                nc.vector.tensor_copy(max_t[:, k % 2], max_ps).then_inc(max_t_ready, 1)

            def normalise(k, p):
                sums = nat_ps[:].rearrange("p (n m) -> p n m", m=16)
                dve.wait_ge(nat_done, p + 1)
                if k >= 1:
                    dve.wait_ge(heads_ready, p)
                nc.vector.reciprocal(recip[:], sums[:, :, 8]).then_inc(recip_ready, 1)
                dve.wait_ge(recip_ready, p + 1)
                if k >= 1:
                    dve.wait_ge(back_done, p)
                nc.vector.tensor_tensor(
                    heads_out[:].rearrange("p a (n d) -> p n a d", d=HEAD_DIM),
                    nat_ps[:].rearrange("p (n a m) -> p n a m", a=2, m=16)[:, :, :, 0:8],
                    recip[:].rearrange("p (n a) -> p n a", a=2).unsqueeze(3).to_broadcast([P, HP, 2, HEAD_DIM]),
                    ALU.mult).then_inc(heads_ready, 1)

            def add_residual(k, p):
                dve.wait_ge(out_done, p + 1)
                nc.vector.tensor_tensor(x_sb[:, bass.ds(p, 1), :], out_ps[:].unsqueeze(1),
                                        x_sb[:, bass.ds(p, 1), :], ALU.add).then_inc(x_ready, 1)

            def slot(k, r):
                s = k + PERIOD * r
                a_on, b_on, f_on = k <= TILES - 1, 1 <= k <= TILES, 2 <= k
                if b_on:
                    copy_max(k - 1, s - 1)
                if a_on:
                    maxima(k, s, (0, 1))
                if f_on:
                    normalise(k - 2, s - 2)
                if a_on:
                    maxima(k, s, (2, 3))
                    negate_maxima(k, s)
                if f_on:
                    add_residual(k - 2, s - 2)
                if k % CHUNK_TILES == 2 and k < TILES - CHUNK_TILES:
                    c = k // CHUNK_TILES + 1
                    place_values(k, c + 2 * r, c % 2, s - 2)
            place_values(0, 0, 0, 0)
            for s in range(run_slots(dve, TILES, 3, PERIOD, slot), TILES + 2):
                slot(s, 0)


MAX_TILES = TOKENS * TOP_K // P + EXPERTS - 1
SHARED = EXPERTS
WINDOW, WINDOW_FIRST = 7, 4
WINDOWS = len(range(WINDOW_FIRST, MAX_TILES - WINDOW + 1, 4))
ROW = EMBED + 1
WAYS = 4
EARLY = 8
SHARED_FIRST = 24


def routing_phase(nc, ctx0, io, keep):
    with ExitStack() as ctx:
        def sb(name, shape, dt):
            return ctx.enter_context(nc.sbuf_tensor(name, shape, dt))

        def psum(name, shape, dt):
            return ctx.enter_context(nc.psum_tensor(name, shape, dt))

        def sem(name):
            return ctx.enter_context(nc.semaphore(name))

        x_sb, ident, xn_all = keep.x_sb, keep.ident, keep.xn_all
        NE = TILES * EXPERTS
        stats = sb("r_stats", [P, 2, CHUNK_TILES, 6], F32)
        mean_var = sb("r_mean_var", [P, 2, CHUNK_TILES, 2], F32)
        var_eps = sb("r_var_eps", [P, 2, CHUNK_TILES], F32)
        rstd = sb("r_rstd", [P, 2, CHUNK_TILES], F32)
        minus_half = sb("r_minus_half", [P, CHUNK_TILES], F32)
        xn = sb("r_xn", [P, 2, CHUNK_TILES, EMBED], F32)
        xn_t = sb("r_xn_t", [P, 2, HALVES, CHUNK], F32)
        gate = sb("r_gate", [P, HALVES, EXPERTS], F32)
        logit_t = sb("r_logit_t", [EXPERTS, CHUNK], F32)
        expert_iota = sb("r_expert_iota", [P, EXPERTS], F32)
        tile_iota = sb("r_tile_iota", [1, MAX_TILES], F32)
        before, ones = sb("r_before", [P, P], BF16), sb("r_ones", [P, P], BF16)
        logits = sb("r_logits", [P, TILES, EXPERTS], F32)
        work = sb("r_work", [P, TILES, EXPERTS], F32)
        scores = sb("r_scores", [P, TILES, EXPERTS], F32)
        hot = [sb(f"r_hot{n}", [P, TILES, EXPERTS], F32) for n in range(TOP_K)]
        mask = sb("r_mask", [P, TILES, EXPERTS], BF16)
        col = sb("r_col", [P, 8, TILES], F32)
        PAD = TILES // 2
        scan = [sb(f"r_scan{n}", [P, EXPERTS, PAD + TILES], F32) for n in range(2)]
        tiles_i = sb("r_tiles_i", [P, 2, EXPERTS], I32)
        ends = [sb(f"r_ends{n}", [P, EXPERTS // 2 + EXPERTS], F32) for n in range(2)]
        place = sb("r_place", [P, TILES, EXPERTS], F32)
        of_tile = sb("r_of_tile", [1, MAX_TILES, EXPERTS], F32)
        window_sum = sb("r_window_sum", [1, WINDOWS], F32)
        of_tile_sum = sb("r_of_tile_sum", [1, MAX_TILES], F32)

        xt_ps = [psum(f"r_xt_ps{i}", [P, CHUNK], F32) for i in range(HALVES)]
        gate_ps = psum("r_gate_ps", [EXPERTS, CHUNK], F32)
        logit_ps = psum("r_logit_ps", [P, CHUNK_TILES, EXPERTS], F32)
        rank_ps = psum("r_rank_ps", [P, TILES, EXPERTS], F32)
        count_ps = psum("r_count_ps", [P, TILES, EXPERTS], F32)

        consts_in, half_set, experts_in = sem("r_consts_in"), sem("r_half_set"), sem("r_experts_in")
        stats_done, stats_ready, eps_added, rstd_ready = (
            sem("r_stats_done"), sem("r_stats_ready"), sem("r_eps_added"), sem("r_rstd_ready"))
        xn_ready, kept, xt_done, xt_ready = (
            sem("r_xn_ready"), sem("r_kept"), sem("r_xt_done"), sem("r_xt_ready"))
        gate_done, gate_ready, logit_done, logit_ready = (
            sem("r_gate_done"), sem("r_gate_ready"), sem("r_logit_done"), sem("r_logit_ready"))
        row_ready = sem("r_row_ready")
        step, exp_done, mask_ready, ranked = sem("r_step"), sem("r_exp_done"), sem("r_mask_ready"), sem("r_ranked")

        block = ctx.enter_context(nc.Block())

        @block.sync
        def _(sp):
            for dst, src in ((gate, io.gate), (expert_iota, io.expert_iota), (tile_iota, io.tile_iota),
                             (before, io.before), (keep.token_rows, io.token_rows)):
                sp.dma_start(dst[:], src).then_inc(consts_in, 16)
            for dst, src in ((keep.w_up, io.w_up), (keep.w_down, io.w_down), (keep.w_down_b, io.w_down_b)):
                sp.dma_start(dst[:], src).then_inc(experts_in, 16)
            sp.wait_ge(consts_in, 80)
            sp.wait_ge(experts_in, 48)

        @block.gpsimd
        def _(pool):
            nc.gpsimd.memset(minus_half[:], -0.5).then_inc(half_set, 1)
            nc.gpsimd.memset(ones[:], 1.0).then_inc(half_set, 1)
            for n in range(2):
                nc.gpsimd.memset(scan[n][:], 0.0).then_inc(half_set, 1)
                nc.gpsimd.memset(ends[n][:], 0.0).then_inc(half_set, 1)
            pool.wait_ge(half_set, 1)

            def reciprocal_deviation(k, r):
                c, b = k + 2 * r, k % 2
                tiles, before = held(pool, CHUNK_TILES * (c + 1)), held(pool, CHUNK_TILES * (c - 1))
                pool.wait_ge(half_set, 1)
                pool.wait_ge(stats_ready, tiles)
                if k >= 2:
                    pool.wait_ge(xn_ready, before)
                nc.gpsimd.tensor_scalar(var_eps[:, b], mean_var[:, b, :, 1], EPS, None, ALU.add
                                        ).then_inc(eps_added, 1)
                pool.wait_ge(eps_added, c + 1)
                nc.gpsimd.tensor_tensor(rstd[:, b], var_eps[:, b], minus_half[:], ALU.pow
                                        ).then_inc(rstd_ready, 1)
            for s in range(run_slots(pool, CHUNKS, 2, 2, reciprocal_deviation), CHUNKS):
                reciprocal_deviation(s, 0)
            pool.wait_ge(consts_in, 80)
            nc.gpsimd.tensor_copy(xn_all[:, :, EMBED:].bitcast(I32), keep.token_rows[:, 0, :].unsqueeze(2)
                                  ).then_inc(keep.rows_set, 1)
            pool.wait_ge(keep.rows_set, 1)
            pool.wait_ge(kept, CHUNKS)
            pool.wait_ge(row_ready, 1)
            for t in range(EARLY):
                nc.gpsimd.indirect_dma_start(
                    io.sorted_x, bass.IndirectOffsetOnAxis(ap=keep.row[:, 0, t:t + 1], axis=0),
                    xn_all[:, t, :], None).then_inc(keep.sorted_in, 16)

        @block.scalar
        def _(act):
            def evacuate(k, c, b):
                act.wait_ge(xt_done, c + 1)
                if k >= 2:
                    act.wait_ge(gate_done, c - 1)
                for h in range(HALVES):
                    nc.scalar.activation(xn_t[:, b, h], xt_ps[h][:], ACT.Copy).then_inc(xt_ready, 1)

            def keep_normalised(c, b):
                act.wait_ge(xn_ready, CHUNK_TILES * (c + 1))
                nc.scalar.activation(xn_all[:, bass.ds(c * CHUNK_TILES, CHUNK_TILES), 0:EMBED], xn[:, b], ACT.Copy
                                     ).then_inc(kept, 1)

            def copy_gate(k, c):
                act.wait_ge(gate_done, c + 1)
                if k >= 1:
                    act.wait_ge(logit_done, c)
                nc.scalar.activation(logit_t[:], gate_ps[:], ACT.Copy).then_inc(gate_ready, 1)

            def slot(k, r):
                s = k + 2 * r
                if k <= CHUNKS - 1:
                    evacuate(k, s, k % 2)
                if k >= 1:
                    copy_gate(k - 1, s - 1)
                if k <= CHUNKS - 1:
                    keep_normalised(s, k % 2)
            for s in range(run_slots(act, CHUNKS, 2, 2, slot), CHUNKS + 1):
                slot(s, 0)
            act.wait_ge(exp_done, 1)
            nc.scalar.activation(scores[:], work[:], ACT.Exp).then_inc(exp_done, 1)

        @block.tensor
        def _(pe):
            pe.wait_ge(consts_in, 80)

            def transpose_x(k, c, b):
                pe.wait_ge(xn_ready, CHUNK_TILES * (c + 1))
                if k >= 1:
                    pe.wait_ge(xt_ready, HALVES * c)
                for i in range(CHUNK_TILES):
                    for h in range(HALVES):
                        last = nc.tensor.transpose(xt_ps[h][:, i * P:(i + 1) * P],
                                                   xn[:, b, i, h * P:(h + 1) * P], ident[:])
                last.then_inc(xt_done, 1)

            def gate_scores(k, c, b):
                pe.wait_ge(xt_ready, HALVES * (c + 1))
                if k >= 1:
                    pe.wait_ge(gate_ready, c)
                for h in range(HALVES):
                    last = nc.tensor.matmul(gate_ps[:], gate[:, h], xn_t[:, b, h],
                                            start=(h == 0), stop=(h == HALVES - 1))
                last.then_inc(gate_done, 1)

            def transpose_logits(k, c):
                chunks, before = held(pe, c + 1), held(pe, c)
                pe.wait_ge(consts_in, 80)
                pe.wait_ge(gate_ready, chunks)
                if k >= 1:
                    pe.wait_ge(logit_ready, before)
                for i in range(CHUNK_TILES):
                    last = nc.tensor.transpose(logit_ps[:, i, :], logit_t[:, i * P:(i + 1) * P],
                                               ident[0:EXPERTS, 0:EXPERTS])
                last.then_inc(logit_done, 1)

            def slot(k, r):
                s = k + 2 * r
                if k <= CHUNKS - 1:
                    transpose_x(k, s, k % 2)
                if 1 <= k <= CHUNKS:
                    gate_scores(k - 1, s - 1, (k - 1) % 2)
                if k >= 2:
                    transpose_logits(k - 2, s - 2)
            for s in range(run_slots(pe, CHUNKS, 3, 2, slot), CHUNKS + 2):
                slot(s, 0)
            pe.wait_ge(half_set, 6)
            pe.wait_ge(mask_ready, 1)
            chosen = mask[:].rearrange("p t e -> p (t e)")
            nc.tensor.matmul(rank_ps[:].rearrange("p t e -> p (t e)"), before[:], chosen, start=True, stop=True)
            nc.tensor.matmul(count_ps[:].rearrange("p t e -> p (t e)"), ones[:], chosen, start=True, stop=True
                             ).then_inc(ranked, 1)

        @block.vector
        def _(dve):
            def moments(k, c, b):
                for i in range(CHUNK_TILES):
                    nc.vector.bn_stats(stats[:, b, i, :], x_sb[:, bass.ds(c * CHUNK_TILES + i, 1), :]
                                       ).then_inc(stats_done, 1)
                for i in range(CHUNK_TILES):
                    so_far = held(dve, CHUNK_TILES * c + i + 1)
                    dve.wait_ge(half_set, 1)
                    dve.wait_ge(stats_done, so_far)
                    nc.vector.bn_aggr(mean_var[:, b, i, :], stats[:, b, i, :]).then_inc(stats_ready, 1)

            def normalise(k, c, b):
                dve.wait_ge(rstd_ready, c + 1)
                if k >= 2:
                    dve.wait_ge(xt_done, c - 1)
                    dve.wait_ge(kept, c - 1)
                for i in range(CHUNK_TILES):
                    nc.vector.tensor_scalar(xn[:, b, i, :], x_sb[:, bass.ds(c * CHUNK_TILES + i, 1), :],
                                            mean_var[:, b, i, 0:1], rstd[:, b, i:i + 1],
                                            ALU.subtract, ALU.mult).then_inc(xn_ready, 1)

            def copy_logits(c):
                dve.wait_ge(logit_done, c + 1)
                nc.vector.tensor_copy(logits[:, bass.ds(c * CHUNK_TILES, CHUNK_TILES), :], logit_ps[:]
                                      ).then_inc(logit_ready, 1)

            def slot(k, r):
                s = k + 2 * r
                if 2 <= k <= CHUNKS + 1:
                    normalise(k - 2, s - 2, k % 2)
                if k <= CHUNKS - 1:
                    moments(k, s, k % 2)
                if k >= 5:
                    copy_logits(s - 5)
            for s in range(run_slots(dve, CHUNKS, 4, 2, slot), CHUNKS + 5):
                slot(s, 0)

            done = [0]

            def then(instruction):
                instruction.then_inc(step, 1)
                done[0] += 1
                dve.wait_ge(step, done[0])

            def by_tile(c):
                return c.unsqueeze(2).to_broadcast([P, TILES, EXPERTS])

            iota = expert_iota[:].unsqueeze(1).to_broadcast([P, TILES, EXPERTS])
            dve.wait_ge(half_set, 6)
            dve.wait_ge(consts_in, 80)
            dve.wait_ge(logit_ready, CHUNKS)
            then(nc.vector.reduce_max(col[:, 0], logits[:], AX.X))
            nc.vector.tensor_tensor(work[:], logits[:], by_tile(col[:, 0]), ALU.subtract).then_inc(exp_done, 1)
            dve.wait_ge(exp_done, 2)
            then(nc.vector.reduce_sum(col[:, 1], scores[:], AX.X))
            then(nc.vector.reciprocal(col[:, 2], col[:, 1]))
            then(nc.vector.tensor_tensor(scores[:], scores[:], by_tile(col[:, 2]), ALU.mult))
            for n in range(TOP_K):
                best = col[:, 3 + n]
                then(nc.vector.reduce_max(best, scores[:], AX.X))
                then(nc.vector.tensor_tensor(work[:], scores[:], by_tile(best), ALU.is_equal))
                then(nc.vector.scalar_tensor_tensor(work[:], work[:], -float(EXPERTS), iota, ALU.mult, ALU.add))
                then(nc.vector.tensor_reduce(col[:, 5], work[:], AX.X, ALU.min))
                then(nc.vector.tensor_scalar(col[:, 5], col[:, 5], float(EXPERTS), None, ALU.add))
                then(nc.vector.tensor_tensor(hot[n][:], iota, by_tile(col[:, 5]), ALU.is_equal))
                if n == 0:
                    then(nc.vector.scalar_tensor_tensor(scores[:], hot[0][:], -2.0, scores[:], ALU.mult, ALU.add))
            nc.vector.tensor_tensor(mask[:], hot[0][:], hot[1][:], ALU.add).then_inc(mask_ready, 1)
            dve.wait_ge(ranked, 1)
            then(nc.vector.tensor_copy(scan[0][:, :, PAD:], count_ps[:].rearrange("p t e -> p e t")))
            side, far = 0, 1
            while far < TILES:
                then(nc.vector.tensor_tensor(scan[1 - side][:, :, PAD:], scan[side][:, :, PAD:],
                                             scan[side][:, :, PAD - far:PAD + TILES - far], ALU.add))
                side, far = 1 - side, 2 * far
            upto = scan[side]
            then(nc.vector.tensor_scalar(tiles_i[:, 0], upto[:, :, PAD + TILES - 1], float(P - 1), None, ALU.add))
            then(nc.vector.tensor_scalar(tiles_i[:, 1], tiles_i[:, 0], 7, None, ALU.logical_shift_right))
            LEFT = EXPERTS // 2
            then(nc.vector.tensor_copy(ends[0][:, LEFT:], tiles_i[:, 1]))
            e_side, far = 0, 1
            while far < EXPERTS:
                then(nc.vector.tensor_tensor(ends[1 - e_side][:, LEFT:], ends[e_side][:, LEFT:],
                                             ends[e_side][:, LEFT - far:LEFT + EXPERTS - far], ALU.add))
                e_side, far = 1 - e_side, 2 * far
            end = ends[e_side]
            first_tile = end[:, LEFT - 1:LEFT + EXPERTS - 1].unsqueeze(1).to_broadcast([P, TILES, EXPERTS])
            then(nc.vector.tensor_tensor(place[:], rank_ps[:],
                                         upto[:, :, PAD - 1:PAD + TILES - 1].rearrange("p e t -> p t e"), ALU.add))
            then(nc.vector.scalar_tensor_tensor(place[:], first_tile, float(P), place[:], ALU.mult, ALU.add))
            for n in range(TOP_K):
                then(nc.vector.tensor_tensor(work[:], hot[n][:], place[:], ALU.mult))
                then(nc.vector.reduce_sum(col[:, 5], work[:], AX.X))
                nc.vector.tensor_copy(keep.row[:, n], col[:, 5]).then_inc(row_ready, 1)
                dve.wait_ge(row_ready, n + 1)
            then(nc.vector.tensor_tensor(col[:, 6], col[:, 3], col[:, 4], ALU.add))
            then(nc.vector.tensor_scalar(col[:, 6], col[:, 6], 1e-20, None, ALU.add))
            then(nc.vector.reciprocal(col[:, 7], col[:, 6]))
            for n in range(TOP_K):
                then(nc.vector.tensor_tensor(keep.weight[:, n], col[:, 3 + n], col[:, 7], ALU.mult))
            then(nc.vector.tensor_tensor(
                of_tile[:], end[0:1, LEFT:].unsqueeze(1).to_broadcast([1, MAX_TILES, EXPERTS]),
                tile_iota[:].unsqueeze(2).to_broadcast([1, MAX_TILES, EXPERTS]), ALU.is_le))
            then(nc.vector.reduce_sum(of_tile_sum[:], of_tile[:], AX.X))
            then(nc.vector.tensor_scalar(of_tile_sum[:], of_tile_sum[:], float(EXPERTS - 1), None, ALU.min))
            then(nc.vector.tensor_copy(keep.tile_expert[:], of_tile_sum[:]))
            then(nc.vector.tensor_copy(window_sum[:], of_tile_sum[:, WINDOW_FIRST:MAX_TILES - WINDOW + 1:4]))
            for n in range(1, WINDOW):
                then(nc.vector.scalar_tensor_tensor(
                    window_sum[:], of_tile_sum[:, WINDOW_FIRST + n:MAX_TILES - WINDOW + 1 + n:4],
                    float(EXPERTS ** n), window_sum[:], ALU.mult, ALU.add))
            then(nc.vector.tensor_copy(keep.windows[:], window_sum[:]))


def ffn_phase(nc, ctx0, io, keep):
    with ExitStack() as ctx:
        def sb(name, shape, dt):
            return ctx.enter_context(nc.sbuf_tensor(name, shape, dt))

        def psum(name, shape, dt):
            return ctx.enter_context(nc.psum_tensor(name, shape, dt))

        def sem(name):
            return ctx.enter_context(nc.semaphore(name))

        x_sb, ident, xn_all = keep.x_sb, keep.ident, keep.xn_all
        w_up, w_down, w_down_b = keep.w_up, keep.w_down, keep.w_down_b
        x_in = [sb(f"f_x_in{way}", [P, ROW], F32) for way in range(WAYS)]
        x_t = [sb(f"f_x_t{b}", [P, HALVES, P], F32) for b in range(2)]
        gated = [sb(f"f_gated{b}", [P, INNER], F32) for b in range(2)]
        act_sb = [sb(f"f_act{b}", [P, INNER], F32) for b in range(2)]
        act_t = [sb(f"f_act_t{b}", [P, 2, P], F32) for b in range(2)]
        y_sb = [sb(f"f_y{way}", [P, EMBED], F32) for way in range(WAYS)]
        y_rows = [sb(f"f_y_rows{way}", [P, 1], I32) for way in range(WAYS)]
        chosen = sb("f_chosen", [P, TILES, TOP_K, EMBED], F32)

        xt_ps = [psum(f"f_xt_ps{b}", [P, HALVES, P], F32) for b in range(2)]
        up_ps = [psum(f"f_up_ps{b}", [P, 2 * INNER], F32) for b in range(2)]
        at_ps = [psum(f"f_at_ps{b}", [P, 2, P], F32) for b in range(2)]
        y_ps = [psum(f"f_y_ps{b}", [P, EMBED], F32) for b in range(2)]

        x_loaded = [sem(f"f_x_loaded{way}") for way in range(WAYS)]
        sorted_in, y_stored = keep.sorted_in, [sem(f"f_y_stored{way}") for way in range(WAYS)]
        xt_done, xt_ready = sem("f_xt_done"), sem("f_xt_ready")
        up_done, gated_ready, act_ready = sem("f_up_done"), sem("f_gated_ready"), sem("f_act_ready")
        at_done, at_a_ready, at_b_ready = sem("f_at_done"), sem("f_at_a_ready"), sem("f_at_b_ready")
        down_done, y_ready = sem("f_down_done"), sem("f_y_ready")
        GROUP = 4
        returned = [sem(f"f_returned{g}") for g in range(TILES // GROUP)]
        rows_set = keep.rows_set
        summed, added, out_stored = sem("f_summed"), sem("f_added"), sem("f_out_stored")

        ITEMS = TILES + MAX_TILES
        COMBINE_LAG = 4
        EXPERT_END = SHARED_FIRST + MAX_TILES

        def tile_of(k, r):
            return (k if k < SHARED_FIRST else k - MAX_TILES) + WAYS * r

        def is_sorted(k):
            return SHARED_FIRST <= k < EXPERT_END

        def pipeline(eng, stages, ahead=None, straight=None):
            lag = len(stages) - 1

            def slot(k, r, slots=1):
                if ahead is not None and slots > 0:
                    ahead(k, r, slots)
                for j in range(lag, -1, -1):
                    if stages[j] is not None and 0 <= k - j < ITEMS:
                        stages[j](k - j, r)

            s = 0
            for start, end in ((0, SHARED_FIRST), (SHARED_FIRST, EXPERT_END), (EXPERT_END, ITEMS)):
                while s < min(end, start + lag + WAYS):
                    slot(s, 0)
                    s += 1
                turns = (end - s) // WAYS
                if turns > 1 and start != straight:
                    with eng.Fori(0, turns) as r:
                        for i in range(WAYS):
                            slot(s + i, r, WAYS if i == 0 else 0)
                    s += WAYS * turns
                while s < end:
                    slot(s, 0)
                    s += 1
            for s in range(ITEMS, ITEMS + lag):
                slot(s, 0)

        block = ctx.enter_context(nc.Block())

        @block.sync
        def _(sp):
            def load(k, r):
                way = k % WAYS
                if k >= WAYS:
                    if is_sorted(k - WAYS):
                        sp.wait_ge(at_b_ready, k + WAYS * r - WAYS + 1)
                    else:
                        sp.wait_ge(xt_done, k + WAYS * r - WAYS + 1)
                if is_sorted(k):
                    if k == SHARED_FIRST:
                        sp.wait_ge(sorted_in, 16 * TOP_K * TILES)
                    sp.dma_start(x_in[way][:], io.sorted_x[bass.ds((k - SHARED_FIRST + WAYS * r) * P, P), :]
                                 ).then_inc(x_loaded[way], 16)
                else:
                    sp.dma_start(x_in[way][:, 0:EMBED].unsqueeze(1), xn_all[:, bass.ds(tile_of(k, r), 1), 0:EMBED]
                                 ).then_inc(x_loaded[way], 16)
            pipeline(sp, [load])
            for t in range(0, TILES, 2):
                sp.wait_ge(summed, t + 2)
                sp.dma_start(io.out[t * P:(t + 2) * P, :].rearrange("(t p) f -> p t f", p=P),
                             x_sb[:, t:t + 2, :]).then_inc(out_stored, 16)
            sp.wait_ge(out_stored, 16 * TILES // 2)

        @block.gpsimd
        def _(pool):
            for n in range(TOP_K):
                if n > 0:
                    pool.wait_ge(sorted_in, 16 * n * TILES)
                    nc.gpsimd.tensor_copy(xn_all[:, :, EMBED:].bitcast(I32),
                                          keep.token_rows[:, n, :].unsqueeze(2)).then_inc(rows_set, 1)
                    pool.wait_ge(rows_set, n + 1)
                for t in range(EARLY if n == 0 else 0, TILES):
                    nc.gpsimd.indirect_dma_start(
                        io.sorted_x, bass.IndirectOffsetOnAxis(ap=keep.row[:, n, t:t + 1], axis=0),
                        xn_all[:, t, :], None).then_inc(sorted_in, 16)

            def scatter(k, r):
                if is_sorted(k):
                    items = held(pool, k + WAYS * r + 1)
                    pool.wait_ge(rows_set, TOP_K)
                    pool.wait_ge(y_ready, items)
                    nc.gpsimd.indirect_dma_start(
                        io.token_y, bass.IndirectOffsetOnAxis(ap=y_rows[k % WAYS][:], axis=0),
                        y_sb[k % WAYS][:], None).then_inc(y_stored[k % WAYS], 16)
            pipeline(pool, [scatter])
            for way in range(WAYS):
                pool.wait_ge(y_stored[way], 16 * len(range(way, MAX_TILES, WAYS)))
            for g in range(TILES // GROUP):
                tiles = slice(g * GROUP, (g + 1) * GROUP)
                pool.dma_start(chosen[:, tiles].rearrange("p t n f -> p t (n f)"),
                               io.token_y[0:TOP_K * TOKENS, :].rearrange("(t p n) f -> p t (n f)", p=P, n=TOP_K)
                               [:, tiles, :]).then_inc(returned[g], 16)

        @block.tensor
        def _(pe):
            def transpose_x(k, r):
                b, way = k % 2, k % WAYS
                pe.wait_ge(x_loaded[way], 16 * (k // WAYS + 1 + r))
                if k >= 2:
                    pe.wait_ge(xt_ready, k + WAYS * r - 1)
                for h in range(HALVES):
                    last = nc.tensor.transpose(xt_ps[b][:, h], x_in[way][:, h * P:(h + 1) * P], ident[:])
                last.then_inc(xt_done, 1)

            experts = {}

            def find_experts(k, r, slots):
                window = None if slots == 1 else pe.value_load(
                    keep.windows[0:1, bass.ds(r, 1)], min_val=0, max_val=EXPERTS ** WINDOW - 1)
                for n, item in enumerate(range(k - 3, k + slots - 1)):
                    if not is_sorted(item):
                        experts[item] = slice(SHARED, SHARED + 1)
                    elif window is not None:
                        experts[item] = bass.ds(pe.snap((window >> (3 * n)) & (EXPERTS - 1),
                                                        min_val=0, max_val=EXPERTS - 1), 1)
                    elif slots == 1 and r == 0 and item not in fresh:
                        fresh.add(item)
                        experts[item] = bass.ds(pe.value_load(
                            keep.tile_expert[0:1, item - SHARED_FIRST:item - SHARED_FIRST + 1],
                            min_val=0, max_val=EXPERTS - 1), 1)
            fresh = set()

            def up(k, r):
                b, e = k % 2, experts[k]
                pe.wait_ge(xt_ready, k + WAYS * r + 1)
                if k >= 2:
                    pe.wait_ge(act_ready, k + WAYS * r - 1)
                for h in range(HALVES):
                    last = nc.tensor.matmul(up_ps[b][:], x_t[b][:, h], w_up[:, h, e, :],
                                            start=(h == 0), stop=(h == HALVES - 1))
                last.then_inc(up_done, 1)

            def transpose_act(k, r):
                b = k % 2
                pe.wait_ge(act_ready, k + WAYS * r + 1)
                if k >= 2:
                    pe.wait_ge(at_a_ready, k + WAYS * r - 1)
                    pe.wait_ge(at_b_ready, k + WAYS * r - 1)
                nc.tensor.transpose(at_ps[b][:, 0], act_sb[b][:, 0:P], ident[:])
                nc.tensor.transpose(at_ps[b][0:INNER_B, 1], act_sb[b][:, P:INNER], ident[:]).then_inc(at_done, 1)

            def down(k, r):
                b, e = k % 2, experts[k]
                pe.wait_ge(at_a_ready, k + WAYS * r + 1)
                pe.wait_ge(at_b_ready, k + WAYS * r + 1)
                if k >= 2:
                    pe.wait_ge(y_ready, k + WAYS * r - 1)
                nc.tensor.matmul(y_ps[b][:], act_t[b][:, 0], w_down[:, e, :], start=True, stop=False)
                nc.tensor.matmul(y_ps[b][:], act_t[b][0:INNER_B, 1], w_down_b[:, e, :], start=False, stop=True
                                 ).then_inc(down_done, 1)
            pipeline(pe, [transpose_x, up, transpose_act, down], find_experts)

        @block.scalar
        def _(act):
            def copy_x(k, r):
                b = k % 2
                act.wait_ge(xt_done, k + WAYS * r + 1)
                if k >= 2:
                    act.wait_ge(up_done, k + WAYS * r - 1)
                nc.scalar.activation(x_t[b][:], xt_ps[b][:], ACT.Copy).then_inc(xt_ready, 1)

            def gate(k, r):
                b = k % 2
                act.wait_ge(up_done, k + WAYS * r + 1)
                if k >= 2:
                    act.wait_ge(act_ready, k + WAYS * r - 1)
                nc.scalar.activation(gated[b][:], up_ps[b][:, 0:INNER], ACT.Silu).then_inc(gated_ready, 1)

            def copy_act(k, r):
                b = k % 2
                act.wait_ge(at_done, k + WAYS * r + 1)
                if k >= 2:
                    act.wait_ge(down_done, k + WAYS * r - 1)
                nc.scalar.activation(act_t[b][:, 0], at_ps[b][:, 0], ACT.Copy).then_inc(at_a_ready, 1)
            pipeline(act, [copy_x, gate, copy_act])

        @block.vector
        def _(dve):
            def multiply(k, r):
                b = k % 2
                dve.wait_ge(gated_ready, k + WAYS * r + 1)
                if k >= 2:
                    dve.wait_ge(at_done, k + WAYS * r - 1)
                nc.vector.tensor_tensor(act_sb[b][:], up_ps[b][:, INNER:], gated[b][:], ALU.mult
                                        ).then_inc(act_ready, 1)

            def copy_act_b(k, r):
                b = k % 2
                dve.wait_ge(at_a_ready, k + WAYS * r + 1)
                if k >= 2:
                    dve.wait_ge(down_done, k + WAYS * r - 1)
                if is_sorted(k):
                    if k >= SHARED_FIRST + WAYS:
                        uses = (k - SHARED_FIRST) // WAYS + r
                        dve.wait_ge(y_stored[k % WAYS], 16 * uses)
                    nc.vector.tensor_copy(y_rows[k % WAYS][:], x_in[k % WAYS][:, EMBED:].bitcast(I32))
                nc.vector.tensor_copy(act_t[b][0:INNER_B, 1], at_ps[b][0:INNER_B, 1]).then_inc(at_b_ready, 1)

            def output(k, r):
                b = k % 2
                dve.wait_ge(down_done, k + WAYS * r + 1)
                if is_sorted(k):
                    nc.vector.tensor_copy(y_sb[k % WAYS][:], y_ps[b][:]).then_inc(y_ready, 1)
                else:
                    t = bass.ds(tile_of(k, r), 1)
                    nc.vector.tensor_tensor(x_sb[:, t, :], y_ps[b][:].unsqueeze(1), x_sb[:, t, :], ALU.add
                                            ).then_inc(y_ready, 1)

            def combine(first, count):
                tiles = range(first, first + count)
                dve.wait_ge(returned[first // GROUP], 16)
                for n in range(TOP_K):
                    for t in tiles:
                        if n > 0:
                            dve.wait_ge(added, t + 1)
                        total = nc.vector.scalar_tensor_tensor(
                            x_sb[:, t, :], chosen[:, t, n, :], keep.weight[:, n, t:t + 1],
                            x_sb[:, t, :], ALU.mult, ALU.add)
                        total.then_inc(added if n == 0 else summed, 1)

            def combine_ready(k, r):
                first = (k - EXPERT_END - COMBINE_LAG) * (GROUP // 2)
                if isinstance(r, int) and first >= 0:
                    dve.wait_ge(y_ready, k - 1)
                    combine(first, GROUP // 2)
            pipeline(dve, [multiply, copy_act_b, output, combine_ready], straight=EXPERT_END)
            dve.wait_ge(y_ready, ITEMS)
            left = max(0, ITEMS - EXPERT_END - COMBINE_LAG) * (GROUP // 2)
            while left < TILES:
                count = GROUP - left % GROUP
                combine(left, count)
                left += count



def cross_attention_experts(nc, io):
    with ExitStack() as ctx:
        def sb(scope, name, shape, dt):
            return scope.enter_context(nc.sbuf_tensor(name, shape, dt))

        def scratch(name, shape, dt):
            return nc.dram_tensor(name, shape, dt, kind="Internal").ap()

        io.q_dram = scratch("q_dram", [3 * EMBED, CHUNKS, CHUNK], BF16)
        io.k_dram = scratch("k_dram", [3 * KV, CHUNKS, CHUNK], BF16)
        io.sorted_x = scratch("sorted_x", [MAX_TILES * P, ROW], F32)
        io.token_y = scratch("token_y", [TOP_K * TOKENS + WAYS * P, EMBED], F32)

        keep = Sizes()
        keep.x_sb = sb(ctx, "x_sb", [P, TILES, EMBED], F32)
        keep.ident = sb(ctx, "ident", [P, P], F32)
        keep.prefetched = ctx.enter_context(nc.semaphore("prefetched"))
        with ExitStack() as attention:
            keep.bias_sb = sb(attention, "bias_sb", [P, EMBED], F32)
            keep.q_op = [sb(attention, f"q_op{b}", [P, HEADS, RUN], BF16) for b in range(2)]
            keep.k_op = [sb(attention, f"k_op{b}", [P, GROUPS, 2, RUN], BF16) for b in range(2)]
            keep.v_op = [sb(attention, f"v_op{b}", [P, CHUNK_TILES, GROUPS, 32], F32) for b in range(2)]
            keep.v_all = sb(attention, "v_all", [P, TILES, KV], F32)
            keep.qkv_in = [ctx.enter_context(nc.semaphore(f"qkv_in{b}")) for b in range(2)]
            keep.blank = sb(attention, "blank", [P, WAYS, ROW], F32)
            keep.blank_set = ctx.enter_context(nc.semaphore("blank_set"))
            keep.zeroed = [op[:].rearrange("p h n -> p (h n)") for op in keep.q_op]
            keep.zeroed += [op[:].rearrange("p g a n -> p (g a n)") for op in keep.k_op]
            keep.zeroed += [op[:].rearrange("p i g m -> p (i g m)").bitcast(BF16) for op in keep.v_op]
            keep.zeroed.append(keep.blank[:].rearrange("p w f -> p (w f)").bitcast(BF16))
            keep.prefetch = []
            for t in range(0, MAX_TILES, WAYS):
                n = min(WAYS, MAX_TILES - t)
                keep.prefetch.append((keep.blank[:, 0:n, :],
                                      io.sorted_x[t * P:(t + n) * P, :].rearrange("(t p) f -> p t f", p=P)))
            project_phase(nc, ctx, io, keep)
            attention_phase(nc, ctx, io, keep)
        keep.w_up = sb(ctx, "w_up", [P, HALVES, EXPERTS + 1, 2 * INNER], F32)
        keep.w_down = sb(ctx, "w_down", [P, EXPERTS + 1, EMBED], F32)
        keep.w_down_b = sb(ctx, "w_down_b", [INNER_B, EXPERTS + 1, EMBED], F32)
        keep.xn_all = sb(ctx, "xn_all", [P, TILES, ROW], F32)
        keep.token_rows = sb(ctx, "token_rows", [P, TOP_K, TILES], I32)
        keep.row = sb(ctx, "row", [P, TOP_K, TILES], I32)
        keep.weight = sb(ctx, "weight", [P, TOP_K, TILES], F32)
        keep.windows = sb(ctx, "windows", [1, WINDOWS], I32)
        keep.tile_expert = sb(ctx, "tile_expert", [1, MAX_TILES], I32)
        keep.rows_set = ctx.enter_context(nc.semaphore("rows_set"))
        keep.sorted_in = ctx.enter_context(nc.semaphore("sorted_in"))
        routing_phase(nc, ctx, io, keep)
        ffn_phase(nc, ctx, io, keep)


def kernel(**inputs):
    import numpy as _np
    import concourse.bacc as _bacc
    from concourse import mybir as _mybir
    from concourse.bass_utils import run_bass_kernel_spmd as _run

    def rows_first(w, n):
        return w.T.reshape(HALVES, P, n).transpose(1, 0, 2)

    def at(name):
        return _np.asarray(inputs[name])

    pairs = (CHUNKS, CHUNK_TILES, 2, SEQ, HALVES, P)
    w1 = at("L0_ffn_w1").reshape(EXPERTS, HALVES, P, 2 * INNER).transpose(2, 1, 0, 3)
    shared_up = rows_first(_np.concatenate([at("L0_ffn_sw1"), at("L0_ffn_sw2")]), 2 * INNER)
    w_down = _np.concatenate([at("L0_ffn_w2"), at("L0_ffn_sw3").T[None]]).transpose(1, 0, 2)
    token = _np.arange(P)
    row = _np.arange(SEQ)
    select = _np.zeros((SEQ, HP, 2, SEQ), _np.uint16)
    select[row, (row % 32) // 2, row % 2] = 0x3F80
    arrays = {
        "in_x": at("x").reshape(TOKENS, EMBED),
        "in_ctx_t": at("ctx_2048").reshape(pairs).transpose(0, 5, 4, 2, 3, 1).reshape(CHUNKS * P, HALVES, CHUNK),
        "in_wq": rows_first(at("L0_xattn_Wq"), EMBED),
        "in_wkv": rows_first(_np.concatenate([at("L0_xattn_Wk"), at("L0_xattn_Wv")]), 2 * KV),
        "in_wfc": at("L0_xattn_Wfc").T.reshape(2, 4, 2, 2, HEAD_DIM, EMBED)
                  .transpose(0, 2, 1, 4, 3, 5).reshape(P, HALVES, EMBED),
        "in_bias": at("L0_xattn_bfc").reshape(EMBED),
        "in_gate": rows_first(at("L0_ffn_gate_w"), EXPERTS),
        "in_w_up": _np.concatenate([w1, shared_up[:, :, None]], axis=2),
        "in_w_down": w_down[:P],
        "in_w_down_b": w_down[P:],
        "in_ident": _np.eye(P, dtype=_np.float32),
        "in_select": select.reshape(SEQ, HP, P),
        "in_before": _np.where(token[:, None] < token[None], 0x3F80, 0).astype(_np.uint16),
        "in_expert_iota": _np.tile(_np.arange(EXPERTS, dtype=_np.float32), (P, 1)),
        "in_token_rows": (TOP_K * _np.arange(TOKENS, dtype=_np.int32).reshape(TILES, 1, P)
                          + _np.arange(TOP_K, dtype=_np.int32)[:, None]).transpose(2, 1, 0),
        "in_blank_rows": TOP_K * TOKENS + _np.arange(WAYS * P, dtype=_np.int32).reshape(WAYS, P).T,
        "in_tile_iota": _np.arange(MAX_TILES, dtype=_np.float32)[None],
    }
    nc = _bacc.Bacc("TRN2", target_bir_lowering=False, num_devices=1)
    io = Sizes()
    access = {}
    for name in arrays:
        arrays[name] = a = _np.ascontiguousarray(arrays[name])
        access[name] = nc.dram_tensor(name, a.shape, _mybir.dt.from_np(a.dtype), kind="ExternalInput").ap()
    io.x, io.ctx_t, io.wq, io.wkv = access["in_x"], access["in_ctx_t"], access["in_wq"], access["in_wkv"]
    io.wfc, io.bias, io.gate = access["in_wfc"], access["in_bias"], access["in_gate"]
    io.w_up, io.w_down, io.w_down_b = access["in_w_up"], access["in_w_down"], access["in_w_down_b"]
    io.ident, io.select, io.before = access["in_ident"], access["in_select"].bitcast(BF16), access["in_before"].bitcast(BF16)
    io.token_rows, io.blank_rows = access["in_token_rows"], access["in_blank_rows"]
    io.expert_iota, io.tile_iota = access["in_expert_iota"], access["in_tile_iota"]
    io.out = nc.dram_tensor("out", (TOKENS, EMBED), F32, kind="ExternalOutput").ap()
    cross_attention_experts(nc, io)
    r = _run(nc, [arrays], core_ids=[0])
    return r.results[0]["out"].reshape(BATCH, SEQ, EMBED)
```

```python
import math
from contextlib import ExitStack

import concourse.bass as bass
from concourse import mybir

F32 = mybir.dt.float32
BF16 = mybir.dt.bfloat16
I32 = mybir.dt.int32
ALU = mybir.AluOpType
ACT = mybir.ActivationFunctionType
AX = mybir.AxisListType

P = 128
BATCH, SEQ, EMBED = 64, 64, 256
TOKENS = BATCH * SEQ
TILES = TOKENS // P
HALVES = EMBED // P
HEADS, GROUPS, HEAD_DIM = 32, 8, 8
KV = GROUPS * HEAD_DIM
CHUNK_TILES = 4
CHUNK = CHUNK_TILES * P
CHUNKS = TOKENS // CHUNK
RUN = CHUNK_TILES * SEQ
SCALE = 1.0 / math.sqrt(HEAD_DIM)
EPS = 1e-5
Q_PART = (0, 0, 0, 1, 1, 2)
K_PART = (0, 1, 2, 0, 1, 0)
UNITS = 4
HP = HEADS // 2
EXPERTS, INNER, TOP_K = 8, 176, 2
INNER_B = INNER - P


def run_slots(eng, total, first, period, slot):
    turns = (total - 1 - first) // period
    if turns < 2:
        return 0
    for s in range(first):
        slot(s, 0)
    with eng.Fori(0, turns) as r:
        for i in range(period):
            slot(first + i, r)
    return first + turns * period


def held(eng, value):
    return value if isinstance(value, int) else eng.to_reg(value)


STORED = 2 * 16


class Shared:
    pass


MAX_TILES = TOKENS * TOP_K // P + EXPERTS - 1
SHARED = EXPERTS
WINDOW, WINDOW_FIRST = 6, 4
WINDOWS = len(range(WINDOW_FIRST, MAX_TILES - WINDOW + 1, 4))
ROW = EMBED + 1
WAYS = 4
FIRST_PART = 6
SORT_TILES = TILES // 2
EARLY = 8
SHARED_FIRST = 24
BLANK_GROUPS = MAX_TILES // WAYS


def blank_rows_at(io, tile, count):
    return io.sorted_x[bass.ds(tile * P, count * P), :].rearrange("(t p) f -> p t f", p=P)


def load_operands(sp, io, keep, c, b):
    q_op, k_op, qkv_in = keep.q_op, keep.k_op, keep.qkv_in
    for a in range(2):
        for n in range(len(Q_PART)):
            rows = slice(64 * a + HEAD_DIM * n, 64 * a + HEAD_DIM * (n + 1))
            sp.dma_start(k_op[b][rows, :, a, :],
                         io.k_dram[K_PART[n] * KV:(K_PART[n] + 1) * KV, bass.ds(c, 1),
                                   a * RUN:(a + 1) * RUN]
                         .rearrange("(g d) c n -> d g (c n)", d=HEAD_DIM)).then_inc(qkv_in[b], 16)
            sp.dma_start(q_op[b][rows, :, :],
                         io.q_dram[Q_PART[n] * EMBED:(Q_PART[n] + 1) * EMBED, bass.ds(c, 1),
                                   a * RUN:(a + 1) * RUN]
                         .rearrange("(h d) c n -> d h (c n)", d=HEAD_DIM)).then_inc(qkv_in[b], 16)


def project_phase(nc, ctx0, io, keep):
    with ExitStack() as ctx:
        def sb(name, shape, dt):
            return ctx.enter_context(nc.sbuf_tensor(name, shape, dt))

        def psum(name, shape, dt):
            return ctx.enter_context(nc.psum_tensor(name, shape, dt))

        def sem(name):
            return ctx.enter_context(nc.semaphore(name))

        x_sb, ident, bias_sb = keep.x_sb, keep.ident, keep.bias_sb
        wq, wkv = sb("wq", [P, HALVES, EMBED], F32), sb("wkv", [P, HALVES, 2 * KV], F32)
        blank_rows = sb("blank_rows", [P, WAYS], I32)
        ctx_t = sb("ctx_t", [P, 2, HALVES, CHUNK], F32)
        stats = sb("stats", [P, 2, CHUNK_TILES, 6], F32)
        mean_var = sb("mean_var", [P, 2, CHUNK_TILES, 2], F32)
        var_eps = sb("var_eps", [P, 2, CHUNK_TILES], F32)
        rstd = sb("rstd", [P, 2, CHUNK_TILES], F32)
        minus_half = sb("minus_half", [P, CHUNK_TILES], F32)
        xn = sb("xn", [P, 2, CHUNK_TILES, EMBED], F32)
        xn_t = sb("xn_t", [P, 2, HALVES, CHUNK], F32)
        q_parts = sb("q_parts", [P, 2, 3, HALVES, CHUNK], BF16)
        q_rest = sb("q_rest", [P, HALVES, CHUNK], F32)
        k_parts = sb("k_parts", [KV, 2, 3, CHUNK], BF16)
        k_rest = sb("k_rest", [KV, CHUNK], F32)
        v_t = sb("v_t", [P, 2, CHUNK], F32)

        xt_ps = [psum(f"xt_ps{i}", [P, CHUNK], F32) for i in range(HALVES)]
        q_ps = [psum(f"q_ps{i}", [P, CHUNK], F32) for i in range(HALVES)]
        kv_ps = psum("kv_ps", [P, CHUNK], F32)
        v_ps = psum("v_ps", [P, CHUNK_TILES, KV], F32)

        weights_in = sem("weights_in")
        x_in, ctx_in = [sem(f"x_in{b}") for b in range(2)], [sem(f"ctx_in{b}") for b in range(2)]
        stats_done, stats_ready, eps_added, rstd_ready, half_set = (
            sem("stats_done"), sem("stats_ready"), sem("eps_added"), sem("rstd_ready"), sem("half_set"))
        xn_ready, xt_done, xt_ready = sem("xn_ready"), sem("xt_done"), sem("xt_ready")
        q_done, kv_done, vt_done = sem("q_done"), sem("kv_done"), sem("vt_done")
        q1_ready, q_rest_ready, q2_ready, q3_ready = (
            sem("q1_ready"), sem("q_rest_ready"), sem("q2_ready"), sem("q3_ready"))
        k1_ready, k_rest_ready, k2_ready, k3_ready = (
            sem("k1_ready"), sem("k_rest_ready"), sem("k2_ready"), sem("k3_ready"))
        v_t_ready, v_ready = sem("v_t_ready"), sem("v_ready")
        blocks_set, bias_added = sem("blocks_set"), sem("bias_added")
        zeros_set = sem("zeros_set")
        stored = keep.stored

        block = ctx.enter_context(nc.Block())

        @block.sync
        def _(sp):
            def load_x(k, c, b):
                if k >= 2:
                    sp.wait_ge(stats_ready, CHUNK_TILES * (c - 1))
                sp.dma_start(x_sb[:, bass.ds(c * CHUNK_TILES, CHUNK_TILES), :],
                             io.x[bass.ds(c * CHUNK, CHUNK), :].rearrange("(i p) f -> p i f", p=P)
                             ).then_inc(x_in[b], 16)

            def load_context(k, c, b):
                if k >= 2:
                    sp.wait_ge(kv_done, c - 1)
                sp.dma_start(ctx_t[:, b], io.ctx_t[bass.ds(c * P, P)]).then_inc(ctx_in[b], 16)

            def store(c, b):
                sp.wait_ge(q3_ready, HALVES * (c + 1))
                sp.dma_start(io.q_dram[:, bass.ds(c, 1)].rearrange("(t p) c n -> p t (c n)", p=P),
                             q_parts[:, b].rearrange("p t h n -> p (t h) n")).then_inc(stored[b], 16)
                sp.wait_ge(k3_ready, c + 1)
                sp.dma_start(io.k_dram[:, bass.ds(c, 1)].rearrange("(t p) c n -> p t (c n)", p=KV),
                             k_parts[:, b]).then_inc(stored[b], 16)

            def slot(k, r):
                s = k + 2 * r
                if k == 0:
                    load_x(0, 0, 0)
                if k <= CHUNKS - 2:
                    load_x(k + 1, s + 1, (k + 1) % 2)
                if k == 0:
                    sp.dma_start(ident[:], io.ident).then_inc(weights_in, 16)
                    sp.dma_start(wq[:], io.wq).then_inc(weights_in, 16)
                if k >= 3:
                    if k == CHUNKS - 1:
                        sp.wait_ge(stored[(k - 3) % 2], STORED * ((k - 3) // 2))
                    store(s - 3, (k - 3) % 2)
                if k <= CHUNKS - 1:
                    load_context(k, s, k % 2)
                if k == 0:
                    sp.dma_start(wkv[:], io.wkv).then_inc(weights_in, 16)
                    sp.dma_start(bias_sb[:], io.bias.partition_broadcast(P)).then_inc(weights_in, 16)
                    sp.dma_start(blank_rows[:], io.blank_rows).then_inc(weights_in, 16)
                if k == CHUNKS - 1:
                    sp.dma_start(keep.select[:], io.select).then_inc(keep.consts_in, 16)
                    sp.dma_start(keep.w_out[:], io.wfc).then_inc(keep.consts_in, 16)
                if k == CHUNKS - 1:
                    sp.wait_ge(zeros_set, 4)
                    load_operands(sp, io, keep, 0, 0)
            for s in range(run_slots(sp, CHUNKS, 3, 2, slot), CHUNKS + 3):
                slot(s, 0)

        @block.gpsimd
        def _(pool):
            nc.gpsimd.memset(minus_half[:], -0.5).then_inc(half_set, 1)
            pool.wait_ge(half_set, 1)

            def reciprocal_deviation(c):
                b = c % 2
                pool.wait_ge(stats_ready, CHUNK_TILES * (c + 1))
                if c >= 2:
                    pool.wait_ge(xn_ready, CHUNK_TILES * (c - 1))
                nc.gpsimd.tensor_scalar(var_eps[:, b], mean_var[:, b, :, 1], EPS, None, ALU.add
                                        ).then_inc(eps_added, 1)
                pool.wait_ge(eps_added, c + 1)
                nc.gpsimd.tensor_tensor(rstd[:, b], var_eps[:, b], minus_half[:], ALU.pow
                                        ).then_inc(rstd_ready, 1)

            def add_bias(c):
                pool.wait_ge(xn_ready, CHUNK_TILES * (c + 1))
                tiles = slice(c * CHUNK_TILES, (c + 1) * CHUNK_TILES)
                nc.gpsimd.tensor_tensor(x_sb[:, tiles, :], x_sb[:, tiles, :],
                                        bias_sb[:].unsqueeze(1).to_broadcast([P, CHUNK_TILES, EMBED]), ALU.add
                                        ).then_inc(bias_added, 1)
            for c in range(CHUNKS + 2):
                if c < CHUNKS:
                    reciprocal_deviation(c)
                if 1 <= c <= len(keep.zeroed):
                    nc.gpsimd.memset(keep.zeroed[c - 1].bitcast(F32), 0.0).then_inc(zeros_set, 1)
                if c == 1:
                    pool.wait_ge(weights_in, 80)
                if c >= 2:
                    add_bias(c - 2)
                if c == len(keep.zeroed):
                    pool.wait_ge(zeros_set, c)
                    pool.wait_ge(bias_added, c - 1)
                    for a in range(2):
                        if a == 1:
                            pool.wait_ge(blocks_set, len(keep.v_op))
                        rows = slice(a * SEQ, (a + 1) * SEQ)
                        for v_op in keep.v_op:
                            ones = v_op[rows, :, :, 16 * a + 8:16 * a + 16].rearrange("p i g d -> p (i g) d")
                            nc.gpsimd.memset(ones, 1.0).then_inc(blocks_set, 1)
                    pool.wait_ge(blocks_set, 2 * len(keep.v_op))
                    nc.gpsimd.tensor_copy(keep.blank[:, :, EMBED:].bitcast(I32), blank_rows[:].unsqueeze(2)
                                          ).then_inc(keep.blank_set, 1)

        @block.vector
        def _(dve):
            def moments(k, c, b, turn):
                dve.wait_ge(x_in[b], 16 * (turn + 1))
                for i in range(CHUNK_TILES):
                    nc.vector.bn_stats(stats[:, b, i, :], x_sb[:, bass.ds(c * CHUNK_TILES + i, 1), :]
                                       ).then_inc(stats_done, 1)
                for i in range(CHUNK_TILES):
                    so_far = held(dve, CHUNK_TILES * c + i + 1)
                    dve.wait_ge(half_set, 1)
                    dve.wait_ge(stats_done, so_far)
                    nc.vector.bn_aggr(mean_var[:, b, i, :], stats[:, b, i, :]).then_inc(stats_ready, 1)

            def normalise(k, c, b):
                dve.wait_ge(rstd_ready, c + 1)
                if k >= 2:
                    dve.wait_ge(xt_done, c - 1)
                for i in range(CHUNK_TILES):
                    nc.vector.tensor_scalar(xn[:, b, i, :], x_sb[:, bass.ds(c * CHUNK_TILES + i, 1), :],
                                            mean_var[:, b, i, 0:1], rstd[:, b, i:i + 1],
                                            ALU.subtract, ALU.mult).then_inc(xn_ready, 1)

            def split_middle(k, c, b):
                if k >= 1:
                    dve.wait_ge(q3_ready, HALVES * c)
                    dve.wait_ge(k3_ready, c)
                for h in range(HALVES):
                    dve.wait_ge(q1_ready, HALVES * c + h + 1)
                    nc.vector.scalar_tensor_tensor(q_rest[:, h], q_ps[h][:], SCALE, q_parts[:, b, 0, h],
                                                   ALU.mult, ALU.subtract).then_inc(q_rest_ready, 1)
                dve.wait_ge(k1_ready, c + 1)
                nc.vector.tensor_tensor(k_rest[:], kv_ps[0:KV, :], k_parts[:, b, 0], ALU.subtract
                                        ).then_inc(k_rest_ready, 1)

            def split_small(c, b):
                for h in range(HALVES):
                    dve.wait_ge(q2_ready, HALVES * c + h + 1)
                    nc.vector.tensor_tensor(q_parts[:, b, 2, h], q_rest[:, h], q_parts[:, b, 1, h],
                                            ALU.subtract).then_inc(q3_ready, 1)
                dve.wait_ge(k2_ready, c + 1)
                nc.vector.tensor_tensor(k_parts[:, b, 2], k_rest[:], k_parts[:, b, 1], ALU.subtract
                                        ).then_inc(k3_ready, 1)

            def keep_values(c):
                dve.wait_ge(vt_done, c + 1)
                nc.vector.tensor_copy(keep.v_all[:, bass.ds(c * CHUNK_TILES, CHUNK_TILES), :], v_ps[:]
                                      ).then_inc(v_ready, 1)

            def slot(k, r):
                s = k + 2 * r
                if k >= 4:
                    keep_values(s - 4)
                if 1 <= k <= CHUNKS:
                    normalise(k - 1, s - 1, (k - 1) % 2)
                if 3 <= k <= CHUNKS + 2:
                    split_middle(k - 3, s - 3, (k - 3) % 2)
                if k <= CHUNKS - 1:
                    moments(k, s, k % 2, k // 2 + r)
                if 3 <= k <= CHUNKS + 2:
                    split_small(s - 3, (k - 3) % 2)
            for s in range(run_slots(dve, CHUNKS, 6, 2, slot), CHUNKS + 4):
                slot(s, 0)

        @block.scalar
        def _(act):
            def evacuate(k, c, b):
                act.wait_ge(xt_done, c + 1)
                if k >= 2:
                    act.wait_ge(kv_done, c - 1)
                for h in range(HALVES):
                    nc.scalar.activation(
                        xn_t[:, b, h].rearrange("p (a q i) -> p a i q", a=2, i=CHUNK_TILES),
                        xt_ps[h][:].rearrange("p (i a q) -> p a i q", a=2, i=CHUNK_TILES),
                        ACT.Copy).then_inc(xt_ready, 1)

            def split_large(k, c, b, turn):
                if k >= 2:
                    act.wait_ge(stored[b], STORED * turn)
                for h in range(HALVES):
                    act.wait_ge(q_done, HALVES * c + h + 1)
                    nc.scalar.activation(q_parts[:, b, 0, h], q_ps[h][:], ACT.Copy, scale=SCALE
                                         ).then_inc(q1_ready, 1)
                act.wait_ge(kv_done, c + 1)
                nc.scalar.activation(k_parts[:, b, 0], kv_ps[0:KV, :], ACT.Copy).then_inc(k1_ready, 1)
                nc.scalar.activation(v_t[KV:P, b], kv_ps[KV:P, :], ACT.Copy).then_inc(v_t_ready, 1)

            def split_middle(c, b):
                for h in range(HALVES):
                    act.wait_ge(q_rest_ready, HALVES * c + h + 1)
                    nc.scalar.activation(q_parts[:, b, 1, h], q_rest[:, h], ACT.Copy).then_inc(q2_ready, 1)
                act.wait_ge(k_rest_ready, c + 1)
                nc.scalar.activation(k_parts[:, b, 1], k_rest[:], ACT.Copy).then_inc(k2_ready, 1)

            def slot(k, r):
                s = k + 2 * r
                if k <= CHUNKS - 1:
                    evacuate(k, s, k % 2)
                if k >= 2:
                    split_middle(s - 2, k % 2)
                if 1 <= k <= CHUNKS:
                    split_large(k - 1, s - 1, (k - 1) % 2, (k - 1) // 2 + r)
            for s in range(run_slots(act, CHUNKS, 3, 2, slot), CHUNKS + 2):
                slot(s, 0)

        @block.tensor
        def _(pe):
            pe.wait_ge(weights_in, 80)

            def transpose_x(k, c, b):
                pe.wait_ge(xn_ready, CHUNK_TILES * (c + 1))
                if k >= 1:
                    pe.wait_ge(xt_ready, HALVES * c)
                for i in range(CHUNK_TILES):
                    for h in range(HALVES):
                        last = nc.tensor.transpose(xt_ps[h][:, i * P:(i + 1) * P],
                                                   xn[:, b, i, h * P:(h + 1) * P], ident[:])
                last.then_inc(xt_done, 1)

            def project(k, c, b, turn):
                pe.wait_ge(ctx_in[b], 16 * (turn + 1))
                pe.wait_ge(xt_ready, HALVES * (c + 1))
                for m in range(HALVES):
                    if k >= 1:
                        pe.wait_ge(q_rest_ready, HALVES * c)
                    for h in range(HALVES):
                        last = nc.tensor.matmul(q_ps[m][:], wq[:, h, m * P:(m + 1) * P], xn_t[:, b, h],
                                                start=(h == 0), stop=(h == HALVES - 1))
                    last.then_inc(q_done, 1)
                if k >= 1:
                    pe.wait_ge(k_rest_ready, c)
                    pe.wait_ge(v_t_ready, c)
                for h in range(HALVES):
                    last = nc.tensor.matmul(kv_ps[:], wkv[:, h], ctx_t[:, b, h],
                                            start=(h == 0), stop=(h == HALVES - 1))
                last.then_inc(kv_done, 1)

            def transpose_v(k, c, b):
                chunks, before = held(pe, c + 1), held(pe, c)
                pe.wait_ge(weights_in, 80)
                pe.wait_ge(v_t_ready, chunks)
                if k >= 1:
                    pe.wait_ge(v_ready, before)
                for i in range(CHUNK_TILES):
                    keys = v_t[KV:P, b].rearrange("p (n i) -> p n i", i=CHUNK_TILES)[:, :, i]
                    last = nc.tensor.transpose(v_ps[:, i, :], keys, ident[KV:P, KV:P])
                last.then_inc(vt_done, 1)

            def slot(k, r):
                s = k + 2 * r
                if k <= CHUNKS - 1:
                    transpose_x(k, s, k % 2)
                if 1 <= k <= CHUNKS:
                    project(k - 1, s - 1, (k - 1) % 2, (k - 1) // 2 + r)
                if k >= 2:
                    transpose_v(k - 2, s - 2, k % 2)
            for s in range(run_slots(pe, CHUNKS, 3, 2, slot), CHUNKS + 2):
                slot(s, 0)


def attention_phase(nc, ctx0, io, keep):
    with ExitStack() as ctx:
        def sb(name, shape, dt):
            return ctx.enter_context(nc.sbuf_tensor(name, shape, dt))

        def psum(name, shape, dt):
            return ctx.enter_context(nc.psum_tensor(name, shape, dt))

        def sem(name):
            return ctx.enter_context(nc.semaphore(name))

        x_sb, ident = keep.x_sb, keep.ident
        q_op, k_op = keep.q_op, keep.k_op
        w_out, select = keep.w_out, keep.select
        v_op, qkv_in, v_placed = keep.v_op, keep.qkv_in, sem("v_placed")
        ident_b = sb("ident_b", [P, P], BF16)
        row_max = sb("row_max", [P, 2, 2 * HP], F32)
        minus_max = sb("minus_max", [P, 2, 2, 2 * HP], BF16)
        max_t = sb("max_t", [SEQ, 2, P], BF16)
        probs = sb("probs", [P, UNITS, 512], F32)
        pv_sb = sb("pv_sb", [P, 512], F32)
        recip = sb("recip", [P, 2 * HP], F32)
        heads_out = sb("heads_out", [P, 2, P], F32)
        heads_t = sb("heads_t", [P, 2, 2, SEQ], F32)

        score_ps = [psum(f"score_ps{b}", [P, 512], F32) for b in range(2)]
        shift_ps = [psum(f"shift_ps{b}", [P, 512], F32) for b in range(2)]
        pv_ps = psum("pv_ps", [P, 512], F32)
        nat_ps = psum("nat_ps", [P, 512], F32)
        misc_ps = psum("misc_ps", [P, 512], F32)
        max_ps = misc_ps[:].bitcast(BF16)[0:SEQ, 0:P]
        back_ps = misc_ps[:, 0:2 * P]
        out_ps = psum("out_ps", [P, EMBED], F32)

        xn_all = keep.xn_all
        moments = sb("a_moments", [P, 2, 6], F32)
        mean_var = sb("a_mean_var", [P, 2, 2], F32)
        var_eps, rstd = sb("a_var_eps", [P, 2], F32), sb("a_rstd", [P, 2], F32)
        minus_half = sb("a_minus_half", [P, 1], F32)
        centred = sb("centred", [P, 2, EMBED], F32)

        consts_in, identb_ready = keep.consts_in, sem("identb_ready")
        half_set, moments_done, mean_ready, eps_ready = (
            sem("a_half_set"), sem("a_moments_done"), sem("a_mean_ready"), sem("a_eps_ready"))
        rstd_ready, centred_ready, xn_ready = sem("a_rstd_ready"), sem("a_centred_ready"), sem("a_xn_ready")
        scores_done, max_ready, hi_ready, minus_ready = (
            sem("scores_done"), sem("max_ready"), sem("hi_ready"), sem("minus_ready"))
        max_t_done, max_t_ready = sem("max_t_done"), sem("max_t_ready")
        shifted_done, probs_ready = sem("shifted_done"), sem("probs_ready")
        pv_done, pv_ready = sem("pv_done"), sem("pv_ready")
        nat_done, recip_ready, heads_ready = sem("nat_done"), sem("recip_ready"), sem("heads_ready")
        back_done, heads_t_ready = sem("back_done"), sem("heads_t_ready")
        out_done, x_ready = sem("out_done"), sem("x_ready")
        LOADS = 2 * (2 * len(Q_PART))
        PERIOD = 2 * CHUNK_TILES

        block = ctx.enter_context(nc.Block())

        @block.sync
        def _(sp):
            sp.wait_ge(keep.stored[1], STORED * (CHUNKS // 2))
            load_operands(sp, io, keep, 1, 1)
            sp.wait_ge(keep.stored[0], STORED * (CHUNKS // 2))
            sp.wait_ge(keep.blank_set, 1)
            for src, dst in keep.prefetch:
                sp.dma_start(dst, src).then_inc(keep.prefetched, 16)
            per_turn = BLANK_GROUPS // (CHUNKS // 2 - 1)
            with sp.Fori(1, CHUNKS // 2) as r:
                for b in range(2):
                    sp.wait_ge(pv_done, CHUNK_TILES * (2 * r + b - 1))
                    load_operands(sp, io, keep, 2 * r + b, b)
                for n in range(per_turn):
                    first = (r - 1) * per_turn + n
                    sp.dma_start(blank_rows_at(io, first * WAYS, WAYS), keep.blank[:]).then_inc(keep.prefetched, 16)
            for first in range(per_turn * (CHUNKS // 2 - 1), BLANK_GROUPS):
                sp.dma_start(blank_rows_at(io, first * WAYS, WAYS), keep.blank[:]).then_inc(keep.prefetched, 16)
            sp.wait_ge(keep.prefetched, 16 * (len(keep.prefetch) + BLANK_GROUPS))

        @block.gpsimd
        def _(pool):
            nc.gpsimd.memset(minus_half[:], -0.5).then_inc(half_set, 1)
            pool.wait_ge(half_set, 1)

            def normalise(k, r):
                p, b = k + 2 * r, k % 2
                now, before = held(pool, p + 1), held(pool, p - 1)
                pool.wait_ge(half_set, 1)
                pool.wait_ge(mean_ready, now)
                if k >= 2:
                    pool.wait_ge(xn_ready, before)
                nc.gpsimd.tensor_scalar(var_eps[:, b:b + 1], mean_var[:, b, 1:2], EPS, None, ALU.add
                                        ).then_inc(eps_ready, 1)
                nc.gpsimd.tensor_tensor(centred[:, b:b + 1, :], x_sb[:, bass.ds(p, 1), :],
                                        mean_var[:, b:b + 1, 0:1].to_broadcast([P, 1, EMBED]), ALU.subtract
                                        ).then_inc(centred_ready, 1)
                now = held(pool, p + 1)
                pool.wait_ge(half_set, 1)
                pool.wait_ge(eps_ready, now)
                nc.gpsimd.tensor_tensor(rstd[:, b:b + 1], var_eps[:, b:b + 1], minus_half[:], ALU.pow
                                        ).then_inc(rstd_ready, 1)
                now = held(pool, p + 1)
                pool.wait_ge(half_set, 1)
                pool.wait_ge(rstd_ready, now)
                pool.wait_ge(centred_ready, now)
                nc.gpsimd.tensor_tensor(xn_all[:, bass.ds(p, 1), 0:EMBED], centred[:, b:b + 1, :],
                                        rstd[:, b:b + 1].unsqueeze(2).to_broadcast([P, 1, EMBED]), ALU.mult
                                        ).then_inc(xn_ready, 1)
            for s in range(run_slots(pool, TILES, 2, 2, normalise), TILES):
                normalise(s, 0)

        @block.tensor
        def _(pe):
            pe.wait_ge(consts_in, 32)
            pe.wait_ge(identb_ready, 1)

            def scores(k, p, us, kc, turn):
                b, i = kc
                if us[0] == 0:
                    pe.wait_ge(qkv_in[b], 16 * LOADS * (turn + 1))
                for u in us:
                    if UNITS * k + u >= 2:
                        pe.wait_ge(max_ready, UNITS * p + u - 1)
                    for j in range(4):
                        g, hp = 2 * u + j // 2, 4 * u + j
                        q = q_op[b][:, 2 * hp:2 * hp + 2].rearrange("p h (q i) -> p (h q) i", i=CHUNK_TILES)[:, :, i]
                        kk = k_op[b][:, g].rearrange("p a (q i) -> p (a q) i", i=CHUNK_TILES)[:, :, i]
                        last = nc.tensor.matmul(score_ps[u % 2][:, j * P:(j + 1) * P], q, kk,
                                                start=True, stop=True)
                    last.then_inc(scores_done, 1)

            def transpose_max(k, p):
                tile, before = held(pe, p + 1), held(pe, p - 1)
                pe.wait_ge(identb_ready, 1)
                pe.wait_ge(minus_ready, tile)
                if k >= 2:
                    pe.wait_ge(heads_t_ready, before)
                nc.tensor.transpose(max_ps, minus_max[:, k % 2].rearrange("p t n -> p (t n)"), ident_b[:]
                                    ).then_inc(max_t_done, 1)

            def shifted(k, p, u, kc):
                b, i = kc
                if u == 0:
                    pe.wait_ge(max_t_ready, p + 1)
                if UNITS * k + u >= 2:
                    pe.wait_ge(probs_ready, UNITS * p + u - 1)
                for g in (2 * u, 2 * u + 1):
                    out = shift_ps[u % 2][:, (g % 2) * 256:(g % 2) * 256 + 256]
                    q = q_op[b][:, 4 * g:4 * g + 4].rearrange("p h (q i) -> p (h q) i", i=CHUNK_TILES)[:, :, i]
                    kk = k_op[b][:, g].rearrange("p a (q i) -> p (a q) i", i=CHUNK_TILES)[:, :, i]
                    nc.tensor.matmul(out, kk, q, start=True, stop=False)
                    for j in range(2):
                        last = nc.tensor.matmul(out[:, j * P:(j + 1) * P], select[:, 2 * g + j, :],
                                                max_t[:, k % 2, :], start=False, stop=(j == 1))
                last.then_inc(shifted_done, 1)

            def values(k, p, u, kc, placed):
                b, i = kc
                if u == 0 and k >= 1:
                    pe.wait_ge(pv_ready, p)
                if u == 0 and i == 0:
                    pe.wait_ge(v_placed, placed)
                pe.wait_ge(probs_ready, UNITS * p + u + 1)
                for g in (2 * u, 2 * u + 1):
                    gi, half = g % 4, g // 4
                    last = nc.tensor.matmul(pv_ps[32 * gi:32 * gi + 32, 256 * half:256 * half + 256],
                                            v_op[b][:, i, g, :], probs[:, u, (g % 2) * 256:(g % 2) * 256 + 256],
                                            start=True, stop=True)
                if u == UNITS - 1:
                    last.then_inc(pv_done, 1)

            def to_tokens(k, p):
                pe.wait_ge(pv_ready, p + 1)
                if k >= 1:
                    pe.wait_ge(heads_ready, p)
                for n in range(4):
                    last = nc.tensor.transpose(nat_ps[:, n * P:(n + 1) * P], pv_sb[:, n * P:(n + 1) * P],
                                               ident[:])
                last.then_inc(nat_done, 1)

            def to_features(k, p, more):
                pe.wait_ge(heads_ready, p + 1)
                if more:
                    pe.wait_ge(max_t_ready, p + 2)
                for a in range(2):
                    last = nc.tensor.transpose(back_ps[:, a * P:(a + 1) * P], heads_out[:, a, :], ident[:])
                last.then_inc(back_done, 1)

            def project_out(k, p):
                pe.wait_ge(heads_t_ready, p + 1)
                if k >= 1:
                    pe.wait_ge(x_ready, p)
                for jj in range(2):
                    last = nc.tensor.matmul(out_ps[:], heads_t[:, jj].rearrange("p a q -> p (a q)"),
                                            w_out[:, jj], start=(jj == 0), stop=(jj == 1))
                last.then_inc(out_done, 1)

            def slot(k, r):
                s = k + PERIOD * r
                now = ((k // CHUNK_TILES) % 2, k % CHUNK_TILES)
                before = (((k - 1) // CHUNK_TILES) % 2, (k - 1) % CHUNK_TILES)
                turn = k // PERIOD + r
                placed = (k - 1) // CHUNK_TILES + 2 * r + 1
                a_on, b_on, f_on = k <= TILES - 1, 1 <= k <= TILES, 2 <= k
                if b_on:
                    transpose_max(k - 1, s - 1)
                if a_on:
                    scores(k, s, (0, 1), now, turn)
                if f_on:
                    to_tokens(k - 2, s - 2)
                if b_on:
                    shifted(k - 1, s - 1, 0, before)
                if a_on:
                    scores(k, s, (2,), now, turn)
                if b_on:
                    shifted(k - 1, s - 1, 1, before)
                if a_on:
                    scores(k, s, (3,), now, turn)
                if f_on:
                    to_features(k - 2, s - 2, b_on)
                if b_on:
                    shifted(k - 1, s - 1, 2, before)
                    values(k - 1, s - 1, 0, before, placed)
                    shifted(k - 1, s - 1, 3, before)
                    values(k - 1, s - 1, 1, before, placed)
                if f_on:
                    project_out(k - 2, s - 2)
                if b_on:
                    values(k - 1, s - 1, 2, before, placed)
                    values(k - 1, s - 1, 3, before, placed)
            for s in range(run_slots(pe, TILES, 3, PERIOD, slot), TILES + 2):
                slot(s, 0)

        @block.scalar
        def _(act):
            def exponentials(k, p, us):
                for u in us:
                    act.wait_ge(shifted_done, UNITS * p + u + 1)
                    if u == 0 and k >= 1:
                        act.wait_ge(pv_done, p)
                    nc.scalar.activation(probs[:, u], shift_ps[u % 2][:], ACT.Exp).then_inc(probs_ready, 1)

            def copy_pv(k, p):
                act.wait_ge(pv_done, p + 1)
                if k >= 1:
                    act.wait_ge(nat_done, p)
                nc.scalar.activation(pv_sb[:], pv_ps[:], ACT.Copy).then_inc(pv_ready, 1)

            def copy_heads(k, p):
                act.wait_ge(back_done, p + 1)
                if k >= 1:
                    act.wait_ge(out_done, p)
                nc.scalar.activation(heads_t[:].rearrange("p j a q -> p a j q"),
                                     back_ps.rearrange("p (a j q) -> p a j q", a=2, j=2),
                                     ACT.Copy).then_inc(heads_t_ready, 1)

            def slot(k, r):
                s = k + PERIOD * r
                b_on, f_on = 1 <= k <= TILES, 2 <= k
                if b_on:
                    exponentials(k - 1, s - 1, (0, 1))
                if f_on:
                    copy_heads(k - 2, s - 2)
                if b_on:
                    exponentials(k - 1, s - 1, (2, 3))
                    copy_pv(k - 1, s - 1)
            for s in range(run_slots(act, TILES, 3, PERIOD, slot), TILES + 2):
                slot(s, 0)

        @block.vector
        def _(dve):
            dve.wait_ge(consts_in, 32)
            nc.vector.tensor_copy(ident_b[:], ident[:]).then_inc(identb_ready, 1)

            def place_values(k, c, b, used):
                if k >= CHUNK_TILES:
                    dve.wait_ge(pv_done, used)
                tiles = bass.ds(c * CHUNK_TILES, CHUNK_TILES)
                for a in range(2):
                    rows = slice(a * SEQ, (a + 1) * SEQ)
                    last = nc.vector.tensor_copy(
                        v_op[b][rows, :, :, 16 * a:16 * a + 8],
                        keep.v_all[rows, tiles, :].rearrange("p i (g d) -> p i g d", g=GROUPS))
                last.then_inc(v_placed, 1)

            def maxima(k, p, us):
                for u in us:
                    dve.wait_ge(scores_done, UNITS * p + u + 1)
                    if u == 0 and k >= 2:
                        dve.wait_ge(minus_ready, p - 1)
                    nc.vector.reduce_max(row_max[:, k % 2, 8 * u:8 * u + 8],
                                         score_ps[u % 2][:].rearrange("p (n t) -> p n t", t=SEQ), AX.X
                                         ).then_inc(max_ready, 1)

            def negate_maxima(k, p):
                dve.wait_ge(max_ready, UNITS * (p + 1))
                if k >= 2:
                    dve.wait_ge(max_t_done, p - 1)
                nc.vector.tensor_scalar(minus_max[:, k % 2, 0], row_max[:, k % 2], -1.0, None, ALU.mult
                                        ).then_inc(hi_ready, 1)
                dve.wait_ge(hi_ready, p + 1)
                nc.vector.scalar_tensor_tensor(minus_max[:, k % 2, 1], row_max[:, k % 2], -1.0,
                                               minus_max[:, k % 2, 0], ALU.mult, ALU.subtract
                                               ).then_inc(minus_ready, 1)

            def copy_max(k, p):
                dve.wait_ge(max_t_done, p + 1)
                if k >= 2:
                    dve.wait_ge(shifted_done, UNITS * (p - 1))
                nc.vector.tensor_copy(max_t[:, k % 2], max_ps).then_inc(max_t_ready, 1)

            def normalise(k, p):
                sums = nat_ps[:].rearrange("p (n m) -> p n m", m=16)
                dve.wait_ge(nat_done, p + 1)
                if k >= 1:
                    dve.wait_ge(heads_ready, p)
                nc.vector.reciprocal(recip[:], sums[:, :, 8]).then_inc(recip_ready, 1)
                dve.wait_ge(recip_ready, p + 1)
                if k >= 1:
                    dve.wait_ge(back_done, p)
                nc.vector.tensor_tensor(
                    heads_out[:].rearrange("p a (n d) -> p n a d", d=HEAD_DIM),
                    nat_ps[:].rearrange("p (n a m) -> p n a m", a=2, m=16)[:, :, :, 0:8],
                    recip[:].rearrange("p (n a) -> p n a", a=2).unsqueeze(3).to_broadcast([P, HP, 2, HEAD_DIM]),
                    ALU.mult).then_inc(heads_ready, 1)

            def add_residual(k, p):
                dve.wait_ge(out_done, p + 1)
                nc.vector.tensor_tensor(x_sb[:, bass.ds(p, 1), :], out_ps[:].unsqueeze(1),
                                        x_sb[:, bass.ds(p, 1), :], ALU.add).then_inc(x_ready, 1)

            def take_moments(k, p):
                now, before = held(dve, p + 1), held(dve, p - 1)
                dve.wait_ge(identb_ready, 1)
                dve.wait_ge(x_ready, now)
                if k >= 2:
                    dve.wait_ge(mean_ready, before)
                nc.vector.bn_stats(moments[:, k % 2], x_sb[:, bass.ds(p, 1), :]).then_inc(moments_done, 1)

            def take_mean(k, p):
                now, before = held(dve, p + 1), held(dve, p - 1)
                dve.wait_ge(identb_ready, 1)
                dve.wait_ge(moments_done, now)
                if k >= 2:
                    dve.wait_ge(xn_ready, before)
                nc.vector.bn_aggr(mean_var[:, k % 2], moments[:, k % 2]).then_inc(mean_ready, 1)

            def slot(k, r):
                s = k + PERIOD * r
                a_on, b_on, f_on, g_on = k <= TILES - 1, 1 <= k <= TILES, 2 <= k <= TILES + 1, 3 <= k
                if b_on:
                    copy_max(k - 1, s - 1)
                if a_on:
                    maxima(k, s, (0, 1))
                if f_on:
                    normalise(k - 2, s - 2)
                if a_on:
                    maxima(k, s, (2, 3))
                if g_on:
                    take_moments(k - 3, s - 3)
                if a_on:
                    negate_maxima(k, s)
                if f_on:
                    add_residual(k - 2, s - 2)
                if g_on:
                    take_mean(k - 3, s - 3)
                if k % CHUNK_TILES == 2 and k < TILES - CHUNK_TILES:
                    c = k // CHUNK_TILES + 1
                    place_values(k, c + 2 * r, c % 2, s - 2)
            place_values(0, 0, 0, 0)
            for s in range(run_slots(dve, TILES, 5, PERIOD, slot), TILES + 3):
                slot(s, 0)


def routing_phase(nc, ctx0, io, keep):
    with ExitStack() as ctx:
        def sb(name, shape, dt):
            return ctx.enter_context(nc.sbuf_tensor(name, shape, dt))

        def psum(name, shape, dt):
            return ctx.enter_context(nc.psum_tensor(name, shape, dt))

        def sem(name):
            return ctx.enter_context(nc.semaphore(name))

        x_sb, ident, xn_all = keep.x_sb, keep.ident, keep.xn_all
        xn_t = sb("r_xn_t", [P, 2, HALVES, CHUNK], F32)
        gate, expert_iota, tile_iota = keep.gate, keep.expert_iota, keep.tile_iota
        before = keep.before
        logit_t = sb("r_logit_t", [EXPERTS, CHUNK], F32)
        ones = sb("r_ones", [P, P], BF16)
        logits = sb("r_logits", [P, TILES, EXPERTS], F32)
        work = sb("r_work", [P, TILES, EXPERTS], F32)
        scores = sb("r_scores", [P, TILES, EXPERTS], F32)
        hot = [sb(f"r_hot{n}", [P, TILES, EXPERTS], F32) for n in range(TOP_K)]
        mask = sb("r_mask", [P, TILES, EXPERTS], BF16)
        col = sb("r_col", [P, 8, TILES], F32)
        PAD = TILES // 2
        scan = [sb(f"r_scan{n}", [P, EXPERTS, PAD + TILES], F32) for n in range(2)]
        tiles_i = sb("r_tiles_i", [P, 2, EXPERTS], I32)
        ends = [sb(f"r_ends{n}", [P, EXPERTS // 2 + EXPERTS], F32) for n in range(2)]
        place = sb("r_place", [P, TILES, EXPERTS], F32)
        of_tile = sb("r_of_tile", [1, MAX_TILES, EXPERTS], F32)
        window_sum = sb("r_window_sum", [1, WINDOWS], F32)
        of_tile_sum = sb("r_of_tile_sum", [1, MAX_TILES], F32)

        xt_ps = [psum(f"r_xt_ps{i}", [P, CHUNK], F32) for i in range(HALVES)]
        gate_ps = psum("r_gate_ps", [EXPERTS, CHUNK], F32)
        logit_ps = psum("r_logit_ps", [P, CHUNK_TILES, EXPERTS], F32)
        rank_ps = psum("r_rank_ps", [P, TILES, EXPERTS], F32)
        count_ps = psum("r_count_ps", [P, TILES, EXPERTS], F32)

        half_set, experts_in = sem("r_half_set"), sem("r_experts_in")
        xt_done, xt_ready = sem("r_xt_done"), sem("r_xt_ready")
        gate_done, gate_ready, logit_done, logit_ready = (
            sem("r_gate_done"), sem("r_gate_ready"), sem("r_logit_done"), sem("r_logit_ready"))
        row_ready = sem("r_row_ready")
        shift_done = sem("r_shift_done")
        PARTS = (slice(0, FIRST_PART * CHUNK_TILES), slice(FIRST_PART * CHUNK_TILES, TILES))
        step, exp_done, mask_ready, ranked = sem("r_step"), sem("r_exp_done"), sem("r_mask_ready"), sem("r_ranked")

        block = ctx.enter_context(nc.Block())

        @block.sync
        def _(sp):
            for dst, src in ((keep.w_up, io.w_up), (keep.w_down, io.w_down), (keep.w_down_b, io.w_down_b)):
                sp.dma_start(dst[:], src).then_inc(experts_in, 16)
            sp.wait_ge(experts_in, 48)

        @block.gpsimd
        def _(pool):
            nc.gpsimd.memset(ones[:], 1.0).then_inc(half_set, 1)
            for n in range(2):
                nc.gpsimd.memset(scan[n][:], 0.0).then_inc(half_set, 1)
                nc.gpsimd.memset(ends[n][:], 0.0).then_inc(half_set, 1)
            nc.gpsimd.tensor_copy(xn_all[:, :, EMBED:].bitcast(I32), keep.token_rows[:, 0, :].unsqueeze(2)
                                  ).then_inc(keep.rows_set, 1)
            pool.wait_ge(keep.rows_set, 1)
            pool.wait_ge(row_ready, 1)
            for t in range(EARLY):
                nc.gpsimd.indirect_dma_start(
                    io.sorted_x, bass.IndirectOffsetOnAxis(ap=keep.row[:, 0, t:t + 1], axis=0),
                    xn_all[:, t, :], None).then_inc(keep.sorted_in[t // SORT_TILES], 16)

        @block.scalar
        def _(act):
            def evacuate(k, c, b):
                act.wait_ge(xt_done, c + 1)
                if k >= 2:
                    act.wait_ge(gate_done, c - 1)
                for h in range(HALVES):
                    nc.scalar.activation(xn_t[:, b, h], xt_ps[h][:], ACT.Copy).then_inc(xt_ready, 1)

            def copy_gate(k, c):
                act.wait_ge(gate_done, c + 1)
                if k >= 1:
                    act.wait_ge(logit_done, c)
                nc.scalar.activation(logit_t[:], gate_ps[:], ACT.Copy).then_inc(gate_ready, 1)

            def slot(k, r):
                s = k + 2 * r
                if k <= CHUNKS - 1:
                    evacuate(k, s, k % 2)
                if k >= 1:
                    copy_gate(k - 1, s - 1)
            def exponentials(part):
                tiles = PARTS[part]
                act.wait_ge(shift_done, part + 1)
                nc.scalar.activation(scores[:, tiles], work[:, tiles], ACT.Exp).then_inc(exp_done, 1)
            for s in range(run_slots(act, CHUNKS, 2, 2, slot), CHUNKS + 1):
                if s == CHUNKS:
                    exponentials(0)
                slot(s, 0)
            exponentials(1)

        @block.tensor
        def _(pe):
            def transpose_x(k, c, b):
                if k >= 1:
                    pe.wait_ge(xt_ready, HALVES * c)
                for i in range(CHUNK_TILES):
                    for h in range(HALVES):
                        last = nc.tensor.transpose(xt_ps[h][:, i * P:(i + 1) * P],
                                                   xn_all[:, c * CHUNK_TILES + i, h * P:(h + 1) * P], ident[:])
                last.then_inc(xt_done, 1)

            def gate_scores(k, c, b):
                pe.wait_ge(xt_ready, HALVES * (c + 1))
                if k >= 1:
                    pe.wait_ge(gate_ready, c)
                for h in range(HALVES):
                    last = nc.tensor.matmul(gate_ps[:], gate[:, h], xn_t[:, b, h],
                                            start=(h == 0), stop=(h == HALVES - 1))
                last.then_inc(gate_done, 1)

            def transpose_logits(k, c):
                pe.wait_ge(gate_ready, c + 1)
                if k >= 1:
                    pe.wait_ge(logit_ready, c)
                for i in range(CHUNK_TILES):
                    last = nc.tensor.transpose(logit_ps[:, i, :], logit_t[:, i * P:(i + 1) * P],
                                               ident[0:EXPERTS, 0:EXPERTS])
                last.then_inc(logit_done, 1)

            def slot(k, r):
                s = k + 2 * r
                if k <= CHUNKS - 1:
                    transpose_x(k, s, k % 2)
                if 1 <= k <= CHUNKS:
                    gate_scores(k - 1, s - 1, (k - 1) % 2)
                if k >= 2:
                    transpose_logits(k - 2, s - 2)
            for s in range(CHUNKS + 2):
                slot(s, 0)
            pe.wait_ge(half_set, 5)
            pe.wait_ge(mask_ready, 2)
            chosen = mask[:].rearrange("p t e -> p (t e)")
            nc.tensor.matmul(rank_ps[:].rearrange("p t e -> p (t e)"), before[:], chosen, start=True, stop=True)
            nc.tensor.matmul(count_ps[:].rearrange("p t e -> p (t e)"), ones[:], chosen, start=True, stop=True
                             ).then_inc(ranked, 1)

        @block.vector
        def _(dve):
            def copy_logits(c):
                dve.wait_ge(logit_done, c + 1)
                nc.vector.tensor_copy(logits[:, bass.ds(c * CHUNK_TILES, CHUNK_TILES), :], logit_ps[:]
                                      ).then_inc(logit_ready, 1)

            done = [0]

            def then(instruction):
                instruction.then_inc(step, 1)
                done[0] += 1
                dve.wait_ge(step, done[0])

            def best_two(part):
                tiles = PARTS[part]
                shape = [P, tiles.stop - tiles.start, EXPERTS]
                dve.wait_ge(logit_ready, tiles.stop // CHUNK_TILES)

                def by_tile(c):
                    return col[:, c, tiles].unsqueeze(2).to_broadcast(shape)

                iota = expert_iota[:].unsqueeze(1).to_broadcast(shape)
                w, p = work[:, tiles], scores[:, tiles]
                then(nc.vector.reduce_max(col[:, 0, tiles], logits[:, tiles], AX.X))
                nc.vector.tensor_tensor(w, logits[:, tiles], by_tile(0), ALU.subtract).then_inc(shift_done, 1)
                dve.wait_ge(exp_done, part + 1)
                then(nc.vector.reduce_sum(col[:, 1, tiles], p, AX.X))
                then(nc.vector.reciprocal(col[:, 2, tiles], col[:, 1, tiles]))
                then(nc.vector.tensor_tensor(p, p, by_tile(2), ALU.mult))
                for n in range(TOP_K):
                    then(nc.vector.reduce_max(col[:, 3 + n, tiles], p, AX.X))
                    then(nc.vector.tensor_tensor(w, p, by_tile(3 + n), ALU.is_equal))
                    then(nc.vector.scalar_tensor_tensor(w, w, -float(EXPERTS), iota, ALU.mult, ALU.add))
                    then(nc.vector.tensor_reduce(col[:, 5, tiles], w, AX.X, ALU.min))
                    then(nc.vector.tensor_scalar(col[:, 5, tiles], col[:, 5, tiles], float(EXPERTS), None, ALU.add))
                    then(nc.vector.tensor_tensor(hot[n][:, tiles], iota, by_tile(5), ALU.is_equal))
                    if n == 0:
                        then(nc.vector.scalar_tensor_tensor(p, hot[0][:, tiles], -2.0, p, ALU.mult, ALU.add))
                nc.vector.tensor_tensor(mask[:, tiles], hot[0][:, tiles], hot[1][:, tiles], ALU.add
                                        ).then_inc(mask_ready, 1)
            dve.wait_ge(half_set, 5)
            for part in range(2):
                for c in range(PARTS[part].start // CHUNK_TILES, PARTS[part].stop // CHUNK_TILES):
                    copy_logits(c)
                best_two(part)
            dve.wait_ge(ranked, 1)
            then(nc.vector.tensor_copy(scan[0][:, :, PAD:], count_ps[:].rearrange("p t e -> p e t")))
            side, far = 0, 1
            while far < TILES:
                then(nc.vector.tensor_tensor(scan[1 - side][:, :, PAD:], scan[side][:, :, PAD:],
                                             scan[side][:, :, PAD - far:PAD + TILES - far], ALU.add))
                side, far = 1 - side, 2 * far
            upto = scan[side]
            then(nc.vector.tensor_scalar(tiles_i[:, 0], upto[:, :, PAD + TILES - 1], float(P - 1), None, ALU.add))
            then(nc.vector.tensor_scalar(tiles_i[:, 1], tiles_i[:, 0], 7, None, ALU.logical_shift_right))
            LEFT = EXPERTS // 2
            then(nc.vector.tensor_copy(ends[0][:, LEFT:], tiles_i[:, 1]))
            e_side, far = 0, 1
            while far < EXPERTS:
                then(nc.vector.tensor_tensor(ends[1 - e_side][:, LEFT:], ends[e_side][:, LEFT:],
                                             ends[e_side][:, LEFT - far:LEFT + EXPERTS - far], ALU.add))
                e_side, far = 1 - e_side, 2 * far
            end = ends[e_side]
            first_tile = end[:, LEFT - 1:LEFT + EXPERTS - 1].unsqueeze(1).to_broadcast([P, TILES, EXPERTS])
            then(nc.vector.tensor_tensor(place[:], rank_ps[:],
                                         upto[:, :, PAD - 1:PAD + TILES - 1].rearrange("p e t -> p t e"), ALU.add))
            then(nc.vector.scalar_tensor_tensor(place[:], first_tile, float(P), place[:], ALU.mult, ALU.add))
            for n in range(TOP_K):
                then(nc.vector.tensor_tensor(work[:], hot[n][:], place[:], ALU.mult))
                then(nc.vector.reduce_sum(col[:, 5], work[:], AX.X))
                nc.vector.tensor_copy(keep.row[:, n], col[:, 5]).then_inc(row_ready, 1)
                dve.wait_ge(row_ready, n + 1)
            then(nc.vector.tensor_tensor(col[:, 6], col[:, 3], col[:, 4], ALU.add))
            then(nc.vector.tensor_scalar(col[:, 6], col[:, 6], 1e-20, None, ALU.add))
            then(nc.vector.reciprocal(col[:, 7], col[:, 6]))
            for n in range(TOP_K):
                then(nc.vector.tensor_tensor(keep.weight[:, n], col[:, 3 + n], col[:, 7], ALU.mult))
            then(nc.vector.tensor_tensor(
                of_tile[:], end[0:1, LEFT:].unsqueeze(1).to_broadcast([1, MAX_TILES, EXPERTS]),
                tile_iota[:].unsqueeze(2).to_broadcast([1, MAX_TILES, EXPERTS]), ALU.is_le))
            then(nc.vector.reduce_sum(of_tile_sum[:], of_tile[:], AX.X))
            then(nc.vector.tensor_scalar(of_tile_sum[:], of_tile_sum[:], float(EXPERTS - 1), None, ALU.min))
            then(nc.vector.tensor_copy(keep.tile_expert[:], of_tile_sum[:]))
            then(nc.vector.tensor_copy(window_sum[:], of_tile_sum[:, WINDOW_FIRST:MAX_TILES - WINDOW + 1:4]))
            for n in range(1, WINDOW):
                then(nc.vector.scalar_tensor_tensor(
                    window_sum[:], of_tile_sum[:, WINDOW_FIRST + n:MAX_TILES - WINDOW + 1 + n:4],
                    float(EXPERTS ** n), window_sum[:], ALU.mult, ALU.add))
            then(nc.vector.tensor_copy(keep.windows[:], window_sum[:]))


def ffn_phase(nc, ctx0, io, keep):
    with ExitStack() as ctx:
        def sb(name, shape, dt):
            return ctx.enter_context(nc.sbuf_tensor(name, shape, dt))

        def psum(name, shape, dt):
            return ctx.enter_context(nc.psum_tensor(name, shape, dt))

        def sem(name):
            return ctx.enter_context(nc.semaphore(name))

        x_sb, ident, xn_all = keep.x_sb, keep.ident, keep.xn_all
        w_up, w_down, w_down_b = keep.w_up, keep.w_down, keep.w_down_b
        x_in = [sb(f"f_x_in{way}", [P, ROW], F32) for way in range(WAYS)]
        x_t = [sb(f"f_x_t{b}", [P, HALVES, P], F32) for b in range(2)]
        gated = [sb(f"f_gated{b}", [P, INNER], F32) for b in range(2)]
        act_sb = [sb(f"f_act{b}", [P, INNER], F32) for b in range(2)]
        act_t = [sb(f"f_act_t{b}", [P, 2, P], F32) for b in range(2)]
        y_sb = [sb(f"f_y{way}", [P, EMBED], F32) for way in range(WAYS)]
        y_rows = [sb(f"f_y_rows{way}", [P, 1], I32) for way in range(WAYS)]
        chosen = sb("f_chosen", [P, TILES, TOP_K, EMBED], F32)

        xt_ps = [psum(f"f_xt_ps{b}", [P, HALVES, P], F32) for b in range(2)]
        up_ps = [psum(f"f_up_ps{b}", [P, 2 * INNER], F32) for b in range(2)]
        at_ps = [psum(f"f_at_ps{b}", [P, 2, P], F32) for b in range(2)]
        y_ps = [psum(f"f_y_ps{b}", [P, EMBED], F32) for b in range(2)]

        x_loaded = [sem(f"f_x_loaded{way}") for way in range(WAYS)]
        sorted_in, y_stored = keep.sorted_in, [sem(f"f_y_stored{way}") for way in range(WAYS)]
        xt_done, xt_ready = sem("f_xt_done"), sem("f_xt_ready")
        up_done, gated_ready, act_ready = sem("f_up_done"), sem("f_gated_ready"), sem("f_act_ready")
        at_done, at_a_ready, at_b_ready = sem("f_at_done"), sem("f_at_a_ready"), sem("f_at_b_ready")
        down_done, y_ready = sem("f_down_done"), sem("f_y_ready")
        GROUP = 4
        returned = [sem(f"f_returned{g}") for g in range(TILES // GROUP)]
        rows_set = keep.rows_set
        summed, added, out_stored = sem("f_summed"), sem("f_added"), sem("f_out_stored")

        ITEMS = TILES + MAX_TILES
        COMBINE_LAG = 3
        EXPERT_END = SHARED_FIRST + MAX_TILES

        def tile_of(k, r):
            return (k if k < SHARED_FIRST else k - MAX_TILES) + WAYS * r

        def is_sorted(k):
            return SHARED_FIRST <= k < EXPERT_END

        def pipeline(eng, stages, ahead=None, straight=None):
            lag = len(stages) - 1

            def slot(k, r, slots=1):
                if ahead is not None:
                    ahead(k, r, slots)
                for j in range(lag, -1, -1):
                    if stages[j] is not None and 0 <= k - j < ITEMS:
                        stages[j](k - j, r)

            s = 0
            for start, end in ((0, SHARED_FIRST), (SHARED_FIRST, EXPERT_END), (EXPERT_END, ITEMS)):
                while s < min(end, start + lag + WAYS):
                    slot(s, 0)
                    s += 1
                turns = (end - s) // WAYS
                if turns > 1 and start != straight:
                    with eng.Fori(0, turns) as r:
                        for i in range(WAYS):
                            slot(s + i, r, WAYS if i == 0 else 0)
                    s += WAYS * turns
                while s < end:
                    slot(s, 0)
                    s += 1
            for s in range(ITEMS, ITEMS + lag):
                slot(s, 0)

        block = ctx.enter_context(nc.Block())

        @block.sync
        def _(sp):
            def load(k, r):
                way = k % WAYS
                if k >= EXPERT_END:
                    return
                if k >= WAYS:
                    if is_sorted(k - WAYS):
                        sp.wait_ge(at_b_ready, k + WAYS * r - WAYS + 1)
                    else:
                        sp.wait_ge(xt_done, k + WAYS * r - WAYS + 1)
                if is_sorted(k):
                    if k == SHARED_FIRST:
                        for half in sorted_in:
                            sp.wait_ge(half, 16 * TOP_K * SORT_TILES)
                    sp.dma_start(x_in[way][:], io.sorted_x[bass.ds((k - SHARED_FIRST + WAYS * r) * P, P), :]
                                 ).then_inc(x_loaded[way], 16)
                else:
                    sp.dma_start(x_in[way][:, 0:EMBED].unsqueeze(1), xn_all[:, bass.ds(tile_of(k, r), 1), 0:EMBED]
                                 ).then_inc(x_loaded[way], 16)
            pipeline(sp, [load])
            for t in range(0, TILES, 2):
                sp.wait_ge(summed, t + 2)
                sp.dma_start(io.out[t * P:(t + 2) * P, :].rearrange("(t p) f -> p t f", p=P),
                             x_sb[:, t:t + 2, :]).then_inc(out_stored, 16)
            sp.wait_ge(out_stored, 16 * TILES // 2)

        @block.gpsimd
        def _(pool):
            def sort(n, tiles):
                for t in tiles:
                    nc.gpsimd.indirect_dma_start(
                        io.sorted_x, bass.IndirectOffsetOnAxis(ap=keep.row[:, n, t:t + 1], axis=0),
                        xn_all[:, t, :], None).then_inc(sorted_in[t // SORT_TILES], 16)
            sort(0, range(EARLY, TILES))
            for half in range(TILES // SORT_TILES):
                tiles = range(half * SORT_TILES, (half + 1) * SORT_TILES)
                pool.wait_ge(sorted_in[half], 16 * SORT_TILES)
                nc.gpsimd.tensor_copy(xn_all[:, tiles.start:tiles.stop, EMBED:].bitcast(I32),
                                      keep.token_rows[:, 1, tiles.start:tiles.stop].unsqueeze(2)
                                      ).then_inc(rows_set, 1)
                pool.wait_ge(rows_set, half + 2)
                sort(1, tiles)

            def scatter(k, r):
                if is_sorted(k):
                    items = held(pool, k + WAYS * r + 1)
                    pool.wait_ge(rows_set, TOP_K)
                    pool.wait_ge(y_ready, items)
                    nc.gpsimd.indirect_dma_start(
                        io.token_y, bass.IndirectOffsetOnAxis(ap=y_rows[k % WAYS][:], axis=0),
                        y_sb[k % WAYS][:], None).then_inc(y_stored[k % WAYS], 16)
            pipeline(pool, [scatter])
            for way in range(WAYS):
                pool.wait_ge(y_stored[way], 16 * len(range(way, MAX_TILES, WAYS)))
            for g in range(TILES // GROUP):
                tiles = slice(g * GROUP, (g + 1) * GROUP)
                pool.dma_start(chosen[:, tiles].rearrange("p t n f -> p t (n f)"),
                               io.token_y[0:TOP_K * TOKENS, :].rearrange("(t p n) f -> p t (n f)", p=P, n=TOP_K)
                               [:, tiles, :]).then_inc(returned[g], 16)

        @block.tensor
        def _(pe):
            def transpose_x(k, r):
                b, way = k % 2, k % WAYS
                if k >= EXPERT_END:
                    x = xn_all[:, tile_of(k, r), 0:EMBED]
                else:
                    x = x_in[way][:, 0:EMBED]
                    pe.wait_ge(x_loaded[way], 16 * (k // WAYS + 1 + r))
                if k >= 2:
                    pe.wait_ge(xt_ready, k + WAYS * r - 1)
                for h in range(HALVES):
                    last = nc.tensor.transpose(xt_ps[b][:, h], x[:, h * P:(h + 1) * P], ident[:])
                last.then_inc(xt_done, 1)

            experts = {}

            def place(digit):
                return bass.ds(pe.snap(pe.to_reg(digit), min_val=0, max_val=EXPERTS - 1), 1)

            def find_experts(k, r, slots):
                if slots == 0:
                    if k - 1 in digits:
                        experts[k - 1] = place(digits[k - 1])
                    return
                window = None if slots == 1 else pe.value_load(keep.windows[0:1, bass.ds(r, 1)])
                for n, item in enumerate(range(k - 3, k + slots - 1)):
                    if not is_sorted(item):
                        experts[item] = slice(SHARED, SHARED + 1)
                    elif window is not None:
                        digits[item] = (window >> (3 * n)) & (EXPERTS - 1)
                        experts[item] = place(digits[item]) if item == k - 1 else bass.ds(
                            pe.snap(digits[item], min_val=0, max_val=EXPERTS - 1), 1)
                    elif slots == 1 and r == 0 and item not in fresh:
                        fresh.add(item)
                        experts[item] = bass.ds(pe.value_load(
                            keep.tile_expert[0:1, item - SHARED_FIRST:item - SHARED_FIRST + 1],
                            min_val=0, max_val=EXPERTS - 1), 1)
            digits = {}
            fresh = set()

            def up(k, r):
                b, e = k % 2, experts[k]
                pe.wait_ge(xt_ready, k + WAYS * r + 1)
                if k >= 2:
                    pe.wait_ge(act_ready, k + WAYS * r - 1)
                for h in range(HALVES):
                    last = nc.tensor.matmul(up_ps[b][:], x_t[b][:, h], w_up[:, h, e, :],
                                            start=(h == 0), stop=(h == HALVES - 1))
                last.then_inc(up_done, 1)

            def transpose_act(k, r):
                b = k % 2
                pe.wait_ge(act_ready, k + WAYS * r + 1)
                if k >= 2:
                    pe.wait_ge(at_a_ready, k + WAYS * r - 1)
                    pe.wait_ge(at_b_ready, k + WAYS * r - 1)
                nc.tensor.transpose(at_ps[b][:, 0], act_sb[b][:, 0:P], ident[:])
                nc.tensor.transpose(at_ps[b][0:INNER_B, 1], act_sb[b][:, P:INNER], ident[:]).then_inc(at_done, 1)

            def down(k, r):
                b, e = k % 2, experts[k]
                pe.wait_ge(at_a_ready, k + WAYS * r + 1)
                pe.wait_ge(at_b_ready, k + WAYS * r + 1)
                if k >= 2:
                    pe.wait_ge(y_ready, k + WAYS * r - 1)
                nc.tensor.matmul(y_ps[b][:], act_t[b][:, 0], w_down[:, e, :], start=True, stop=False)
                nc.tensor.matmul(y_ps[b][:], act_t[b][0:INNER_B, 1], w_down_b[:, e, :], start=False, stop=True
                                 ).then_inc(down_done, 1)
            pipeline(pe, [transpose_x, up, transpose_act, down], find_experts, straight=EXPERT_END)

        @block.scalar
        def _(act):
            def copy_x(k, r):
                b = k % 2
                act.wait_ge(xt_done, k + WAYS * r + 1)
                if k >= 2:
                    act.wait_ge(up_done, k + WAYS * r - 1)
                nc.scalar.activation(x_t[b][:], xt_ps[b][:], ACT.Copy).then_inc(xt_ready, 1)

            def gate(k, r):
                b = k % 2
                act.wait_ge(up_done, k + WAYS * r + 1)
                if k >= 2:
                    act.wait_ge(act_ready, k + WAYS * r - 1)
                nc.scalar.activation(gated[b][:], up_ps[b][:, 0:INNER], ACT.Silu).then_inc(gated_ready, 1)

            def copy_act(k, r):
                b = k % 2
                act.wait_ge(at_done, k + WAYS * r + 1)
                if k >= 2:
                    act.wait_ge(down_done, k + WAYS * r - 1)
                nc.scalar.activation(act_t[b][:, 0], at_ps[b][:, 0], ACT.Copy).then_inc(at_a_ready, 1)
            pipeline(act, [copy_x, gate, copy_act])

        @block.vector
        def _(dve):
            def multiply(k, r):
                b = k % 2
                dve.wait_ge(gated_ready, k + WAYS * r + 1)
                if k >= 2:
                    dve.wait_ge(at_done, k + WAYS * r - 1)
                nc.vector.tensor_tensor(act_sb[b][:], up_ps[b][:, INNER:], gated[b][:], ALU.mult
                                        ).then_inc(act_ready, 1)

            def copy_act_b(k, r):
                b = k % 2
                dve.wait_ge(at_a_ready, k + WAYS * r + 1)
                if k >= 2:
                    dve.wait_ge(down_done, k + WAYS * r - 1)
                if is_sorted(k):
                    if k >= SHARED_FIRST + WAYS:
                        uses = (k - SHARED_FIRST) // WAYS + r
                        dve.wait_ge(y_stored[k % WAYS], 16 * uses)
                    nc.vector.tensor_copy(y_rows[k % WAYS][:], x_in[k % WAYS][:, EMBED:].bitcast(I32))
                nc.vector.tensor_copy(act_t[b][0:INNER_B, 1], at_ps[b][0:INNER_B, 1]).then_inc(at_b_ready, 1)

            def output(k, r):
                b = k % 2
                dve.wait_ge(down_done, k + WAYS * r + 1)
                if is_sorted(k):
                    nc.vector.tensor_copy(y_sb[k % WAYS][:], y_ps[b][:]).then_inc(y_ready, 1)
                else:
                    t = bass.ds(tile_of(k, r), 1)
                    nc.vector.tensor_tensor(x_sb[:, t, :], y_ps[b][:].unsqueeze(1), x_sb[:, t, :], ALU.add
                                            ).then_inc(y_ready, 1)

            def combine(first, count):
                tiles = range(first, first + count)
                dve.wait_ge(returned[first // GROUP], 16)
                for n in range(TOP_K):
                    for t in tiles:
                        if n > 0:
                            dve.wait_ge(added, t + 1)
                        total = nc.vector.scalar_tensor_tensor(
                            x_sb[:, t, :], chosen[:, t, n, :], keep.weight[:, n, t:t + 1],
                            x_sb[:, t, :], ALU.mult, ALU.add)
                        total.then_inc(added if n == 0 else summed, 1)

            def combine_ready(k, r):
                first = (k - EXPERT_END - COMBINE_LAG) * (GROUP // 2)
                if isinstance(r, int) and first >= 0:
                    dve.wait_ge(y_ready, k - 1)
                    combine(first, GROUP // 2)
            pipeline(dve, [multiply, copy_act_b, output, combine_ready], straight=EXPERT_END)
            dve.wait_ge(y_ready, ITEMS)
            left = max(0, ITEMS - EXPERT_END - COMBINE_LAG) * (GROUP // 2)
            while left < TILES:
                count = GROUP - left % GROUP
                combine(left, count)
                left += count



def cross_attention_experts(nc, io):
    with ExitStack() as ctx:
        def sb(scope, name, shape, dt):
            return scope.enter_context(nc.sbuf_tensor(name, shape, dt))

        def scratch(name, shape, dt):
            return nc.dram_tensor(name, shape, dt, kind="Internal").ap()

        io.q_dram = scratch("q_dram", [3 * EMBED, CHUNKS, CHUNK], BF16)
        io.k_dram = scratch("k_dram", [3 * KV, CHUNKS, CHUNK], BF16)
        io.sorted_x = scratch("sorted_x", [MAX_TILES * P, ROW], F32)
        io.token_y = scratch("token_y", [TOP_K * TOKENS + WAYS * P, EMBED], F32)

        keep = Shared()
        keep.x_sb = sb(ctx, "x_sb", [P, TILES, EMBED], F32)
        keep.ident = sb(ctx, "ident", [P, P], F32)
        keep.xn_all = sb(ctx, "xn_all", [P, TILES, ROW], F32)
        keep.gate = sb(ctx, "gate", [P, HALVES, EXPERTS], F32)
        keep.before = sb(ctx, "before", [P, P], BF16)
        keep.expert_iota = sb(ctx, "expert_iota", [P, EXPERTS], F32)
        keep.tile_iota = sb(ctx, "tile_iota", [1, MAX_TILES], F32)
        keep.token_rows = sb(ctx, "token_rows", [P, TOP_K, TILES], I32)
        keep.prefetched = ctx.enter_context(nc.semaphore("prefetched"))
        with ExitStack() as attention:
            keep.bias_sb = sb(attention, "bias_sb", [P, EMBED], F32)
            keep.q_op = [sb(attention, f"q_op{b}", [P, HEADS, RUN], BF16) for b in range(2)]
            keep.k_op = [sb(attention, f"k_op{b}", [P, GROUPS, 2, RUN], BF16) for b in range(2)]
            keep.v_op = [sb(attention, f"v_op{b}", [P, CHUNK_TILES, GROUPS, 32], F32) for b in range(2)]
            keep.select = sb(attention, "select", [SEQ, HP, P], BF16)
            keep.w_out = sb(attention, "w_out", [P, HALVES, EMBED], F32)
            keep.consts_in = ctx.enter_context(nc.semaphore("consts_in"))
            keep.stored = [ctx.enter_context(nc.semaphore(f"stored{b}")) for b in range(2)]
            keep.v_all = sb(attention, "v_all", [P, TILES, KV], F32)
            keep.qkv_in = [ctx.enter_context(nc.semaphore(f"qkv_in{b}")) for b in range(2)]
            keep.blank = sb(attention, "blank", [P, WAYS, ROW], F32)
            keep.blank_set = ctx.enter_context(nc.semaphore("blank_set"))
            keep.zeroed = [op[:].rearrange("p h n -> p (h n)") for op in keep.q_op]
            keep.zeroed += [op[:].rearrange("p g a n -> p (g a n)") for op in keep.k_op]
            keep.zeroed += [op[:].rearrange("p i g m -> p (i g m)").bitcast(BF16) for op in keep.v_op]
            keep.zeroed.append(keep.blank[:].rearrange("p w f -> p (w f)").bitcast(BF16))
            keep.prefetch = [(io.gate, keep.gate[:]), (io.before, keep.before[:]),
                             (io.expert_iota, keep.expert_iota[:]), (io.tile_iota, keep.tile_iota[:]),
                             (io.token_rows, keep.token_rows[:])]
            last = MAX_TILES - BLANK_GROUPS * WAYS
            keep.prefetch.append((keep.blank[:, 0:last, :], blank_rows_at(io, BLANK_GROUPS * WAYS, last)))
            project_phase(nc, ctx, io, keep)
            attention_phase(nc, ctx, io, keep)
        keep.w_up = sb(ctx, "w_up", [P, HALVES, EXPERTS + 1, 2 * INNER], F32)
        keep.w_down = sb(ctx, "w_down", [P, EXPERTS + 1, EMBED], F32)
        keep.w_down_b = sb(ctx, "w_down_b", [INNER_B, EXPERTS + 1, EMBED], F32)
        keep.row = sb(ctx, "row", [P, TOP_K, TILES], I32)
        keep.weight = sb(ctx, "weight", [P, TOP_K, TILES], F32)
        keep.windows = sb(ctx, "windows", [1, WINDOWS], I32)
        keep.tile_expert = sb(ctx, "tile_expert", [1, MAX_TILES], I32)
        keep.rows_set = ctx.enter_context(nc.semaphore("rows_set"))
        keep.sorted_in = [ctx.enter_context(nc.semaphore(f"sorted_in{h}")) for h in range(TILES // SORT_TILES)]
        routing_phase(nc, ctx, io, keep)
        ffn_phase(nc, ctx, io, keep)


def kernel(**inputs):
    import numpy as _np
    import concourse.bacc as _bacc
    from concourse import mybir as _mybir
    from concourse.bass_utils import run_bass_kernel_spmd as _run

    def rows_first(w, n):
        return w.T.reshape(HALVES, P, n).transpose(1, 0, 2)

    def at(name):
        return _np.asarray(inputs[name])

    pairs = (CHUNKS, CHUNK_TILES, 2, SEQ, HALVES, P)
    w1 = at("L0_ffn_w1").reshape(EXPERTS, HALVES, P, 2 * INNER).transpose(2, 1, 0, 3)
    shared_up = rows_first(_np.concatenate([at("L0_ffn_sw1"), at("L0_ffn_sw2")]), 2 * INNER)
    w_down = _np.concatenate([at("L0_ffn_w2"), at("L0_ffn_sw3").T[None]]).transpose(1, 0, 2)
    token = _np.arange(P)
    row = _np.arange(SEQ)
    select = _np.zeros((SEQ, HP, 2, SEQ), _np.uint16)
    select[row, (row % 32) // 2, row % 2] = 0x3F80
    arrays = {
        "in_x": at("x").reshape(TOKENS, EMBED),
        "in_ctx_t": at("ctx_2048").reshape(pairs).transpose(0, 5, 4, 2, 3, 1).reshape(CHUNKS * P, HALVES, CHUNK),
        "in_wq": rows_first(at("L0_xattn_Wq"), EMBED),
        "in_wkv": rows_first(_np.concatenate([at("L0_xattn_Wk"), at("L0_xattn_Wv")]), 2 * KV),
        "in_wfc": at("L0_xattn_Wfc").T.reshape(2, 4, 2, 2, HEAD_DIM, EMBED)
                  .transpose(0, 2, 1, 4, 3, 5).reshape(P, HALVES, EMBED),
        "in_bias": at("L0_xattn_bfc").reshape(EMBED),
        "in_gate": rows_first(at("L0_ffn_gate_w"), EXPERTS),
        "in_w_up": _np.concatenate([w1, shared_up[:, :, None]], axis=2),
        "in_w_down": w_down[:P],
        "in_w_down_b": w_down[P:],
        "in_ident": _np.eye(P, dtype=_np.float32),
        "in_select": select.reshape(SEQ, HP, P),
        "in_before": _np.where(token[:, None] < token[None], 0x3F80, 0).astype(_np.uint16),
        "in_expert_iota": _np.tile(_np.arange(EXPERTS, dtype=_np.float32), (P, 1)),
        "in_token_rows": (TOP_K * _np.arange(TOKENS, dtype=_np.int32).reshape(TILES, 1, P)
                          + _np.arange(TOP_K, dtype=_np.int32)[:, None]).transpose(2, 1, 0),
        "in_blank_rows": TOP_K * TOKENS + _np.arange(WAYS * P, dtype=_np.int32).reshape(WAYS, P).T,
        "in_tile_iota": _np.arange(MAX_TILES, dtype=_np.float32)[None],
    }
    nc = _bacc.Bacc("TRN2", target_bir_lowering=False, num_devices=1)
    io = Shared()
    access = {}
    for name in arrays:
        arrays[name] = a = _np.ascontiguousarray(arrays[name])
        access[name] = nc.dram_tensor(name, a.shape, _mybir.dt.from_np(a.dtype), kind="ExternalInput").ap()
    io.x, io.ctx_t, io.wq, io.wkv = access["in_x"], access["in_ctx_t"], access["in_wq"], access["in_wkv"]
    io.wfc, io.bias, io.gate = access["in_wfc"], access["in_bias"], access["in_gate"]
    io.w_up, io.w_down, io.w_down_b = access["in_w_up"], access["in_w_down"], access["in_w_down_b"]
    io.ident = access["in_ident"]
    io.select, io.before = access["in_select"].bitcast(BF16), access["in_before"].bitcast(BF16)
    io.token_rows, io.blank_rows = access["in_token_rows"], access["in_blank_rows"]
    io.expert_iota, io.tile_iota = access["in_expert_iota"], access["in_tile_iota"]
    io.out = nc.dram_tensor("out", (TOKENS, EMBED), F32, kind="ExternalOutput").ap()
    cross_attention_experts(nc, io)
    r = _run(nc, [arrays], core_ids=[0])
    return r.results[0]["out"].reshape(BATCH, SEQ, EMBED)
```
